# Optimizing a Trainium2 kernel written in Bass

```python
import numpy as np
import jax
import jax.numpy as jnp

def _softmax(x, axis=-1):
    return jax.nn.softmax(x, axis=axis)

def _gelu(x):
    return jax.nn.gelu(x, approximate=True)

def _silu(x):
    return jax.nn.silu(x)

def _sigmoid(x):
    return jax.nn.sigmoid(x)

def _layernorm(x, axis=-1, eps=1e-05):
    m = jnp.mean(x, axis=axis, keepdims=True)
    v = jnp.var(x, axis=axis, keepdims=True)
    return (x - m) / jnp.sqrt(v + eps)

def _scatter_add(tgt, idx, src, axis=0):
    return tgt.at[idx].add(src)

def _segment_sum(src, seg, n):
    return jax.ops.segment_sum(src, seg, n)
kernel_name = 'mk_pixart_seq_d2_seqx_r8_b09bc9'

def setup_inputs(seed: int=0):
    np.random.seed(seed)
    _w = jnp.asarray

    def _rec_inputs():
        import jax
        import jax.numpy as jnp
        _rk = jax.random.key(seed)
        x = -0.0003929 + 0.9999 * jax.random.normal(jax.random.fold_in(_rk, 1), (8, 128, 128), jnp.float32)
        _lenS = 128 - jax.random.randint(jax.random.fold_in(_rk, 7), (8,), 0, max(1, 128 // 4) + 1, jnp.int32)
        _lenS2 = 128 - jax.random.randint(jax.random.fold_in(_rk, 8), (8,), 0, max(1, 128 // 4) + 1, jnp.int32)
        cond_1024 = 0.00782532 + 1.00527 * jax.random.normal(jax.random.fold_in(_rk, 11), (8, 128), jnp.float32)
        _ctx_1024P = jax.random.normal(jax.random.fold_in(_rk, 12), (8, 16, 128), jnp.float32)
        _ctx_1024c = jax.random.dirichlet(jax.random.fold_in(_rk, 512), 0.3 * jnp.ones((16,), jnp.float32), (8, 128))
        _ctx_1024t = jnp.einsum('bsk,bkd->bsd', _ctx_1024c, _ctx_1024P)
        _ctx_1024t = _ctx_1024t * jax.lax.rsqrt(jnp.mean(jnp.square(_ctx_1024t)) + 1e-12) * 0.953939
        ctx_1024 = -0.000761806 + 0.999296 * (_ctx_1024t + 0.3 * jax.random.normal(jax.random.fold_in(_rk, 612), (8, 128, 128), jnp.float32))
        return (x, cond_1024, ctx_1024)
    x, cond_1024, ctx_1024 = _rec_inputs()

    def _L0_xcond_setup():
        import jax, jax.numpy as jnp
        import numpy as np
        H = 128
        RH = 2 * H
        E = 3
        B, T, P = (8, 256, 64)
        LN_EPS = 1e-05

        def _layer_norm(x, gamma, beta):
            mu = jnp.mean(x, axis=-1, keepdims=True)
            var = jnp.mean(jnp.square(x - mu), axis=-1, keepdims=True)
            return (x - mu) * jax.lax.rsqrt(var + LN_EPS) * gamma + beta
        key = jax.random.key(seed)
        ks = jax.random.split(key, 24)
        s = lambda fan_in: 1.0 / np.sqrt(fan_in)
        inp = {'mix_hidden_states': jax.random.normal(ks[0], (B, T, H), jnp.float32), 'global_anchor': jax.random.normal(ks[1], (B, H), jnp.float32), 'prototype_bank': jax.random.normal(ks[2], (B, P, H), jnp.float32), 'ln_gamma': jnp.ones((H,), jnp.float32), 'ln_beta': jnp.zeros((H,), jnp.float32), 'Wq': jax.random.normal(ks[3], (H, H), jnp.float32) * s(H), 'Wk': jax.random.normal(ks[4], (H, H), jnp.float32) * s(H), 'Wv': jax.random.normal(ks[5], (H, H), jnp.float32) * s(H), 'router_W': jax.random.normal(ks[6], (3 * H, E), jnp.float32) * s(3 * H), 'router_b': jnp.zeros((E,), jnp.float32), 'e_w1': jax.random.normal(ks[7], (E, 3 * H, RH), jnp.float32) * s(3 * H), 'e_b1': jnp.zeros((E, RH), jnp.float32), 'e_w2': jax.random.normal(ks[8], (E, RH, H), jnp.float32) * s(RH), 'e_b2': jnp.zeros((E, H), jnp.float32), 'gate_w1': jax.random.normal(ks[9], (3 * H, H), jnp.float32) * s(3 * H), 'gate_b1': jnp.zeros((H,), jnp.float32), 'gate_w2': jax.random.normal(ks[10], (H, H), jnp.float32) * s(H), 'gate_b2': jnp.zeros((H,), jnp.float32), 'out_w': jax.random.normal(ks[11], (H, H), jnp.float32) * s(H), 'out_b': jnp.zeros((H,), jnp.float32)}
        return inp
    _L0_xcond_all = _L0_xcond_setup()
    _L0_xcond_in = {k: v for k, v in _L0_xcond_all.items() if k in ('ln_gamma', 'ln_beta', 'Wq', 'Wk', 'Wv', 'router_W', 'router_b', 'e_w1', 'e_b1', 'e_w2', 'e_b2', 'gate_w1', 'gate_b1', 'gate_w2', 'gate_b2', 'out_w', 'out_b')}
    del _L0_xcond_all

    def _L1_xcond_setup():
        import jax, jax.numpy as jnp
        import numpy as np
        LN_EPS = 1e-06

        def _ln(x):
            mu = jnp.mean(x, axis=-1, keepdims=True)
            var = jnp.var(x, axis=-1, keepdims=True)
            return (x - mu) * jax.lax.rsqrt(var + LN_EPS)
        key = jax.random.key(seed)
        H, NH = (128, 16)
        B, N, S = (4, 128, 77)
        MLP = int(H * 4.0)
        ks = jax.random.split(key, 20)
        s = 1.0 / np.sqrt(H)
        return {'x': jax.random.normal(ks[0], (B, N, H), jnp.float32), 'c': jax.random.normal(ks[1], (B, H), jnp.float32), 'context': jax.random.normal(ks[2], (B, S, H), jnp.float32), 'W_mod': jax.random.normal(ks[3], (H, 6 * H), jnp.float32) * s, 'b_mod': jnp.zeros((6 * H,), jnp.float32), 'W_qkv': jax.random.normal(ks[4], (H, 3 * H), jnp.float32) * s, 'b_qkv': jnp.zeros((3 * H,), jnp.float32), 'W_proj': jax.random.normal(ks[5], (H, H), jnp.float32) * s, 'b_proj': jnp.zeros((H,), jnp.float32), 'W_qc': jax.random.normal(ks[6], (H, H), jnp.float32) * s, 'b_qc': jnp.zeros((H,), jnp.float32), 'W_kvc': jax.random.normal(ks[7], (H, 2 * H), jnp.float32) * s, 'b_kvc': jnp.zeros((2 * H,), jnp.float32), 'W_cproj': jax.random.normal(ks[8], (H, H), jnp.float32) * s, 'b_cproj': jnp.zeros((H,), jnp.float32), 'W_mlp1': jax.random.normal(ks[9], (H, MLP), jnp.float32) * s, 'b_mlp1': jnp.zeros((MLP,), jnp.float32), 'W_mlp2': jax.random.normal(ks[10], (MLP, H), jnp.float32) * (1.0 / np.sqrt(MLP)), 'b_mlp2': jnp.zeros((H,), jnp.float32)}
    _L1_xcond_all = _L1_xcond_setup()
    _L1_xcond_in = {k: v for k, v in _L1_xcond_all.items() if k in ('W_mod', 'b_mod', 'W_qkv', 'b_qkv', 'W_proj', 'b_proj', 'W_qc', 'b_qc', 'W_kvc', 'b_kvc', 'W_cproj', 'b_cproj', 'W_mlp1', 'b_mlp1', 'W_mlp2', 'b_mlp2')}
    del _L1_xcond_all
    return {'x': x, 'cond_1024': cond_1024, 'ctx_1024': ctx_1024, 'L0_xcond_ln_gamma': _L0_xcond_in['ln_gamma'], 'L0_xcond_ln_beta': _L0_xcond_in['ln_beta'], 'L0_xcond_Wq': _L0_xcond_in['Wq'], 'L0_xcond_Wk': _L0_xcond_in['Wk'], 'L0_xcond_Wv': _L0_xcond_in['Wv'], 'L0_xcond_router_W': _L0_xcond_in['router_W'], 'L0_xcond_router_b': _L0_xcond_in['router_b'], 'L0_xcond_e_w1': _L0_xcond_in['e_w1'], 'L0_xcond_e_b1': _L0_xcond_in['e_b1'], 'L0_xcond_e_w2': _L0_xcond_in['e_w2'], 'L0_xcond_e_b2': _L0_xcond_in['e_b2'], 'L0_xcond_gate_w1': _L0_xcond_in['gate_w1'], 'L0_xcond_gate_b1': _L0_xcond_in['gate_b1'], 'L0_xcond_gate_w2': _L0_xcond_in['gate_w2'], 'L0_xcond_gate_b2': _L0_xcond_in['gate_b2'], 'L0_xcond_out_w': _L0_xcond_in['out_w'], 'L0_xcond_out_b': _L0_xcond_in['out_b'], 'L1_xcond_W_mod': _L1_xcond_in['W_mod'], 'L1_xcond_b_mod': _L1_xcond_in['b_mod'], 'L1_xcond_W_qkv': _L1_xcond_in['W_qkv'], 'L1_xcond_b_qkv': _L1_xcond_in['b_qkv'], 'L1_xcond_W_proj': _L1_xcond_in['W_proj'], 'L1_xcond_b_proj': _L1_xcond_in['b_proj'], 'L1_xcond_W_qc': _L1_xcond_in['W_qc'], 'L1_xcond_b_qc': _L1_xcond_in['b_qc'], 'L1_xcond_W_kvc': _L1_xcond_in['W_kvc'], 'L1_xcond_b_kvc': _L1_xcond_in['b_kvc'], 'L1_xcond_W_cproj': _L1_xcond_in['W_cproj'], 'L1_xcond_b_cproj': _L1_xcond_in['b_cproj'], 'L1_xcond_W_mlp1': _L1_xcond_in['W_mlp1'], 'L1_xcond_b_mlp1': _L1_xcond_in['b_mlp1'], 'L1_xcond_W_mlp2': _L1_xcond_in['W_mlp2'], 'L1_xcond_b_mlp2': _L1_xcond_in['b_mlp2']}

def reference(x, cond_1024, ctx_1024, L0_xcond_ln_gamma, L0_xcond_ln_beta, L0_xcond_Wq, L0_xcond_Wk, L0_xcond_Wv, L0_xcond_router_W, L0_xcond_router_b, L0_xcond_e_w1, L0_xcond_e_b1, L0_xcond_e_w2, L0_xcond_e_b2, L0_xcond_gate_w1, L0_xcond_gate_b1, L0_xcond_gate_w2, L0_xcond_gate_b2, L0_xcond_out_w, L0_xcond_out_b, L1_xcond_W_mod, L1_xcond_b_mod, L1_xcond_W_qkv, L1_xcond_b_qkv, L1_xcond_W_proj, L1_xcond_b_proj, L1_xcond_W_qc, L1_xcond_b_qc, L1_xcond_W_kvc, L1_xcond_b_kvc, L1_xcond_W_cproj, L1_xcond_b_cproj, L1_xcond_W_mlp1, L1_xcond_b_mlp1, L1_xcond_W_mlp2, L1_xcond_b_mlp2):
    import jax
    import jax.numpy as jnp

    def _L0_xcond_ref(mix_hidden_states, global_anchor, prototype_bank, ln_gamma, ln_beta, Wq, Wk, Wv, router_W, router_b, e_w1, e_b1, e_w2, e_b2, gate_w1, gate_b1, gate_w2, gate_b2, out_w, out_b):
        import jax, jax.numpy as jnp
        import numpy as np
        H = 128
        RH = 2 * H
        E = 3
        B, T, P = (8, 256, 64)
        LN_EPS = 1e-05

        def _layer_norm(x, gamma, beta):
            mu = jnp.mean(x, axis=-1, keepdims=True)
            var = jnp.mean(jnp.square(x - mu), axis=-1, keepdims=True)
            return (x - mu) * jax.lax.rsqrt(var + LN_EPS) * gamma + beta
        x = mix_hidden_states
        nx = _layer_norm(x, ln_gamma, ln_beta)
        q = nx @ Wq
        k = prototype_bank @ Wk
        v = prototype_bank @ Wv
        scores = jnp.einsum('bth,bph->btp', q, k) * H ** (-0.5)
        weights = jax.nn.softmax(scores, axis=-1)
        evidence = jnp.einsum('btp,bph->bth', weights, v)
        anchor = jnp.broadcast_to(global_anchor[:, None, :], nx.shape)
        combined = jnp.concatenate([nx, evidence, anchor], axis=-1)
        router_logits = combined @ router_W + router_b
        router_probs = jax.nn.softmax(router_logits, axis=-1)
        h = jax.nn.silu(jnp.einsum('btc,ecr->bter', combined, e_w1) + e_b1)
        expert_out = jnp.einsum('bter,erh->bteh', h, e_w2) + e_b2
        routed = jnp.sum(expert_out * router_probs[..., None], axis=-2)
        g = jax.nn.sigmoid(jax.nn.silu(combined @ gate_w1 + gate_b1) @ gate_w2 + gate_b2)
        refined_delta = g * (routed @ out_w + out_b)
        return x + refined_delta

    def _L1_xcond_ref(x, c, context, W_mod, b_mod, W_qkv, b_qkv, W_proj, b_proj, W_qc, b_qc, W_kvc, b_kvc, W_cproj, b_cproj, W_mlp1, b_mlp1, W_mlp2, b_mlp2):
        import jax, jax.numpy as jnp
        import numpy as np
        LN_EPS = 1e-06

        def _ln(x):
            mu = jnp.mean(x, axis=-1, keepdims=True)
            var = jnp.var(x, axis=-1, keepdims=True)
            return (x - mu) * jax.lax.rsqrt(var + LN_EPS)
        B, N, H = x.shape
        NH = 16
        hd = H // NH
        scale = hd ** (-0.5)
        c_proj = jax.nn.silu(c) @ W_mod + b_mod
        shift_a, scale_a, gate_a, shift_m, scale_m, gate_m = jnp.split(c_proj, 6, axis=-1)

        def modulate(t, shift, sc):
            return t * (1 + sc[:, None]) + shift[:, None]
        x_norm = modulate(_ln(x), shift_a, scale_a)
        qkv = x_norm @ W_qkv + b_qkv
        q, k, v = jnp.split(qkv, 3, axis=-1)
        q = q.reshape(B, N, NH, hd).transpose(0, 2, 1, 3)
        k = k.reshape(B, N, NH, hd).transpose(0, 2, 1, 3)
        v = v.reshape(B, N, NH, hd).transpose(0, 2, 1, 3)
        attn_w = jax.nn.softmax(jnp.einsum('bhqd,bhkd->bhqk', q, k) * scale, axis=-1)
        attn_out = jnp.einsum('bhqk,bhkd->bhqd', attn_w, v)
        attn_out = attn_out.transpose(0, 2, 1, 3).reshape(B, N, H)
        attn_out = attn_out @ W_proj + b_proj
        x = x + gate_a[:, None] * attn_out
        S = context.shape[1]
        q_c = _ln(x) @ W_qc + b_qc
        kv_c = _ln(context) @ W_kvc + b_kvc
        k_c, v_c = jnp.split(kv_c, 2, axis=-1)
        q_c = q_c.reshape(B, N, NH, hd).transpose(0, 2, 1, 3)
        k_c = k_c.reshape(B, S, NH, hd).transpose(0, 2, 1, 3)
        v_c = v_c.reshape(B, S, NH, hd).transpose(0, 2, 1, 3)
        c_attn_w = jax.nn.softmax(jnp.einsum('bhqd,bhsd->bhqs', q_c, k_c) * scale, axis=-1)
        c_attn_out = jnp.einsum('bhqs,bhsd->bhqd', c_attn_w, v_c)
        c_attn_out = c_attn_out.transpose(0, 2, 1, 3).reshape(B, N, H)
        c_attn_out = c_attn_out @ W_cproj + b_cproj
        x = x + c_attn_out
        x_norm2 = modulate(_ln(x), shift_m, scale_m)
        h = jax.nn.gelu(x_norm2 @ W_mlp1 + b_mlp1)
        h = h @ W_mlp2 + b_mlp2
        x = x + gate_m[:, None] * h
        return x
    x = _L0_xcond_ref(x, cond_1024, ctx_1024, L0_xcond_ln_gamma, L0_xcond_ln_beta, L0_xcond_Wq, L0_xcond_Wk, L0_xcond_Wv, L0_xcond_router_W, L0_xcond_router_b, L0_xcond_e_w1, L0_xcond_e_b1, L0_xcond_e_w2, L0_xcond_e_b2, L0_xcond_gate_w1, L0_xcond_gate_b1, L0_xcond_gate_w2, L0_xcond_gate_b2, L0_xcond_out_w, L0_xcond_out_b)
    x = _L1_xcond_ref(x, cond_1024, ctx_1024, L1_xcond_W_mod, L1_xcond_b_mod, L1_xcond_W_qkv, L1_xcond_b_qkv, L1_xcond_W_proj, L1_xcond_b_proj, L1_xcond_W_qc, L1_xcond_b_qc, L1_xcond_W_kvc, L1_xcond_b_kvc, L1_xcond_W_cproj, L1_xcond_b_cproj, L1_xcond_W_mlp1, L1_xcond_b_mlp1, L1_xcond_W_mlp2, L1_xcond_b_mlp2)
    return x

_drawn_inputs = setup_inputs


def setup_inputs(seed=0):
    import zlib

    import numpy as np

    out = dict(_drawn_inputs(seed))
    spreads = {'L0_xcond_ln_gamma': (1.0, 0.539),
     'L0_xcond_ln_beta': (0.0, 0.651),
     'L0_xcond_router_b': (0.0, 0.8),
     'L0_xcond_e_b1': (0.0, 0.386),
     'L0_xcond_e_b2': (0.0, 0.1),
     'L0_xcond_gate_b1': (0.0, 0.8),
     'L0_xcond_gate_b2': (0.0, 0.8),
     'L0_xcond_out_b': (0.0, 0.1),
     'L1_xcond_b_mod': (0.0, 0.1),
     'L1_xcond_b_qkv': (0.0, 0.1),
     'L1_xcond_b_proj': (0.0, 0.1),
     'L1_xcond_b_qc': (0.0, 0.524),
     'L1_xcond_b_kvc': (0.0, 0.1),
     'L1_xcond_b_cproj': (0.0, 0.1),
     'L1_xcond_b_mlp1': (0.0, 0.1),
     'L1_xcond_b_mlp2': (0.0, 0.1)}
    factors = {}
    for name, (base, spread) in spreads.items():
        noise = np.random.default_rng([zlib.crc32(name.encode()), seed]).standard_normal(out[name].shape)
        drawn = base * np.exp(spread * noise) if base else spread * noise
        out[name] = jnp.asarray(drawn.astype(out[name].dtype))
    for name, factor in factors.items():
        out[name] = (out[name] * factor).astype(out[name].dtype)
    return out
```

```python
from contextlib import ExitStack

import concourse.bass as bass
from concourse import mybir

ALU = mybir.AluOpType
ACT = mybir.ActivationFunctionType
AX_X = mybir.AxisListType.X
F32 = mybir.dt.float32
F32R = mybir.dt.float32r
BF16 = mybir.dt.bfloat16
F16 = mybir.dt.float16

P = 128
NB = 8
HB = 4
NHALF = NB // HB
HN = HB * P
E = 3
MH = 6
NH = 16
D = P // NH
NC = 4
HC = NH // NC
NM = 4
VW = 3 * D + 1
NI = 2 * NB
NR = 2
PR = 3
EPS0 = 1e-5
EPS1 = 1e-6
SCALE0 = float(P) ** -0.5
SCALE1 = float(D) ** -0.5

ROW = {}
for _name, _n in (("gamma", 1), ("beta", 1), ("e_b1", MH), ("gate_b1", 1), ("gate_b2", 1), ("out_b", 1), ("b_mod", 6),
                  ("b_qkv", 3), ("b_proj", 1), ("b_qc", 1), ("b_kvc", 2), ("b_cproj", 1), ("b_mlp1", NM),
                  ("b_mlp2", 1), ("cond", NB)):
    ROW[_name] = sum(n for _, n in ROW.values()), _n
ROWS = sum(n for _, n in ROW.values())

NORMS = [("x", 0), ("x", 1), ("c", 0), ("c", 1), ("1", 0), ("1", 1), ("2", 0), ("2", 1), ("3", 0), ("3", 1)]
HEADS = [("kc", 0), ("kc", 1), ("k", 0), ("q", 0), ("k", 1), ("q", 1), ("qc", 0), ("qc", 1)]
VALUES = [(1, 0), (1, 1), (0, 0), (0, 1)]


def schedule():
    o = [("rows",), ("wt",), ("stats", 0), ("stats", 1), ("hat", 0), ("ctx_t", 0), ("hat", 1), ("ctx_t", 1), ("kq_w",),
         ("stats", 2), ("stats", 3), ("anchor",), ("kq", 0), ("v0", 0), ("kq", 1), ("v0", 1), ("mod",),
         ("s0", 0), ("s0", 1), ("hat", 2), ("p0_t", 0), ("hat", 3), ("p0_t", 1), ("ev", 0), ("ev", 1)]
    o += [("proj", 0), ("gate1", 0), ("proj", 1)]
    o += [("hidden", 0, m) for m in range(MH)]
    o += [("sel", 0), ("gate1", 1), ("router", 0)]
    o += [("hidden", 1, m) for m in range(MH)]
    o += [("router", 1), ("probs", 0), ("probs", 1), ("gate2", 0), ("gate2", 1)]
    o += [("expert", b) for b in range(HB)] + [("sel", 1), ("routed_t", 0)]
    o += [("expert", b) for b in range(HB, HB + 2)] + [("out0", 0)]
    o += [("expert", b) for b in range(HB + 2, NB)] + [("delta_t", 0), ("stats", 4)]
    o += [("routed_t", 1), ("values", 0), ("out0", 1), ("values", 1), ("delta_t", 1), ("stats", 5)]
    o += [("hat", 4), ("proj", 2), ("proj", 3), ("values", 2), ("sel", 2), ("sel", 3),
          ("hat", 5), ("proj", 4), ("proj", 5), ("values", 3)]
    side = {
        (0, 1): [("sel", 4)], (0, 3): [("sel", 5)],
        (5, 0): [("attn_t", 0)], (5, 2): [("attn_proj", 0)], (5, 3): [("attn_y", 0), ("stats", 6)],
        (6, 0): [("hat", 6)], (6, 1): [("proj", 6)], (6, 2): [("sel", 6)],
        (9, 0): [("attn_t", 1)], (9, 2): [("attn_proj", 1)], (9, 3): [("attn_y", 1), ("stats", 7)],
        (10, 0): [("hat", 7)], (10, 1): [("proj", 7)], (10, 2): [("sel", 7)],
        (13, 0): [("attn_t", 2)], (13, 2): [("attn_proj", 2)], (13, 3): [("attn_y", 2), ("stats", 8)],
        (14, 0): [("hat", 8)], (14, 1): [("mlp1", 0, 0), ("mlp1", 0, 1)], (14, 3): [("mlp1", 0, 2), ("mlp1", 0, 3)],
        (15, 2): [("mlp2", 0)], (15, 3): [("last", 0)],
    }
    o += [("scores", 0, c) for c in range(NC)] + [("guard", 0)]
    for i in range(NI):
        o.append(("guard_t", i))
        for c in range(NC):
            if i + 1 < NI:
                o.append(("scores", i + 1, c))
                if c == 0:
                    continue
                o.append(("probs1", i, c - 1))
            else:
                o.append(("probs1", i, c))
            o += side.get((i, c - 1), [])
        if i + 1 < NI:
            o += [("guard", i + 1), ("probs1", i, NC - 1)]
        o += side.get((i, NC - 1), [])
        if i >= 1:
            o.append(("mix", i - 1))
    o += [("mix", NI - 1), ("attn_t", 3), ("attn_proj", 3), ("attn_y", 3), ("stats", 9), ("hat", 9)]
    o += [("mlp1", 1, m) for m in range(NM)] + [("mlp2", 1), ("last", 1)]
    return o


def pixart_block(nc, x, cond, ctx, ln_gamma, ln_beta, Wq, Wk, Wv, router_W, router_b, e_w1, e_b1, e_w2, e_b2,
                 gate_w1, gate_b1, gate_w2, gate_b2, out_w, out_b, W_mod, b_mod, W_qkv, b_qkv, W_proj, b_proj,
                 W_qc, b_qc, W_kvc, b_kvc, W_cproj, b_cproj, W_mlp1, b_mlp1, W_mlp2, b_mlp2, out):
    steps = schedule()

    with ExitStack() as stack:
        def sb(name, shape, dt=F32):
            return stack.enter_context(nc.sbuf_tensor(name, shape, dt))

        def sem(name):
            return stack.enter_context(nc.semaphore(name))

        res = sb("res", [P, NB, P])
        ctx_tok = sb("ctx_tok", [P, NB, P])
        rows = sb("rows", [ROWS, P])
        wqkv0 = sb("wqkv0", [P, 3, P])
        ew1 = sb("ew1", [P, E, 3, 2 * P])
        ew2 = sb("ew2", [P, E, 2, P])
        eb2 = sb("eb2", [P, E, P])
        gw1 = sb("gw1", [P, 3, P])
        gw2 = sb("gw2", [P, P])
        ow = sb("ow", [P, P])
        rw = sb("rw", [P, 3, E])
        rb = sb("rb", [E, 1])
        wmod = sb("wmod", [P, 6, P])
        wqkv1 = sb("wqkv1", [P, 3, P])
        wproj = sb("wproj", [P, 2, P])
        wqc = sb("wqc", [P, P])
        wkvc = sb("wkvc", [P, 2, P])
        wm1 = sb("wm1", [P, NM, P])
        wm2 = sb("wm2", [P, NM, P])

        ident = sb("ident", [P, P])
        ident_h = sb("ident_h", [P, P], BF16)
        slot_sel = sb("slot_sel", [P, 4, NC, HC, 4, D], F32R)
        pair_sel = sb("pair_sel", [P, NH])
        head_sel = sb("head_sel", [P, NH, P], BF16)
        power = sb("power", [P, HB])

        cols = sb("cols", [P, ROWS])
        gate_b2_half = sb("gate_b2_half", [P, 1])
        silu_c = sb("silu_c", [P, NB])
        wt = sb("wt", [P, 2, P])
        kq_w = sb("kq_w", [P, P])
        abias = sb("abias", [P, MH + 1, NB])
        rbias = sb("rbias", [E, NB])
        mod = sb("mod", [P, 6, NB])
        mod1 = sb("mod1", [P, 2, NB])
        bn = sb("bn", [P, HB, 6])
        moments = sb("moments", [P, len(NORMS), HB, 2])
        rstd = sb("rstd", [P, len(NORMS), HB])
        var_eps = sb("var_eps", [P, HB])
        small = sb("small", [P, 4, HB])
        small3 = sb("small3", [P, 4, HB, E])
        smallm = sb("smallm", [P, HB])
        smalls = sb("smalls", [P, 2, HB])
        router_p = sb("router_p", [P, NHALF, HB, E])
        guard = sb("guard", [P, 2, NH])
        guard_pair = sb("guard_pair", [P, 2, P], BF16)
        guard_t = sb("guard_t", [P, 2, P], BF16)
        rden = sb("rden", [P, NH])

        ctx_hat_t = sb("ctx_hat_t", [P, NB * P])
        norm_t = sb("norm_t", [P, NB * P])
        hat = sb("hat", [P, 2, HB, P])
        high = sb("high", [P, 2, HN], F32R)
        low = sb("low", [P, 2, HN], F32R)
        slots_kc = sb("slots_kc", [P, NC, NB * P], F32R)
        diag = {"k": sb("diag_k", [P, NR, NC, HC, P], F32R), "q": sb("diag_q", [P, NR, NC, HC, P], F32R)}
        vals = sb("vals", [P, 2, NB, NH, VW], BF16)
        vrest = sb("vrest", [P, HN])
        bias2_term = hat[:, 0]

        with nc.sbuf_tensor("hidden", [P, NHALF, NC, NB * P], F32) as hidden:
            pass
        slots_q = sb("slots_q", [P, NC, NB * P], F32R)
        slots_k = sb("slots_k", [P, NC, NB * P], F32R)
        arena = sb("arena", [P, 9728])

        def part(at, n):
            return arena[:, at:at + n]

        def hid(g, m):
            return hidden[:, g, m // 2, (m % 2) * HN:(m % 2 + 1) * HN]

        def gate_h(g):
            return hidden[:, g, 3, 0:HN]

        def gate(g):
            return hidden[:, g, 3, HN:2 * HN]

        x_hat_t, ctx_t, kq_t = part(0, 1024), part(1024, 1024), part(2048, 1024)
        v0 = part(3072, 1024).rearrange("p (b n) -> p b n", b=NB)
        ev_t = part(4096, 1024)
        p0 = part(5120, 1024).rearrange("p (b n) -> p b n", b=NB)
        p0_t = part(6144, 1024).rearrange("p (b n) -> p b n", b=NB)
        bias2 = part(7168, 1024).rearrange("p (b n) -> p b n", b=NB)
        routed = p0
        routed_t = part(8192, 512)
        delta_t = part(8704, 512)
        logit_t = part(9216, 512)

        pf = part(0, PR * HN).rearrange("p (r n) -> p r n", r=PR)
        ph = part(1536, 2048).bitcast(F16).rearrange("p (r c n) -> p r c n", r=2, c=NC)
        pl = part(3584, 2048).bitcast(F16).rearrange("p (r c n) -> p r c n", r=2, c=NC)
        attn = part(5632, 1024).rearrange("p (b n) -> p b n", b=NB)
        attn_t = part(6656, 512)
        y_t = part(7168, 512)
        mlp_h = part(7680, 2048).rearrange("p (m n) -> p m n", m=NM)

        banks = stack.enter_context(nc.psum_tensor("banks", [P, 8, HN], F32))

        S = {n: sem(n) for n in (
            "x_in0", "x_in1", "ctx_in0", "ctx_in1", "rows_in", "wqkv0_in", "gate1_in", "expert1_in", "expert2_in", "layer0_in", "mod_in",
            "heads_in", "rest_in", "out_done",
            "pool", "ident_made", "pair_sel_made", "diag_zero", "rstd_made", "bias2_made", "values_low", "p_low",
            "rows_t_made", "wt_made", "hat_t_made", "ctx_t_made", "kq_w_made", "anchor_made", "mod_made", "kq_made",
            "v0_made", "s0_made", "p0_t_made", "ev_made", "gate1_made", "hidden_made", "router_made", "probs_t_made",
            "gate2_made", "expert_made", "routed_t_made", "out0_made", "delta_made", "proj_made", "sel_made",
            "values_made", "guard_t_made", "scores_made", "scores_t_made", "mix_made", "attn_t_made",
            "attn_proj_made", "attn_y_made", "mlp1_made", "mlp2_made", "last_made",
            "vec", "vec_const", "cols_ready", "kq_w_ready", "abias_ready", "mod_ready", "moments_ready", "hat_ready",
            "norm_t_ready", "ctx_t_ready", "kq_ready", "s0_max", "p0_ready", "ev_ready", "router_ready",
            "probs_centered", "router_p_ready", "gate_ready", "routed_ready", "delta_t_ready", "res_ready",
            "low_ready", "slots_even", "values_high", "values_rest", "guard_ready", "scores_read", "mix_read",
            "attn_ready", "y_ready",
            "head_sel_ready", "silu_c_ready", "wt_ready", "hat_t_ready", "v0_ready", "s0_exp", "p0_t_ready", "gate_h_ready",
            "hidden_ready", "probs_exp", "gate_tanh", "routed_t_ready", "high_ready", "slots_odd", "guard_t_ready",
            "p_full", "p_high", "attn_t_ready", "mlp1_ready")}
        diag_in = {k: [sem(f"diag_{k}_in{r}") for r in range(NR)] for k in "kq"}

        def col(name, j=0):
            a = ROW[name][0] + j
            return cols[:, a:a + 1]

        def cols_of(name):
            a, n = ROW[name]
            return cols[:, a:a + n]

        def half(t, g):
            return t[:, g * HN:(g + 1) * HN]

        def tok(t, b):
            return t[:, b * P:(b + 1) * P]

        def by_batch(ap):
            return ap.rearrange("p (b n) -> p b n", b=HB)

        nth = {}
        seen = {}
        for st in steps:
            nth[st] = seen.get(st[0], 0)
            seen[st[0]] = nth[st] + 1
        hat_a = [n for n, (k, _) in enumerate(NORMS) if k in "xc2"]
        hat_v = [n for n, (k, _) in enumerate(NORMS) if k in "13"]

        one = lambda v: v.rearrange("(r p) -> r p", p=P)
        row_sources = {"cond": cond, "gamma": one(ln_gamma), "beta": one(ln_beta),
                       "e_b1": e_b1.rearrange("e (r p) -> (e r) p", p=P), "gate_b1": one(gate_b1),
                       "gate_b2": one(gate_b2), "out_b": one(out_b), "b_mod": one(b_mod), "b_qkv": one(b_qkv),
                       "b_proj": one(b_proj), "b_qc": one(b_qc), "b_kvc": one(b_kvc), "b_cproj": one(b_cproj),
                       "b_mlp1": one(b_mlp1), "b_mlp2": one(b_mlp2)}

        bank_of = {}
        block = stack.enter_context(nc.Block())

        @block.tensor
        def _(pe):
            released = {}
            turn = [0]

            def claim(key, reader, count, among):
                bank = among[turn[0] % len(among)]
                turn[0] += 1
                bank_of[key] = bank
                if bank in released:
                    pe.wait_ge(S[released[bank][0]], released[bank][1])
                released[bank] = (reader, count)
                return banks[:, bank, :]

            ALL = list(range(8))
            SIDE = [6, 7]
            loop = [False]

            def free():
                return SIDE if loop[0] else ALL

            def transposes(o, src, b0):
                for j in range(HB):
                    last = pe.transpose(o[:, j * P:(j + 1) * P], src[:, b0 + j, :], ident[:, :])
                return last

            def rows_(_):
                pe.wait_ge(S["ident_made"], 1)
                pe.wait_ge(S["rows_in"], 16 * len(ROW))
                o = claim("rows", "cols_ready", 1, ALL)
                pe.transpose(o[:, 0:ROWS], rows[:, :], ident[0:ROWS, 0:ROWS]).then_inc(S["rows_t_made"], 1)

            def wt_(_):
                pe.wait_ge(S["wqkv0_in"], 48)
                o = claim("wt", "wt_ready", 1, ALL)
                for j in range(2):
                    last = pe.transpose(o[:, j * P:(j + 1) * P], wqkv0[:, j, :], ident[:, :])
                last.then_inc(S["wt_made"], 1)

            def hat_(n):
                pe.wait_ge(S["hat_ready"], n + 1)
                if n in hat_a:
                    o = claim(("hat", n), "hat_t_ready", hat_a.index(n) + 1, free())
                else:
                    o = claim(("hat", n), "norm_t_ready", hat_v.index(n) + 1, free())
                transposes(o, hat[:, n % 2], 0).then_inc(S["hat_t_made"], 1)

            def ctx_t_(g):
                pe.wait_ge(S[f"ctx_in{g}"], 16)
                o = claim(("ctx_t", g), "ctx_t_ready", g + 1, ALL)
                transposes(o, ctx_tok, g * HB).then_inc(S["ctx_t_made"], 1)

            def kq_w_(_):
                pe.wait_ge(S["wt_ready"], 1)
                o = claim("kq_w", "kq_w_ready", 1, ALL)
                pe.matmul(o[:, 0:P], wt[:, 1, :], wt[:, 0, :], start=True, stop=True).then_inc(S["kq_w_made"], 1)

            def anchor_(_):
                pe.wait_ge(S["cols_ready"], 1)
                pe.wait_ge(S["gate1_in"], 48)
                pe.wait_ge(S["expert1_in"], 16)
                o = claim("anchor", "abias_ready", 1, ALL)
                c = cols_of("cond")
                for m in range(MH):
                    pe.matmul(o[:, m * NB:(m + 1) * NB], ew1[:, m // 2, 2, (m % 2) * P:(m % 2 + 1) * P], c,
                              start=True, stop=True)
                pe.matmul(o[:, MH * NB:(MH + 1) * NB], gw1[:, 2, :], c, start=True, stop=True)
                pe.matmul(o[0:E, (MH + 1) * NB:(MH + 2) * NB], rw[:, 2, :], c, start=True, stop=True)\
                    .then_inc(S["anchor_made"], 1)

            def mod_(_):
                pe.wait_ge(S["silu_c_ready"], 1)
                pe.wait_ge(S["mod_in"], 16)
                o = claim("mod", "mod_ready", 1, ALL)
                for j in range(6):
                    last = pe.matmul(o[:, j * NB:(j + 1) * NB], wmod[:, j, :], silu_c[:, :], start=True, stop=True)
                last.then_inc(S["mod_made"], 1)

            def kq_(g):
                if g == 0:
                    pe.wait_ge(S["kq_w_ready"], 1)
                pe.wait_ge(S["ctx_t_ready"], g + 1)
                o = claim(("kq", g), "kq_ready", g + 1, ALL)
                pe.matmul(o, kq_w[:, :], half(ctx_t, g), start=True, stop=True).then_inc(S["kq_made"], 1)

            def v0_(g):
                o = claim(("v0", g), "v0_ready", g + 1, ALL)
                for j in range(HB):
                    last = pe.matmul(o[:, j * P:(j + 1) * P], tok(ctx_t, g * HB + j), wqkv0[:, 2, :],
                                     start=True, stop=True)
                last.then_inc(S["v0_made"], 1)

            def s0_(g):
                pe.wait_ge(S["kq_ready"], g + 1)
                pe.wait_ge(S["hat_t_ready"], g + 1)
                o = claim(("s0", g), "s0_exp", g + 1, ALL)
                for j in range(HB):
                    b = g * HB + j
                    last = pe.matmul(o[:, j * P:(j + 1) * P], tok(x_hat_t, b), tok(kq_t, b), start=True, stop=True)
                last.then_inc(S["s0_made"], 1)

            def p0_t_(g):
                pe.wait_ge(S["p0_ready"], g + 1)
                o = claim(("p0_t", g), "p0_t_ready", g + 1, ALL)
                transposes(o, p0, g * HB).then_inc(S["p0_t_made"], 1)

            def ev_(g):
                pe.wait_ge(S["v0_ready"], g + 1)
                pe.wait_ge(S["p0_t_ready"], g + 1)
                o = claim(("ev", g), "ev_ready", g + 1, ALL)
                for j in range(HB):
                    b = g * HB + j
                    last = pe.matmul(o[:, j * P:(j + 1) * P], v0[:, b, :], p0_t[:, b, :], start=True, stop=True)
                last.then_inc(S["ev_made"], 1)

            def pair(o, lhs, g):
                pe.matmul(o, lhs(0), half(x_hat_t, g), start=True, stop=False)
                return pe.matmul(o, lhs(1), half(ev_t, g), start=False, stop=True)

            def gate1_(g):
                pe.wait_ge(S["ev_ready"], g + 1)
                o = claim(("gate1", g), "gate_h_ready", g + 1, ALL)
                pair(o, lambda k: gw1[:, k, :], g).then_inc(S["gate1_made"], 1)

            def hidden_(g, m):
                n = g * MH + m
                o = claim(("hidden", n), "hidden_ready", n + 1, ALL)
                pair(o, lambda k: ew1[:, m // 2, k, (m % 2) * P:(m % 2 + 1) * P], g).then_inc(S["hidden_made"], 1)

            def router_(g):
                o = claim(("router", g), "router_ready", g + 1, ALL)
                pair(o[0:E, :], lambda k: rw[:, k, :], g).then_inc(S["router_made"], 1)

            def probs_(g):
                pe.wait_ge(S["router_ready"], g + 1)
                o = claim(("probs", g), "probs_centered", g + 1, ALL)
                for j in range(HB):
                    last = pe.transpose(o[:, j * E:(j + 1) * E], logit_t[0:E, j * P:(j + 1) * P], ident[0:E, 0:E])
                last.then_inc(S["probs_t_made"], 1)

            def gate2_(g):
                pe.wait_ge(S["gate_h_ready"], g + 1)
                pe.wait_ge(S["layer0_in"], 48)
                o = claim(("gate2", g), "gate_tanh", g + 1, ALL)
                pe.matmul(o, gw2[:, :], gate_h(g), start=True, stop=True).then_inc(S["gate2_made"], 1)

            def expert_(b):
                if b == 0:
                    pe.wait_ge(S["expert2_in"], 16)
                if b % HB == 0:
                    pe.wait_ge(S["hidden_ready"], MH * (b // HB + 1))
                o = claim(("expert", b), "routed_ready", b + 1, ALL)
                for e in range(E):
                    for r in range(2):
                        last = pe.matmul(o[:, e * P:(e + 1) * P], tok(hid(b // HB, 2 * e + r), b % HB),
                                         ew2[:, e, r, :], start=(r == 0), stop=(r == 1))
                last.then_inc(S["expert_made"], 1)

            def routed_t_(g):
                pe.wait_ge(S["routed_ready"], HB * (g + 1))
                o = claim(("routed_t", g), "routed_t_ready", g + 1, ALL)
                transposes(o, routed, g * HB).then_inc(S["routed_t_made"], 1)

            def out0_(g):
                pe.wait_ge(S["routed_t_ready"], g + 1)
                o = claim(("out0", g), "delta_t_ready", g + 1, ALL)
                pe.matmul(o, ow[:, :], routed_t, start=True, stop=True).then_inc(S["out0_made"], 1)

            def delta_t_(g):
                pe.wait_ge(S["delta_t_ready"], g + 1)
                o = claim(("delta_t", g), "res_ready", g + 1, ALL)
                transposes(o, by_batch(delta_t), 0).then_inc(S["delta_made"], 1)

            def proj_(n):
                kind, g = HEADS[n]
                if n == 0:
                    pe.wait_ge(S["heads_in"], 48)
                src, w = {"kc": (ctx_hat_t, wkvc[:, 0, :]), "k": (norm_t, wqkv1[:, 1, :]),
                          "q": (norm_t, wqkv1[:, 0, :]), "qc": (norm_t, wqc[:, :])}[kind]
                if kind == "kc":
                    pe.wait_ge(S["hat_t_ready"], hat_a.index(NORMS.index(("c", g))) + 1)
                elif kind == "qc":
                    pe.wait_ge(S["hat_t_ready"], hat_a.index(NORMS.index(("2", g))) + 1)
                else:
                    pe.wait_ge(S["norm_t_ready"], hat_v.index(NORMS.index(("1", g))) + 1)
                o = claim(("proj", n), "low_ready", n + 1, free())
                pe.matmul(o, w, half(src, g), start=True, stop=True).then_inc(S["proj_made"], 1)

            def sel_(n):
                k = 2 if HEADS[n][0][0] == "k" else 0
                pe.wait_ge(S["vec_const"], 1)
                pe.wait_ge(S["low_ready"], n + 1)
                for c in range(NC):
                    reader = ("slots_even", "slots_odd")[c % 2], 2 * n + c // 2 + 1
                    o = claim(("sel", n, c), *reader, free())
                    pe.matmul(o, slot_sel[:, k, c].rearrange("p j s d -> p (j s d)"), high[:, n % 2, :],
                              start=True, stop=False)
                    pe.matmul(o, slot_sel[:, k + 1, c].rearrange("p j s d -> p (j s d)"), low[:, n % 2, :],
                              start=False, stop=True).then_inc(S["sel_made"], 1)

            def values_(n):
                a, g = VALUES[n]
                if a:
                    pe.wait_ge(S["hat_t_ready"], hat_a.index(NORMS.index(("c", g))) + 1)
                else:
                    pe.wait_ge(S["norm_t_ready"], hat_v.index(NORMS.index(("1", g))) + 1)
                src, w = ((norm_t, wqkv1[:, 2, :]), (ctx_hat_t, wkvc[:, 1, :]))[a]
                o = claim(("values", n), "values_rest", n + 1, free())
                for j in range(HB):
                    last = pe.matmul(o[:, j * P:(j + 1) * P], tok(src, g * HB + j), w, start=True, stop=True)
                last.then_inc(S["values_made"], 1)

            def slots_key(i):
                return slots_k if i < NB else slots_kc

            def scores_(i, c):
                loop[0] = True
                b = i % NB
                if c == 0:
                    pe.wait_ge(diag_in["k"][i % NR], 16 * HC * (i // NR + 1))
                    if i % HB == 0:
                        n = HEADS.index((("q", "qc")[i // NB], b // HB))
                        pe.wait_ge(S["slots_even"], 2 * n + 2)
                        pe.wait_ge(S["slots_odd"], 2 * n + 2)
                bank = [0, 1, 2][(i * NC + c) % 3]
                o = claim(("scores", i, c), "scores_read", i * NC + c + 1, [bank])
                pe.matmul(o, tok(slots_q[:, c, :], b), diag["k"][:, i % NR, c].rearrange("p j n -> p (j n)"),
                          start=True, stop=True).then_inc(S["scores_made"], 1)

            def guard_t_(i):
                pe.wait_ge(S["guard_ready"], i + 1)
                o = claim(("guard_t", i), "guard_t_ready", i + 1, free())
                pe.transpose(o.bitcast(BF16)[:, 0:P], guard_pair[:, i % 2, :], ident_h[:, :])\
                    .then_inc(S["guard_t_made"], 1)

            def probs1_(i, c):
                b = i % NB
                if c == 0:
                    pe.wait_ge(diag_in["q"][i % NR], 16 * HC * (i // NR + 1))
                    pe.wait_ge(S["guard_t_ready"], i + 1)
                    if i == 0:
                        pe.wait_ge(S["head_sel_ready"], 1)
                bank = [3, 4][(i * NC + c) % 2]
                o = claim(("probs1", i, c), "p_high", i * NC + c + 1, [bank])
                pe.matmul(o, tok(slots_key(i)[:, c, :], b), diag["q"][:, i % NR, c].rearrange("p j n -> p (j n)"),
                          start=True, stop=False)
                for j in range(HC):
                    last = pe.matmul(o[:, j * P:(j + 1) * P], head_sel[:, c * HC + j, :], guard_t[:, i % 2, :],
                                     start=False, stop=(j == HC - 1))
                last.then_inc(S["scores_t_made"], 1)

            def mix_(i):
                a, b = divmod(i, NB)
                if b % HB == 0:
                    pe.wait_ge(S["values_low"], VALUES.index((a, b // HB)) + 1)
                pe.wait_ge(S["p_high"], NC * (i + 1))
                pe.wait_ge(S["p_low"], NC * (i + 1))
                o = claim(("mix", i), "mix_read", i + 1, [5])
                for h in range(NH):
                    c, j = divmod(h, HC)
                    at = o[:, h * VW:(h + 1) * VW]
                    pe.matmul(at, ph[:, i % 2, c, j * P:(j + 1) * P], vals[:, a, b, h, :], start=True, stop=False)
                    last = pe.matmul(at, pl[:, i % 2, c, j * P:(j + 1) * P], vals[:, a, b, h, :],
                                     start=False, stop=True)
                last.then_inc(S["mix_made"], 1)

            def attn_t_(p):
                pe.wait_ge(S["attn_ready"], HB * (p + 1))
                o = claim(("attn_t", p), "attn_t_ready", p + 1, free())
                transposes(o, attn, (p % 2) * HB).then_inc(S["attn_t_made"], 1)

            def attn_proj_(p):
                pe.wait_ge(S["rest_in"], 64)
                pe.wait_ge(S["attn_t_ready"], p + 1)
                o = claim(("attn_proj", p), "y_ready", (1, 2, 3, 5)[p], free())
                pe.matmul(o, wproj[:, p // 2, :], attn_t, start=True, stop=True).then_inc(S["attn_proj_made"], 1)

            def attn_y_(p):
                pe.wait_ge(S["y_ready"], (1, 2, 3, 5)[p])
                o = claim(("attn_y", p), "res_ready", (3, 4, 5, 7)[p], free())
                transposes(o, by_batch(y_t), 0).then_inc(S["attn_y_made"], 1)

            def mlp1_(g, m):
                if m == 0:
                    pe.wait_ge(S["norm_t_ready"], hat_v.index(NORMS.index(("3", g))) + 1)
                n = g * NM + m
                o = claim(("mlp1", n), "mlp1_ready", n + 1, free())
                pe.matmul(o, wm1[:, m, :], half(norm_t, g), start=True, stop=True).then_inc(S["mlp1_made"], 1)

            def mlp2_(g):
                o = claim(("mlp2", g), "y_ready", (4, 6)[g], free())
                for m in range(NM):
                    pe.wait_ge(S["mlp1_ready"], g * NM + m + 1)
                    last = pe.matmul(o, wm2[:, m, :], mlp_h[:, m, :], start=(m == 0), stop=(m == NM - 1))
                last.then_inc(S["mlp2_made"], 1)

            def last_(g):
                pe.wait_ge(S["y_ready"], (4, 6)[g])
                o = claim(("last", g), "res_ready", (6, 8)[g], free())
                transposes(o, by_batch(y_t), 0).then_inc(S["last_made"], 1)

            mine = {"rows": rows_, "wt": wt_, "hat": hat_, "ctx_t": ctx_t_, "kq_w": kq_w_, "anchor": anchor_,
                    "mod": mod_, "kq": kq_, "v0": v0_, "s0": s0_, "p0_t": p0_t_, "ev": ev_, "gate1": gate1_,
                    "hidden": hidden_, "router": router_, "probs": probs_, "gate2": gate2_, "expert": expert_,
                    "routed_t": routed_t_, "out0": out0_, "delta_t": delta_t_, "proj": proj_, "sel": sel_,
                    "values": values_, "scores": scores_, "guard_t": guard_t_, "probs1": probs1_, "mix": mix_,
                    "attn_t": attn_t_, "attn_proj": attn_proj_, "attn_y": attn_y_, "mlp1": mlp1_, "mlp2": mlp2_,
                    "last": last_}
            for st in steps:
                if st[0] in mine:
                    mine[st[0]](*(st[1:] or (0,)))

        @block.vector
        def _(dve):
            chain = [0]

            def link(ins):
                chain[0] += 1
                ins.then_inc(S["vec"], 1)
                dve.wait_ge(S["vec"], chain[0])

            def bank(key):
                return banks[:, bank_of[key], :]

            link(dve.memset(slot_sel[:].rearrange("p a c j s d -> p (a c j s d)").bitcast(F32), 0.0))
            dve.memset(guard_pair[:], 0.0)
            dve.memset(vals[:, :, :, :, 3 * D:VW].rearrange("p a b h o -> p (a b h o)"), 1.0)
            dve.wait_ge(S["ident_made"], 1)
            dve.tensor_copy(ident_h[:], ident[:])
            src = ident[:, :].rearrange("p (c j d) -> p c j d", c=NC, j=HC)
            for a, slots in enumerate(((0, 2), (1, 3), (0, 1), (2, 3))):
                for s in slots:
                    last = dve.tensor_copy(slot_sel[:, a, :, :, s, :], src)
            last.then_inc(S["vec_const"], 1)

            def rows_(_):
                dve.wait_ge(S["rows_t_made"], 1)
                link(dve.tensor_copy(cols[:], bank("rows")[:, 0:ROWS]))
                dve.tensor_scalar(gate_b2_half[:], col("gate_b2"), 0.5, None, ALU.mult).then_inc(S["cols_ready"], 1)

            def stats_(n):
                kind, g = NORMS[n]
                if kind == "x":
                    dve.wait_ge(S[f"x_in{g}"], 16)
                elif kind == "c":
                    dve.wait_ge(S[f"ctx_in{g}"], 16)
                else:
                    dve.wait_ge(S["res_ready"], {4: 1, 5: 2, 6: 3, 7: 4, 8: 5, 9: 7}[n])
                if n:
                    dve.wait_ge(S["moments_ready"], n)
                t = ctx_tok if kind == "c" else res
                for j in range(HB):
                    last = dve.bn_stats(bn[:, j, :], t[:, g * HB + j, :])
                link(last)
                for j in range(HB):
                    last = dve.bn_aggr(moments[:, n, j, :], bn[:, j, :])
                last.then_inc(S["moments_ready"], 1)

            def hat_(n):
                kind, g = NORMS[n]
                t = ctx_tok if kind == "c" else res
                dve.wait_ge(S["rstd_made"], n + 1)
                if n >= 2:
                    dve.wait_ge(S["hat_t_made"], n - 1)
                for j in range(HB):
                    last = dve.tensor_scalar(hat[:, n % 2, j, :], t[:, g * HB + j, :], moments[:, n, j, 0:1],
                                             rstd[:, n, j:j + 1], ALU.subtract, ALU.mult)
                last.then_inc(S["hat_ready"], 1)
                if n in hat_v:
                    a = 0 if kind == "1" else 1
                    dve.wait_ge(S["mod_ready"], 1)
                    dve.wait_ge(S["hat_t_made"], n + 1)
                    for j in range(HB):
                        b = g * HB + j
                        last = dve.tensor_scalar(tok(norm_t, b), bank(("hat", n))[:, j * P:(j + 1) * P],
                                                 mod1[:, a, b:b + 1], mod[:, 3 * a, b:b + 1], ALU.mult, ALU.add)
                    last.then_inc(S["norm_t_ready"], 1)

            def ctx_t_(g):
                dve.wait_ge(S["ctx_t_made"], g + 1)
                dve.tensor_copy(half(ctx_t, g), bank(("ctx_t", g))).then_inc(S["ctx_t_ready"], 1)

            def kq_w_(_):
                dve.wait_ge(S["kq_w_made"], 1)
                dve.tensor_copy(kq_w[:], bank("kq_w")[:, 0:P]).then_inc(S["kq_w_ready"], 1)

            def anchor_(_):
                dve.wait_ge(S["anchor_made"], 1)
                o = bank("anchor")
                a = ROW["e_b1"][0]
                dve.tensor_scalar(rbias[:], o[0:E, (MH + 1) * NB:(MH + 2) * NB], rb[:, 0:1], None, ALU.add)
                dve.tensor_tensor(abias[:], o[:, 0:(MH + 1) * NB].rearrange("p (m b) -> p m b", b=NB),
                                  cols[:, a:a + MH + 1].unsqueeze(2).to_broadcast([P, MH + 1, NB]), ALU.add)\
                    .then_inc(S["abias_ready"], 1)

            def mod_(_):
                dve.wait_ge(S["mod_made"], 1)
                link(dve.tensor_tensor(mod[:], bank("mod")[:, 0:6 * NB].rearrange("p (m b) -> p m b", b=NB),
                                       cols_of("b_mod").unsqueeze(2).to_broadcast([P, 6, NB]), ALU.add))
                dve.tensor_scalar(mod1[:], mod[:, 1:6:3, :], 1.0, None, ALU.add).then_inc(S["mod_ready"], 1)

            def kq_(g):
                dve.wait_ge(S["kq_made"], g + 1)
                dve.tensor_copy(half(kq_t, g), bank(("kq", g))).then_inc(S["kq_ready"], 1)

            def s0_(g):
                dve.wait_ge(S["s0_made"], g + 1)
                if g:
                    dve.wait_ge(S["p0_ready"], g)
                link(dve.tensor_reduce(smallm[:], by_batch(bank(("s0", g))), AX_X, ALU.max, negate=True))
                if g:
                    dve.wait_ge(S["s0_exp"], g)
                dve.tensor_scalar(small[:, 0, :], smallm[:], SCALE0, None, ALU.mult).then_inc(S["s0_max"], 1)
                dve.wait_ge(S["s0_exp"], g + 1)
                link(dve.reciprocal(small[:, 2, :], small[:, 1, :]))
                t = p0[:, g * HB:(g + 1) * HB, :]
                dve.tensor_tensor(t, t, small[:, 2, :].unsqueeze(2).to_broadcast([P, HB, P]), ALU.mult)\
                    .then_inc(S["p0_ready"], 1)

            def ev_(g):
                dve.wait_ge(S["ev_made"], g + 1)
                dve.tensor_copy(half(ev_t, g), bank(("ev", g))).then_inc(S["ev_ready"], 1)

            def router_(g):
                dve.wait_ge(S["router_made"], g + 1)
                if g:
                    dve.wait_ge(S["probs_t_made"], g)
                dve.tensor_tensor(by_batch(logit_t[0:E, :]), by_batch(bank(("router", g))[0:E, :]),
                                  rbias[:, g * HB:(g + 1) * HB].unsqueeze(2).to_broadcast([E, HB, P]), ALU.add)\
                    .then_inc(S["router_ready"], 1)

            def probs_(g):
                dve.wait_ge(S["probs_t_made"], g + 1)
                if g:
                    dve.wait_ge(S["router_p_ready"], g)
                o = bank(("probs", g))[:, 0:HB * E].rearrange("p (b e) -> p b e", e=E)
                link(dve.tensor_reduce(smalls[:, 0, :], o, AX_X, ALU.max))
                dve.tensor_tensor(small3[:, 0], o, smalls[:, 0, :].unsqueeze(2).to_broadcast([P, HB, E]),
                                  ALU.subtract).then_inc(S["probs_centered"], 1)
                dve.wait_ge(S["probs_exp"], g + 1)
                link(dve.tensor_reduce(smalls[:, 1, :], small3[:, 1], AX_X, ALU.add))
                link(dve.reciprocal(small[:, 3, :], smalls[:, 1, :]))
                dve.tensor_tensor(router_p[:, g], small3[:, 1], small[:, 3, :].unsqueeze(2).to_broadcast([P, HB, E]),
                                  ALU.mult).then_inc(S["router_p_ready"], 1)

            def gate2_(g):
                dve.wait_ge(S["gate_tanh"], g + 1)
                dve.tensor_scalar(gate(g), gate(g), 0.5, 0.5, ALU.mult, ALU.add).then_inc(S["gate_ready"], 1)

            def expert_(b):
                g, j = divmod(b, HB)
                if j == 0:
                    dve.wait_ge(S["bias2_made"], g + 1)
                dve.wait_ge(S["expert_made"], b + 1)
                o = bank(("expert", b))
                for e in range(E):
                    ins = dve.scalar_tensor_tensor(out=routed[:, b, :], in0=o[:, e * P:(e + 1) * P],
                                                   scalar=router_p[:, g, j, e:e + 1],
                                                   in1=bias2[:, b, :] if e == 0 else routed[:, b, :],
                                                   op0=ALU.mult, op1=ALU.add)
                    if e < E - 1:
                        link(ins)
                ins.then_inc(S["routed_ready"], 1)

            def out0_(g):
                dve.wait_ge(S["out0_made"], g + 1)
                dve.wait_ge(S["gate_ready"], g + 1)
                if g:
                    dve.wait_ge(S["delta_made"], g)
                dve.scalar_tensor_tensor(out=delta_t, in0=bank(("out0", g)), scalar=col("out_b"), in1=gate(g),
                                         op0=ALU.add, op1=ALU.mult).then_inc(S["delta_t_ready"], 1)

            def add_to_res(key, g):
                t = res[:, g * HB:(g + 1) * HB, :]
                dve.tensor_tensor(t, t, by_batch(bank(key)), ALU.add).then_inc(S["res_ready"], 1)

            def delta_t_(g):
                dve.wait_ge(S["delta_made"], g + 1)
                add_to_res(("delta_t", g), g)

            def head_bias(n):
                return {"kc": col("b_kvc"), "k": col("b_qkv", 1), "q": col("b_qkv"), "qc": col("b_qc")}[HEADS[n][0]]

            def proj_(n):
                dve.wait_ge(S["high_ready"], n + 1)
                dve.scalar_tensor_tensor(out=low[:, n % 2, :], in0=bank(("proj", n)), scalar=head_bias(n),
                                         in1=high[:, n % 2, :].bitcast(F32), op0=ALU.add, op1=ALU.subtract)\
                    .then_inc(S["low_ready"], 1)

            def sel_(n):
                kind, g = HEADS[n]
                t = {"kc": slots_kc, "k": slots_k, "q": slots_q, "qc": slots_q}[kind]
                if kind == "qc":
                    dve.wait_ge(S["scores_t_made"], NC * HB * (g + 1))
                for c in (0, 2):
                    dve.wait_ge(S["sel_made"], n * NC + c + 1)
                    dve.tensor_copy(half(t[:, c, :], g), bank(("sel", n, c))).then_inc(S["slots_even"], 1)

            def values_(n):
                a, g = VALUES[n]
                dve.wait_ge(S["values_made"], n + 1)
                if n:
                    dve.wait_ge(S["values_low"], n)
                o = bank(("values", n)).rearrange("p (x d) -> p x d", d=D)
                v = vals[:, a, g * HB:(g + 1) * HB].rearrange("p b h w -> p (b h) w")
                link(dve.tensor_copy(v[:, :, 0:D], o))
                dve.tensor_tensor(vrest[:, :].rearrange("p (x d) -> p x d", d=D), o, v[:, :, 0:D], ALU.subtract)\
                    .then_inc(S["values_rest"], 1)

            def scores_(i, c):
                n = i * NC + c
                dve.wait_ge(S["scores_made"], n + 1)
                if i >= 2 and c == 0:
                    dve.wait_ge(S["guard_ready"], i - 1)
                dve.tensor_reduce(guard[:, i % 2, c * HC:(c + 1) * HC], by_batch(bank(("scores", i, c))), AX_X,
                                  ALU.max, negate=True).then_inc(S["scores_read"], 1)

            def guard_(i):
                dve.wait_ge(S["scores_read"], NC * (i + 1))
                if i == 0:
                    dve.wait_ge(S["vec_const"], 1)
                if i >= 2:
                    dve.wait_ge(S["guard_t_made"], i - 1)
                link(dve.tensor_copy(guard_pair[:, i % 2, 0:NH], guard[:, i % 2, :]))
                dve.tensor_tensor(guard_pair[:, i % 2, NH:2 * NH], guard[:, i % 2, :], guard_pair[:, i % 2, 0:NH],
                                  ALU.subtract).then_inc(S["guard_ready"], 1)

            def mix_(i):
                dve.wait_ge(S["mix_made"], i + 1)
                b = i % NB
                if i >= NB and i % HB == 0:
                    dve.wait_ge(S["attn_t_made"], i // HB - 1)
                if i:
                    dve.wait_ge(S["attn_ready"], i)
                o = bank(("mix", i))[:, 0:NH * VW].rearrange("p (h w) -> p h w", w=VW)
                t = attn[:, b, :].rearrange("p (h d) -> p h d", d=D)
                link(dve.tensor_reduce(t, o[:, :, 0:3 * D].rearrange("p h (s d) -> p h d s", s=3), AX_X, ALU.add))
                ins = dve.reciprocal(rden[:], o[:, :, 3 * D])
                ins.then_inc(S["mix_read"], 1)
                dve.wait_ge(S["mix_read"], i + 1)
                dve.tensor_tensor(t, t, rden[:, :].unsqueeze(2).to_broadcast([P, NH, D]), ALU.mult)\
                    .then_inc(S["attn_ready"], 1)

            def attn_proj_(p):
                dve.wait_ge(S["attn_proj_made"], p + 1)
                o = bank(("attn_proj", p))
                if p < 2:
                    for j in range(HB):
                        b = p * HB + j
                        last = dve.tensor_scalar(y_t[:, j * P:(j + 1) * P], o[:, j * P:(j + 1) * P], col("b_proj"),
                                                 mod[:, 2, b:b + 1], ALU.add, ALU.mult)
                else:
                    last = dve.tensor_scalar(y_t, o, col("b_cproj"), None, ALU.add)
                last.then_inc(S["y_ready"], 1)

            def attn_y_(p):
                dve.wait_ge(S["attn_y_made"], p + 1)
                add_to_res(("attn_y", p), p % 2)

            def mlp2_(g):
                dve.wait_ge(S["mlp2_made"], g + 1)
                o = bank(("mlp2", g))
                for j in range(HB):
                    b = g * HB + j
                    last = dve.tensor_scalar(y_t[:, j * P:(j + 1) * P], o[:, j * P:(j + 1) * P], col("b_mlp2"),
                                             mod[:, 5, b:b + 1], ALU.add, ALU.mult)
                last.then_inc(S["y_ready"], 1)

            def last_(g):
                dve.wait_ge(S["last_made"], g + 1)
                add_to_res(("last", g), g)

            mine = {"rows": rows_, "stats": stats_, "hat": hat_, "ctx_t": ctx_t_, "kq_w": kq_w_, "anchor": anchor_,
                    "mod": mod_, "kq": kq_, "s0": s0_, "ev": ev_, "router": router_, "probs": probs_,
                    "gate2": gate2_, "expert": expert_, "out0": out0_, "delta_t": delta_t_, "proj": proj_,
                    "sel": sel_, "values": values_, "scores": scores_, "guard": guard_, "mix": mix_,
                    "attn_proj": attn_proj_, "attn_y": attn_y_, "mlp2": mlp2_, "last": last_}
            for st in steps:
                if st[0] in mine:
                    mine[st[0]](*(st[1:] or (0,)))

        @block.scalar
        def _(act):
            def bank(key):
                return banks[:, bank_of[key], :]

            for name, src in row_sources.items():
                a, n = ROW[name]
                act.dma_start(rows[a:a + n, :], src).then_inc(S["rows_in"], 16)
            act.wait_ge(S["pair_sel_made"], 1)
            act.copy(head_sel[:], pair_sel[:, :].unsqueeze(2).to_broadcast([P, NH, P])).then_inc(S["head_sel_ready"], 1)

            def rows_(_):
                act.wait_ge(S["cols_ready"], 1)
                act.activation(silu_c[:], cols_of("cond"), ACT.Silu).then_inc(S["silu_c_ready"], 1)

            def wt_(_):
                act.wait_ge(S["wt_made"], 1)
                act.copy(wt[:].rearrange("p a n -> p (a n)"), bank("wt")[:, 0:2 * P]).then_inc(S["wt_ready"], 1)

            def hat_(n):
                kind, g = NORMS[n]
                if n in hat_v:
                    return
                act.wait_ge(S["hat_t_made"], n + 1)
                if kind == "x":
                    ins = act.activation(half(x_hat_t, g), bank(("hat", n)), ACT.Identity, scale=col("gamma"),
                                         bias=col("beta"))
                else:
                    ins = act.copy(half(ctx_hat_t if kind == "c" else norm_t, g), bank(("hat", n)))
                ins.then_inc(S["hat_t_ready"], 1)

            def v0_(g):
                act.wait_ge(S["v0_made"], g + 1)
                act.copy(v0[:, g * HB:(g + 1) * HB, :], by_batch(bank(("v0", g)))).then_inc(S["v0_ready"], 1)

            def s0_(g):
                act.wait_ge(S["s0_max"], g + 1)
                if g:
                    act.wait_ge(S["p0_ready"], g)
                for j in range(HB):
                    last = act.activation(p0[:, g * HB + j, :], bank(("s0", g))[:, j * P:(j + 1) * P], ACT.Exp,
                                          scale=SCALE0, bias=small[:, 0, j:j + 1], accum_out=small[:, 1, j:j + 1])
                last.then_inc(S["s0_exp"], 1)

            def p0_t_(g):
                act.wait_ge(S["p0_t_made"], g + 1)
                act.copy(p0_t[:, g * HB:(g + 1) * HB, :], by_batch(bank(("p0_t", g)))).then_inc(S["p0_t_ready"], 1)

            def silu_by_batch(out, o, m, g):
                for j in range(HB):
                    last = act.activation(out[:, j * P:(j + 1) * P], o[:, j * P:(j + 1) * P], ACT.Silu,
                                          bias=abias[:, m, g * HB + j:g * HB + j + 1])
                return last

            def gate1_(g):
                act.wait_ge(S["abias_ready"], 1)
                act.wait_ge(S["gate1_made"], g + 1)
                silu_by_batch(gate_h(g), bank(("gate1", g)), MH, g).then_inc(S["gate_h_ready"], 1)

            def hidden_(g, m):
                n = g * MH + m
                act.wait_ge(S["hidden_made"], n + 1)
                silu_by_batch(hid(g, m), bank(("hidden", n)), m, g).then_inc(S["hidden_ready"], 1)

            def probs_(g):
                act.wait_ge(S["probs_centered"], g + 1)
                if g:
                    act.wait_ge(S["router_p_ready"], g)
                act.activation(small3[:, 1], small3[:, 0], ACT.Exp).then_inc(S["probs_exp"], 1)

            def gate2_(g):
                act.wait_ge(S["gate2_made"], g + 1)
                act.activation(gate(g), bank(("gate2", g)), ACT.Tanh, scale=0.5, bias=gate_b2_half[:, 0:1])\
                    .then_inc(S["gate_tanh"], 1)

            def routed_t_(g):
                act.wait_ge(S["routed_t_made"], g + 1)
                if g:
                    act.wait_ge(S["out0_made"], g)
                act.copy(routed_t, bank(("routed_t", g))).then_inc(S["routed_t_ready"], 1)

            def head_bias(n):
                return {"kc": col("b_kvc"), "k": col("b_qkv", 1), "q": col("b_qkv"), "qc": col("b_qc")}[HEADS[n][0]]

            def proj_(n):
                act.wait_ge(S["proj_made"], n + 1)
                if n >= 2:
                    act.wait_ge(S["sel_made"], NC * (n - 1))
                act.activation(high[:, n % 2, :], bank(("proj", n)), ACT.Identity, bias=head_bias(n))\
                    .then_inc(S["high_ready"], 1)

            def sel_(n):
                kind, g = HEADS[n]
                t = {"kc": slots_kc, "k": slots_k, "q": slots_q, "qc": slots_q}[kind]
                if kind == "qc":
                    act.wait_ge(S["scores_t_made"], NC * HB * (g + 1))
                for c in (1, 3):
                    act.wait_ge(S["sel_made"], n * NC + c + 1)
                    act.copy(half(t[:, c, :], g), bank(("sel", n, c))).then_inc(S["slots_odd"], 1)

            def guard_t_(i):
                act.wait_ge(S["guard_t_made"], i + 1)
                if i >= 2:
                    act.wait_ge(S["scores_t_made"], NC * (i - 1))
                act.copy(guard_t[:, i % 2, :], bank(("guard_t", i)).bitcast(BF16)[:, 0:P])\
                    .then_inc(S["guard_t_ready"], 1)

            def probs1_(i, c):
                n = i * NC + c
                act.wait_ge(S["scores_t_made"], n + 1)
                if n >= PR:
                    act.wait_ge(S["p_low"], n - PR + 1)
                act.activation(pf[:, n % PR, :], bank(("probs1", i, c)), ACT.Exp, scale=SCALE1)\
                    .then_inc(S["p_full"], 1)
                if i >= 2 and c == 0:
                    act.wait_ge(S["mix_made"], i - 1)
                act.activation(ph[:, i % 2, c, :], bank(("probs1", i, c)), ACT.Exp, scale=SCALE1)\
                    .then_inc(S["p_high"], 1)

            def attn_t_(p):
                act.wait_ge(S["attn_t_made"], p + 1)
                if p:
                    act.wait_ge(S["attn_proj_made"], p)
                act.activation(attn_t, bank(("attn_t", p)), ACT.Identity,
                               bias=col("b_qkv", 2) if p < 2 else col("b_kvc", 1)).then_inc(S["attn_t_ready"], 1)

            def mlp1_(g, m):
                n = g * NM + m
                act.wait_ge(S["mlp1_made"], n + 1)
                if g:
                    act.wait_ge(S["mlp2_made"], g)
                act.activation(mlp_h[:, m, :], bank(("mlp1", n)), ACT.Gelu_apprx_tanh, bias=col("b_mlp1", m))\
                    .then_inc(S["mlp1_ready"], 1)

            mine = {"rows": rows_, "wt": wt_, "hat": hat_, "v0": v0_, "s0": s0_, "p0_t": p0_t_, "gate1": gate1_,
                    "hidden": hidden_, "probs": probs_, "gate2": gate2_, "routed_t": routed_t_, "proj": proj_,
                    "sel": sel_, "guard_t": guard_t_, "probs1": probs1_, "attn_t": attn_t_, "mlp1": mlp1_}
            for st in steps:
                if st[0] in mine:
                    mine[st[0]](*(st[1:] or (0,)))

        @block.gpsimd
        def _(pool):
            chain = [0]

            def link(ins):
                chain[0] += 1
                ins.then_inc(S["pool"], 1)
                pool.wait_ge(S["pool"], chain[0])

            link(pool.memset(ident[:], 0.0))
            pool.affine_select(out=ident[:, :], in_=ident[:, :], compare_op=ALU.not_equal, fill=1.0, base=0,
                               pattern=[[-1, P]], channel_multiplier=1).then_inc(S["ident_made"], 1)
            pool.wait_ge(S["ident_made"], 1)
            pool.tensor_tensor(pair_sel[:], ident[:, 0:NH], ident[:, NH:2 * NH], ALU.add)\
                .then_inc(S["pair_sel_made"], 1)
            link(pool.memset(power[:], -0.5))

            def stats_(n):
                pool.wait_ge(S["moments_ready"], n + 1)
                if n:
                    pool.wait_ge(S["rstd_made"], n)
                link(pool.tensor_scalar(var_eps[:], moments[:, n, :, 1], EPS0 if NORMS[n][0] == "x" else EPS1, None,
                                        ALU.add))
                pool.tensor_tensor(rstd[:, n, :], var_eps[:], power[:], ALU.pow).then_inc(S["rstd_made"], 1)

            def anchor_(_):
                pool.memset(diag["k"][:].rearrange("p r c j n -> p (r c j n)").bitcast(F32), 0.0)
                pool.memset(diag["q"][:].rearrange("p r c j n -> p (r c j n)").bitcast(F32), 0.0)\
                    .then_inc(S["diag_zero"], 1)

            def probs_(g):
                pool.wait_ge(S["router_p_ready"], g + 1)
                if g:
                    pool.wait_ge(S["bias2_made"], g)
                if g == 0:
                    pool.wait_ge(S["layer0_in"], 48)
                t = bias2[:, g * HB:(g + 1) * HB, :]
                for e in range(E):
                    p = router_p[:, g, :, e:e + 1].to_broadcast([P, HB, P])
                    b = eb2[:, e:e + 1, :].to_broadcast([P, HB, P])
                    if e == 0:
                        link(pool.tensor_tensor(t, b, p, ALU.mult))
                    else:
                        link(pool.tensor_tensor(bias2_term, b, p, ALU.mult))
                        ins = pool.tensor_tensor(t, t, bias2_term, ALU.add)
                        if e < E - 1:
                            link(ins)
                ins.then_inc(S["bias2_made"], 1)

            def values_(n):
                a, g = VALUES[n]
                v = vals[:, a, g * HB:(g + 1) * HB].rearrange("p b h w -> p (b h) w")
                r = vrest[:, :].rearrange("p (x d) -> p x d", d=D)
                pool.wait_ge(S["values_rest"], n + 1)
                link(pool.tensor_copy(v[:, :, D:2 * D], r))
                pool.tensor_tensor(v[:, :, 2 * D:3 * D], r, v[:, :, D:2 * D], ALU.subtract)\
                    .then_inc(S["values_low"], 1)

            def probs1_(i, c):
                n = i * NC + c
                pool.wait_ge(S["p_high"], n + 1)
                pool.tensor_tensor(pl[:, i % 2, c, :], pf[:, n % PR, :], ph[:, i % 2, c, :], ALU.subtract)\
                    .then_inc(S["p_low"], 1)

            mine = {"stats": stats_, "anchor": anchor_, "probs": probs_, "values": values_, "probs1": probs1_}
            for st in steps:
                if st[0] in mine:
                    mine[st[0]](*(st[1:] or (0,)))

        @block.sync
        def _(sp):
            x_tok = x.rearrange("b t f -> t b f")
            c_tok = ctx.rearrange("b t f -> t b f")
            for g in range(NHALF):
                sp.dma_start(res[:, g * HB:(g + 1) * HB, :], x_tok[:, g * HB:(g + 1) * HB, :])\
                    .then_inc(S[f"x_in{g}"], 16)
            for w, src in enumerate((Wq, Wk, Wv)):
                sp.dma_start(wqkv0[:, w, :], src).then_inc(S["wqkv0_in"], 16)
            for g in range(NHALF):
                sp.dma_start(ctx_tok[:, g * HB:(g + 1) * HB, :], c_tok[:, g * HB:(g + 1) * HB, :])\
                    .then_inc(S[f"ctx_in{g}"], 16)
            sp.dma_start(gw1[:], gate_w1.rearrange("(k p) h -> p k h", p=P)).then_inc(S["gate1_in"], 16)
            sp.dma_start(rw[:], router_W.rearrange("(k p) e -> p k e", p=P)).then_inc(S["gate1_in"], 16)
            sp.dma_start(rb[:], router_b.rearrange("(e o) -> e o", o=1)).then_inc(S["gate1_in"], 16)
            sp.dma_start(ew1[:].rearrange("p e k r -> p (e k) r"), e_w1.rearrange("e (k p) r -> p (e k) r", p=P))\
                .then_inc(S["expert1_in"], 16)
            sp.dma_start(wmod[:].rearrange("p m n -> p (m n)"), W_mod).then_inc(S["mod_in"], 16)
            sp.dma_start(wkvc[:].rearrange("p m n -> p (m n)"), W_kvc).then_inc(S["heads_in"], 16)
            sp.dma_start(wqkv1[:].rearrange("p m n -> p (m n)"), W_qkv).then_inc(S["heads_in"], 16)
            sp.dma_start(wqc[:], W_qc).then_inc(S["heads_in"], 16)
            sp.dma_start(gw2[:], gate_w2).then_inc(S["layer0_in"], 16)
            sp.dma_start(ow[:], out_w).then_inc(S["layer0_in"], 16)
            sp.dma_start(eb2[:], e_b2.rearrange("e h -> (e h)").partition_broadcast(P).rearrange("p (e h) -> p e h", e=E))\
                .then_inc(S["layer0_in"], 16)
            sp.dma_start(ew2[:].rearrange("p e r h -> p (e r) h"), e_w2.rearrange("e (r p) h -> p (e r) h", p=P))\
                .then_inc(S["expert2_in"], 16)
            sp.dma_start(wproj[:, 0, :], W_proj).then_inc(S["rest_in"], 16)
            sp.dma_start(wproj[:, 1, :], W_cproj).then_inc(S["rest_in"], 16)
            sp.dma_start(wm1[:].rearrange("p m n -> p (m n)"), W_mlp1).then_inc(S["rest_in"], 16)
            sp.dma_start(wm2[:], W_mlp2.rearrange("(m p) n -> p m n", p=P)).then_inc(S["rest_in"], 16)

            sp.wait_ge(S["diag_zero"], 1)
            for i in range(NI):
                a, b = divmod(i, NB)
                for k, kind, dense, used in (("k", ("k", "kc")[a], (slots_k, slots_kc)[a], "scores_made"),
                                             ("q", ("q", "qc")[a], slots_q, "scores_t_made")):
                    n = HEADS.index((kind, b // HB))
                    sp.wait_ge(S["slots_even"], 2 * n + 2)
                    sp.wait_ge(S["slots_odd"], 2 * n + 2)
                    if i >= NR:
                        sp.wait_ge(S[used], NC * (i - NR + 1))
                    for j in range(HC):
                        at = slice(j * 4 * D, (j + 1) * 4 * D)
                        sp.dma_start(diag[k][at, i % NR, :, j, :].bitcast(F32),
                                     dense[at, :, b * P:(b + 1) * P].bitcast(F32))\
                            .then_inc(diag_in[k][i % NR], 16)

            o_tok = out.rearrange("b t f -> t b f")
            for g in range(NHALF):
                sp.wait_ge(S["res_ready"], (6, 8)[g])
                sp.dma_start(o_tok[:, g * HB:(g + 1) * HB, :], res[:, g * HB:(g + 1) * HB, :])\
                    .then_inc(S["out_done"], 16)
            sp.wait_ge(S["out_done"], 32)


_L0 = ["ln_gamma", "ln_beta", "Wq", "Wk", "Wv", "router_W", "router_b", "e_w1", "e_b1", "e_w2", "e_b2", "gate_w1",
       "gate_b1", "gate_w2", "gate_b2", "out_w", "out_b"]
_L1 = ["W_mod", "b_mod", "W_qkv", "b_qkv", "W_proj", "b_proj", "W_qc", "b_qc", "W_kvc", "b_kvc", "W_cproj",
       "b_cproj", "W_mlp1", "b_mlp1", "W_mlp2", "b_mlp2"]
_INS = ["x", "cond_1024", "ctx_1024"] + ["L0_xcond_" + n for n in _L0] + ["L1_xcond_" + n for n in _L1]
_OUTS = [((NB, P, P), "float32")]


def kernel(**inputs):
    import numpy as _np
    import concourse.bacc as _bacc
    from concourse import mybir as _mybir
    from concourse.bass_utils import run_bass_kernel_spmd as _run

    nc = _bacc.Bacc("TRN2", target_bir_lowering=False, num_devices=1)
    arrays, args = {}, []
    for name in _INS:
        a = _np.ascontiguousarray(inputs[name])
        arrays[f"in_{name}_dram"] = a
        args.append(nc.dram_tensor(f"in_{name}_dram", a.shape, _mybir.dt.from_np(a.dtype), kind="ExternalInput").ap())
    for i, (shape, dtype) in enumerate(_OUTS):
        dt = _mybir.dt.from_np(_np.dtype(dtype))
        args.append(nc.dram_tensor(f"out_{i}_dram", shape, dt, kind="ExternalOutput").ap())
    pixart_block(nc, *args)
    r = _run(nc, [arrays], core_ids=[0])
    got = tuple(r.results[0][f"out_{i}_dram"] for i in range(len(_OUTS)))
    return got[0]
```

```python
from contextlib import ExitStack

import concourse.bass as bass
from concourse import mybir

ALU = mybir.AluOpType
ACT = mybir.ActivationFunctionType
AX_X = mybir.AxisListType.X
F32 = mybir.dt.float32
F32R = mybir.dt.float32r
BF16 = mybir.dt.bfloat16
F16 = mybir.dt.float16

P = 128
NB = 8
HB = 4
NHALF = NB // HB
HN = HB * P
E = 3
MH = 6
NH = 16
D = P // NH
NC = 4
HC = NH // NC
NM = 4
VW = 3 * D + 1
NI = 2 * NB
NR = 2
PR = 3
EPS0 = 1e-5
EPS1 = 1e-6
SCALE0 = float(P) ** -0.5
SCALE1 = float(D) ** -0.5

COL = {}
for _name, _n in (("gamma", 1), ("beta", 1), ("e_b1", MH), ("gate_b1", 1), ("gate_b2", 1), ("out_b", 1), ("b_mod", 6),
                  ("b_qkv", 3), ("b_proj", 1), ("b_qc", 1), ("b_kvc", 2), ("b_cproj", 1), ("b_mlp1", NM),
                  ("b_mlp2", 1), ("cond", NB), ("router_b", 1)):
    COL[_name] = sum(n for _, n in COL.values()), _n
COLS = sum(n for _, n in COL.values())

NORMS = [("x", 0, HB), ("x", HB, HB), ("c", 0, HB), ("c", HB, HB), ("1", 0, HB), ("1", HB, HB), ("2", 0, HB),
         ("2", HB, HB), ("3", 0, HB), ("3", HB, 2), ("3", HB + 2, 2)]
HEADS = [("k", 0), ("q", 0), ("k", 1), ("q", 1), ("kc", 0), ("qc", 0), ("kc", 1), ("qc", 1)]
VALUES = [(1, 0), (1, 1), (0, 0), (0, 1)]
OUTS = [(0, 0, HB), (0, HB, HB), (1, 0, HB), (1, HB, 2), (1, HB + 2, 2)]
MLPS = [(0, HB, 8), (HB, 2, 9), (HB + 2, 2, 10)]


START = [
    ("kq_w",), ("stats", 0), ("stats", 1), ("cols",), ("norm", 0), ("kq", 0), ("kq", 1), ("norm", 1), ("v0", 0),
    ("hat", 0), ("hat", 1), ("s0", 0), ("p0", 0), ("v0", 1), ("s0", 1), ("p0", 1), ("anchor",), ("stats", 2),
    ("stats", 3), ("p0_t", 0), ("mod",), ("p0_t", 1), ("split",), ("ev", 0), ("ev", 1), ("hidden", 0, 0),
    ("hidden", 0, 1), ("norm", 2), ("hidden", 0, 2), ("hat", 2), ("hidden", 0, 3), ("hidden", 0, 4), ("norm", 3),
    ("router", 0), ("gate1", 0), ("hat", 3), ("hidden", 0, 5), ("probs", 0), ("gate2", 0), ("router_p", 0),
    ("expert", 0), ("expert", 1), ("expert", 2), ("expert", 3), ("values", 0), ("routed_t", 0), ("values", 1),
    ("hidden", 1, 0), ("hidden", 1, 1), ("out0", 0), ("delta_t", 0), ("stats", 4), ("gate1", 1), ("hidden", 1, 2),
    ("hidden", 1, 3), ("norm", 4), ("hat", 4), ("hidden", 1, 4), ("proj", 0), ("proj", 1), ("sel", 0, 0),
    ("sel", 0, 1), ("sel", 0, 2), ("sel", 0, 3), ("gate2", 1), ("sel", 1, 0), ("sel", 1, 1), ("sel", 1, 2),
    ("sel", 1, 3), ("router", 1), ("hidden", 1, 5), ("scores", 0, 0), ("scores", 0, 1), ("scores", 0, 2),
    ("scores", 0, 3), ("guard", 0), ("guard_t", 0)]
ITEM = [
    ("scores", 1, 0), ("scores", 1, 1), ("probs1", 0, 0), ("scores", 1, 2), ("probs1", 0, 1), ("scores", 1, 3),
    ("probs1", 0, 2), ("mix", -1), ("guard", 1), ("probs1", 0, 3), ("guard_t", 1)]

SIDE_WORK = {
    (0, 5): [("probs", 1)], (0, 7): [("router_p", 1)], (0, 9): [("expert", 4), ("values", 2)],
    (0, 10): [("expert", 5)], (1, 5): [("expert", 6), ("expert", 7)], (1, 8): [("routed_t", 1)],
    (1, 10): [("out0", 1)], (1, 11): [("delta_t", 1), ("stats", 5)], (2, 5): [("norm", 5)], (2, 7): [("hat", 5)],
    (2, 9): [("values", 3)],
    (2, 10): [("proj", 2), ("proj", 3), ("sel", 2, 0), ("sel", 2, 1), ("sel", 2, 2), ("sel", 2, 3), ("sel", 3, 0), ("sel", 3, 1)],
    (2, 11): [("sel", 3, 2), ("sel", 3, 3)], (5, 1): [("attn_t", 0), ("attn_proj", 0)],
    (5, 3): [("attn_y", 0), ("stats", 6), ("proj", 4)], (5, 10): [("sel", 4, 0), ("sel", 4, 1)],
    (6, 1): [("norm", 6), ("sel", 4, 2), ("sel", 4, 3)], (6, 2): [("hat", 6)], (6, 4): [("proj", 5)],
    (6, 6): [("sel", 5, 0), ("sel", 5, 1), ("sel", 5, 2)], (6, 9): [("sel", 5, 3)], (7, 1): [("proj", 6)],
    (8, 10): [("attn_t", 1)], (9, 4): [("attn_proj", 1)], (9, 6): [("attn_y", 1)], (9, 7): [("stats", 7)],
    (9, 8): [("sel", 6, 0)], (9, 9): [("sel", 6, 1)], (9, 11): [("norm", 7)],
    (10, 2): [("sel", 6, 2), ("sel", 6, 3)], (10, 3): [("hat", 7)], (10, 4): [("proj", 7)],
    (10, 7): [("sel", 7, 0), ("sel", 7, 1), ("sel", 7, 2), ("sel", 7, 3)], (12, 11): [("attn_t", 2)],
    (13, 5): [("attn_proj", 2)], (13, 10): [("attn_y", 2), ("stats", 8)], (14, 3): [("norm", 8)],
    (14, 11): [("attn_t", 3)], (15, 5): [("attn_proj", 3), ("hat", 8)],
    (15, 10): [("attn_y", 3), ("stats", 9), ("norm", 9), ("mlp1", 0, 0), ("mlp1", 0, 1), ("mlp1", 0, 2)]}
END = [
    ("hat", 9), ("mlp1", 0, 3), ("attn_t", 4), ("mlp2", 0), ("attn_proj", 4), ("attn_y", 4), ("mlp1", 1, 0),
    ("mlp1", 1, 1), ("mlp1", 1, 2), ("stats", 10), ("norm", 10), ("mlp1", 1, 3), ("last", 0), ("hat", 10),
    ("mlp2", 1), ("mlp1", 2, 0), ("mlp1", 2, 1), ("mlp1", 2, 2), ("mlp1", 2, 3), ("mlp2", 2), ("last", 1),
    ("last", 2)]


def schedule():
    o = list(START)
    for i in range(NI):
        o += SIDE_WORK.get((i, 0), [])
        for k, (kind, ahead, *c) in enumerate(ITEM):
            if 0 <= i + ahead < NI:
                o.append((kind, i + ahead, *c))
            o += SIDE_WORK.get((i, k + 1), [])
    o += [("mix", NI - 1)] + END
    return [st if len(st) > 1 else st + (0,) for st in o]


FIRST = [("cols", COLS), ("WqT", P), ("WkT", P), ("Wv", P)]
HIDDEN = [("gate_w1", 3 * P), ("router_W", 3 * E), ("e_w1", E * 3 * 2 * P)]
SECOND = [("gate_w2", P), ("out_w", P), ("e_w2", E * 2 * P)]
LAYER1 = [("W_mod", 6 * P), ("W_qkv", 3 * P), ("W_kvc", 2 * P), ("W_qc", P)]
LATE = [("W_proj", P), ("W_cproj", P), ("W_mlp1", NM * P), ("W_mlp2", NM * P)]


def width(parts):
    return sum(n for _, n in parts)


def pixart_block(nc, x, ctx, ctx_turned, first, hidden_w, second, layer1, late, e_b2, out):
    steps = schedule()

    with ExitStack() as stack:
        def sb(name, shape, dt=F32):
            return stack.enter_context(nc.sbuf_tensor(name, shape, dt))

        def sem(name):
            return stack.enter_context(nc.semaphore(name))

        res = sb("res", [P, NB, P])
        ctx_tok = sb("ctx_tok", [P, NB, P])
        first_sb = sb("first_sb", [P, width(FIRST)])
        hidden_sb = sb("hidden_sb", [P, width(HIDDEN)])
        second_sb = sb("second_sb", [P, width(SECOND)])
        layer1_sb = sb("layer1_sb", [P, width(LAYER1)])
        late_sb = sb("late_sb", [P, width(LATE)])
        eb2 = sb("eb2", [P, E * P])

        def cut(tile, parts, name):
            names = [n for n, _ in parts]
            at = width(parts[:names.index(name)])
            return tile[:, at:at + parts[names.index(name)][1]]

        cols = cut(first_sb, FIRST, "cols")
        wq_t = cut(first_sb, FIRST, "WqT")
        wk_t = cut(first_sb, FIRST, "WkT")
        wv = cut(first_sb, FIRST, "Wv")
        gw1 = cut(hidden_sb, HIDDEN, "gate_w1").rearrange("p (k h) -> p k h", k=3)
        rw = cut(hidden_sb, HIDDEN, "router_W").rearrange("p (k e) -> p k e", k=3)
        ew1 = cut(hidden_sb, HIDDEN, "e_w1").rearrange("p (e k r) -> p e k r", e=E, k=3)
        gw2 = cut(second_sb, SECOND, "gate_w2")
        ow = cut(second_sb, SECOND, "out_w")
        ew2 = cut(second_sb, SECOND, "e_w2").rearrange("p (e r h) -> p e r h", e=E, r=2)
        wmod = cut(layer1_sb, LAYER1, "W_mod").rearrange("p (m n) -> p m n", m=6)
        wqkv1 = cut(layer1_sb, LAYER1, "W_qkv").rearrange("p (m n) -> p m n", m=3)
        wkvc = cut(layer1_sb, LAYER1, "W_kvc").rearrange("p (m n) -> p m n", m=2)
        wqc = cut(layer1_sb, LAYER1, "W_qc")
        wproj = [cut(late_sb, LATE, "W_proj"), cut(late_sb, LATE, "W_cproj")]
        wm1 = cut(late_sb, LATE, "W_mlp1").rearrange("p (m n) -> p m n", m=NM)
        wm2 = cut(late_sb, LATE, "W_mlp2").rearrange("p (m n) -> p m n", m=NM)

        ident = sb("ident", [P, P])
        ident_h = sb("ident_h", [P, P], BF16)
        slot_sel = sb("slot_sel", [P, 4, NC, HC, 4, D], F32R)
        pair_sel = sb("pair_sel", [P, NH])
        head_sel = sb("head_sel", [P, NH, P], BF16)
        power = sb("power", [P, HB])
        share = sb("share", [P, P], BF16)
        eb2_parts = sb("eb2_parts", [P, E * P], BF16)

        gate_b2_half = sb("gate_b2_half", [P, 1])
        silu_c = sb("silu_c", [P, NB])
        kq_w = sb("kq_w", [P, P])
        abias = sb("abias", [P, MH + 1, NB])
        rbias = sb("rbias", [E, NB])
        mod = sb("mod", [P, 6, NB])
        mod1 = sb("mod1", [P, 2, NB])
        bn = sb("bn", [P, HB, 6])
        moments = sb("moments", [P, len(NORMS), HB, 2])
        rstd = sb("rstd", [P, len(NORMS), HB])
        var_eps = sb("var_eps", [P, HB])
        small = sb("small", [P, 4, HB])
        small3 = sb("small3", [P, 4, HB, E])
        smallm = sb("smallm", [P, HB])
        smalls = sb("smalls", [P, 2, HB])
        router_p = sb("router_p", [P, NHALF, HB, E])
        guard = sb("guard", [P, 2, NH])
        guard_pair = sb("guard_pair", [P, 2, P], BF16)
        guard_t = sb("guard_t", [P, 2, P], BF16)
        rden = sb("rden", [P, NH])

        ctx_hat_t = sb("ctx_hat_t", [P, NB * P])
        norm_t = sb("norm_t", [P, NB * P])
        hat = sb("hat", [P, 2, HB, P])
        high = sb("high", [P, 2, HN], F32R)
        low = sb("low", [P, 2, HN], F32R)
        diag = {k: sb("diag_" + k, [P, NR, HC, NC, P], F32R) for k in "kq"}
        vals = sb("vals", [P, 2, NB, NH, VW], BF16)
        vrest = sb("vrest", [P, HN])
        slots_q = sb("slots_q", [P, NB, NC, P], F32R)
        slots_k = sb("slots_k", [P, NB, NC, P], F32R)

        arena0 = sb("arena0", [P, 6144])
        ev_t = arena0[:, 0:1024]
        hidden = arena0[:, 1024:4096].rearrange("p (m n) -> p m n", m=MH)
        gate = [arena0[:, 4096:4608], arena0[:, 4608:5120]]
        logit_t = arena0[:, 5120:5632]
        routed_t = arena0[:, 5120:5632]
        delta_t = arena0[:, 5632:6144]
        mlp_h = [arena0[:, 1024:3072], arena0[:, 3072:4096], arena0[:, 4096:5120]]
        mlp_y = [arena0[:, 5120:5632], arena0[:, 5632:5888], arena0[:, 5888:6144]]
        routed = ctx_tok
        x_hat_t = norm_t

        arena1 = sb("arena1", [P, 7680])

        def part(at, n):
            return arena1[:, at:at + n]

        ctx_t, kq_t = part(0, 1024), part(1024, 1024)
        v0 = part(2048, 1024).rearrange("p (b n) -> p b n", b=NB)
        p0 = part(3072, 1024).rearrange("p (b n) -> p b n", b=NB)
        p0_t = part(4096, 1024).rearrange("p (b n) -> p b n", b=NB)

        pf = part(0, PR * HN).rearrange("p (r n) -> p r n", r=PR)
        ph = part(1536, 2048).bitcast(F16).rearrange("p (r c n) -> p r c n", r=2, c=NC)
        pl = part(3584, 2048).bitcast(F16).rearrange("p (r c n) -> p r c n", r=2, c=NC)
        attn = part(5632, 1024).rearrange("p (b n) -> p b n", b=NB)
        attn_t = part(6656, 512)
        y_t = part(7168, 512)

        banks = stack.enter_context(nc.psum_tensor("banks", [P, 8, HN], F32))

        S = {n: sem(n) for n in (
            "x_in0", "x_in1", "ctx_in", "ctx_turned_in", "first_in", "hidden_w_in", "second_in", "layer1_in",
            "late_in", "eb2_in", "out_done",
            "pool", "ident_made", "pair_sel_made", "diag_zero", "rstd_made", "eb2_split", "values_low", "p_low",
            "hat_t_made", "kq_w_made", "anchor_made", "mod_made", "kq_made",
            "v0_made", "s0_made", "p0_t_made", "ev_made", "gate1_made", "hidden_made", "router_made", "probs_t_made",
            "gate2_made", "expert_made", "routed_t_made", "out0_made", "delta_made", "proj_made", "sel_made",
            "values_made", "guard_t_made", "scores_made", "scores_t_made", "mix_made", "attn_t_made",
            "attn_proj_made", "attn_y_made", "mlp1_made", "mlp2_made", "last_made",
            "vec", "vec_const", "cols_ready", "kq_w_ready", "abias_ready", "mod_ready", "moments_ready", "hat_ready",
            "norm_t_ready", "kq_ready", "s0_max", "p0_ready", "ev_ready", "router_ready",
            "probs_centered", "router_p_ready", "gate_ready", "routed_ready", "delta_t_ready", "res_ready",
            "low_ready", "slots_even", "values_high", "values_rest", "guard_ready", "scores_read", "mix_read",
            "attn_ready", "y_ready",
            "head_sel_ready", "silu_c_ready", "hat_t_ready", "v0_ready", "s0_exp", "p0_t_ready", "gate_h_ready",
            "hidden_ready", "probs_exp", "gate_tanh", "routed_t_ready", "high_ready", "slots_odd", "guard_t_ready",
            "p_full", "p_high", "attn_t_ready", "mlp1_ready")}
        diag_in = {k: [sem(f"diag_{k}_in{r}") for r in range(NR)] for k in "kq"}

        def col(name, j=0):
            a = COL[name][0] + j
            return cols[:, a:a + 1]

        def cols_of(name):
            a, n = COL[name]
            return cols[:, a:a + n]

        def half(t, g):
            return t[:, g * HN:(g + 1) * HN]

        def tok(t, b):
            return t[:, b * P:(b + 1) * P]

        def within(t, b0, nb):
            return t[:, (b0 % HB) * P:(b0 % HB + nb) * P]

        def by_batch(ap):
            return ap.rearrange("p (b n) -> p b n", b=HB)

        def turns(*kinds):
            chosen = [st for st in steps if st[0] in kinds]
            return {st: k + 1 for k, st in enumerate(chosen)}

        norm_turn = turns("stats")
        hat_order = [st[1] for st in steps if st[0] == "hat"]
        hat_a = [n for n in hat_order if NORMS[n][0] in "xc2"]
        hat_v = [n for n in hat_order if NORMS[n][0] in "13"]
        y_turn = turns("attn_proj", "mlp2")
        res_turn = turns("delta_t", "attn_y", "last")
        bank_of = {}
        block = stack.enter_context(nc.Block())

        @block.tensor
        def _(pe):
            released = {}
            turn = [0]

            def claim(key, reader, count, among):
                bank = among[turn[0] % len(among)]
                turn[0] += 1
                bank_of[key] = bank
                if bank in released:
                    pe.wait_ge(S[released[bank][0]], released[bank][1])
                released[bank] = (reader, count)
                return banks[:, bank, :]

            ALL = list(range(8))
            SIDE = [6, 7]
            loop = [False]

            def free():
                return SIDE if loop[0] else ALL

            def transposes(o, src, b0, nb=HB):
                for j in range(nb):
                    last = pe.transpose(o[:, j * P:(j + 1) * P], src[:, b0 + j, :], ident[:, :])
                return last

            def hat_(n):
                k = norm_turn["stats", n]
                pe.wait_ge(S["hat_ready"], k)
                if n in hat_a:
                    o = claim(("hat", n), "hat_t_ready", hat_a.index(n) + 1, free())
                else:
                    o = claim(("hat", n), "norm_t_ready", hat_v.index(n) + 1, free())
                transposes(o, hat[:, k % 2], 0, NORMS[n][2]).then_inc(S["hat_t_made"], 1)

            def kq_w_(_):
                pe.wait_ge(S["first_in"], 16)
                o = claim("kq_w", "kq_w_ready", 1, ALL)
                pe.matmul(o[:, 0:P], wk_t, wq_t, start=True, stop=True).then_inc(S["kq_w_made"], 1)

            def anchor_(_):
                pe.wait_ge(S["hidden_w_in"], 16)
                o = claim("anchor", "abias_ready", 1, ALL)
                c = cols_of("cond")
                for m in range(MH):
                    pe.matmul(o[:, m * NB:(m + 1) * NB], ew1[:, m // 2, 2, (m % 2) * P:(m % 2 + 1) * P], c,
                              start=True, stop=True)
                pe.matmul(o[:, MH * NB:(MH + 1) * NB], gw1[:, 2, :], c, start=True, stop=True)
                pe.matmul(o[0:E, (MH + 1) * NB:(MH + 2) * NB], rw[:, 2, :], c, start=True, stop=True)\
                    .then_inc(S["anchor_made"], 1)

            def mod_(_):
                pe.wait_ge(S["silu_c_ready"], 1)
                pe.wait_ge(S["layer1_in"], 16)
                o = claim("mod", "mod_ready", 1, ALL)
                for j in range(6):
                    last = pe.matmul(o[:, j * NB:(j + 1) * NB], wmod[:, j, :], silu_c[:, :], start=True, stop=True)
                last.then_inc(S["mod_made"], 1)

            def kq_(g):
                if g == 0:
                    pe.wait_ge(S["kq_w_ready"], 1)
                    pe.wait_ge(S["ctx_turned_in"], 16)
                o = claim(("kq", g), "kq_ready", g + 1, ALL)
                pe.matmul(o, kq_w[:, :], half(ctx_t, g), start=True, stop=True).then_inc(S["kq_made"], 1)

            def v0_(g):
                if g == 0:
                    pe.wait_ge(S["first_in"], 16)
                    pe.wait_ge(S["ctx_turned_in"], 16)
                o = claim(("v0", g), "v0_ready", g + 1, ALL)
                for j in range(HB):
                    last = pe.matmul(o[:, j * P:(j + 1) * P], tok(ctx_t, g * HB + j), wv,
                                     start=True, stop=True)
                last.then_inc(S["v0_made"], 1)

            def s0_(g):
                pe.wait_ge(S["kq_ready"], g + 1)
                pe.wait_ge(S["hat_t_ready"], hat_a.index(g) + 1)
                o = claim(("s0", g), "s0_exp", g + 1, ALL)
                for j in range(HB):
                    b = g * HB + j
                    last = pe.matmul(o[:, j * P:(j + 1) * P], tok(x_hat_t, b), tok(kq_t, b), start=True, stop=True)
                last.then_inc(S["s0_made"], 1)

            def p0_t_(g):
                pe.wait_ge(S["p0_ready"], g + 1)
                o = claim(("p0_t", g), "p0_t_ready", g + 1, ALL)
                transposes(o, p0, g * HB).then_inc(S["p0_t_made"], 1)

            def ev_(g):
                pe.wait_ge(S["v0_ready"], g + 1)
                pe.wait_ge(S["p0_t_ready"], g + 1)
                o = claim(("ev", g), "ev_ready", g + 1, ALL)
                for j in range(HB):
                    b = g * HB + j
                    last = pe.matmul(o[:, j * P:(j + 1) * P], v0[:, b, :], p0_t[:, b, :], start=True, stop=True)
                last.then_inc(S["ev_made"], 1)

            def pair(o, lhs, g):
                pe.matmul(o, lhs(0), half(x_hat_t, g), start=True, stop=False)
                return pe.matmul(o, lhs(1), half(ev_t, g), start=False, stop=True)

            def combined_ready(g):
                pe.wait_ge(S["ev_ready"], g + 1)
                if g == 0:
                    pe.wait_ge(S["hidden_w_in"], 16)

            def gate1_(g):
                combined_ready(g)
                o = claim(("gate1", g), "gate_h_ready", g + 1, ALL)
                pair(o, lambda k: gw1[:, k, :], g).then_inc(S["gate1_made"], 1)

            def hidden_(g, m):
                n = g * MH + m
                if m == 0:
                    combined_ready(g)
                o = claim(("hidden", n), "hidden_ready", n + 1, ALL)
                pair(o, lambda k: ew1[:, m // 2, k, (m % 2) * P:(m % 2 + 1) * P], g).then_inc(S["hidden_made"], 1)

            def router_(g):
                combined_ready(g)
                o = claim(("router", g), "router_ready", g + 1, ALL)
                pair(o[0:E, :], lambda k: rw[:, k, :], g).then_inc(S["router_made"], 1)

            def probs_(g):
                pe.wait_ge(S["router_ready"], g + 1)
                o = claim(("probs", g), "probs_centered", g + 1, ALL)
                for j in range(HB):
                    last = pe.transpose(o[:, j * E:(j + 1) * E], logit_t[0:E, j * P:(j + 1) * P], ident[0:E, 0:E])
                last.then_inc(S["probs_t_made"], 1)

            def gate2_(g):
                pe.wait_ge(S["gate_h_ready"], g + 1)
                pe.wait_ge(S["second_in"], 16)
                o = claim(("gate2", g), "gate_tanh", g + 1, ALL)
                pe.matmul(o, gw2, gate[g], start=True, stop=True).then_inc(S["gate2_made"], 1)

            def expert_(b):
                if b % HB == 0:
                    pe.wait_ge(S["hidden_ready"], MH * (b // HB + 1))
                    pe.wait_ge(S["second_in"], 16)
                if b == 0:
                    pe.wait_ge(S["eb2_split"], 1)
                o = claim(("expert", b), "routed_ready", b + 1, ALL)
                pe.matmul(o[:, 0:E * P], share[:, :], eb2_parts[:, :], start=True, stop=False)
                for e in range(E):
                    for r in range(2):
                        last = pe.matmul(o[:, e * P:(e + 1) * P], tok(hidden[:, 2 * e + r, :], b % HB),
                                         ew2[:, e, r, :], start=False, stop=(e == E - 1 and r == 1))
                last.then_inc(S["expert_made"], 1)

            def routed_t_(g):
                pe.wait_ge(S["routed_ready"], HB * (g + 1))
                o = claim(("routed_t", g), "routed_t_ready", g + 1, ALL)
                transposes(o, routed, g * HB).then_inc(S["routed_t_made"], 1)

            def out0_(g):
                pe.wait_ge(S["routed_t_ready"], g + 1)
                o = claim(("out0", g), "delta_t_ready", g + 1, ALL)
                pe.matmul(o, ow, routed_t, start=True, stop=True).then_inc(S["out0_made"], 1)

            def delta_t_(g):
                pe.wait_ge(S["delta_t_ready"], g + 1)
                o = claim(("delta_t", g), "res_ready", res_turn["delta_t", g], ALL)
                transposes(o, by_batch(delta_t), 0).then_inc(S["delta_made"], 1)

            def proj_(n):
                kind, g = HEADS[n]
                if n == 0:
                    pe.wait_ge(S["layer1_in"], 16)
                src, w = {"kc": (ctx_hat_t, wkvc[:, 0, :]), "k": (norm_t, wqkv1[:, 1, :]),
                          "q": (norm_t, wqkv1[:, 0, :]), "qc": (norm_t, wqc)}[kind]
                if kind == "kc":
                    pe.wait_ge(S["hat_t_ready"], hat_a.index(NORMS.index(("c", g * HB, HB))) + 1)
                elif kind == "qc":
                    pe.wait_ge(S["hat_t_ready"], hat_a.index(NORMS.index(("2", g * HB, HB))) + 1)
                else:
                    pe.wait_ge(S["norm_t_ready"], hat_v.index(NORMS.index(("1", g * HB, HB))) + 1)
                o = claim(("proj", n), "low_ready", n + 1, free())
                pe.matmul(o, w, half(src, g), start=True, stop=True).then_inc(S["proj_made"], 1)

            def sel_(n, c):
                k = 2 if HEADS[n][0][0] == "k" else 0
                pe.wait_ge(S["vec_const"], 1)
                pe.wait_ge(S["low_ready"], n + 1)
                reader = ("slots_even", "slots_odd")[c % 2], 2 * n + c // 2 + 1
                o = claim(("sel", n, c), *reader, free())
                pe.matmul(o, slot_sel[:, k, c].rearrange("p j s d -> p (j s d)"), high[:, n % 2, :],
                          start=True, stop=False)
                pe.matmul(o, slot_sel[:, k + 1, c].rearrange("p j s d -> p (j s d)"), low[:, n % 2, :],
                          start=False, stop=True).then_inc(S["sel_made"], 1)

            def values_(n):
                a, g = VALUES[n]
                if a:
                    pe.wait_ge(S["hat_t_ready"], hat_a.index(NORMS.index(("c", g * HB, HB))) + 1)
                else:
                    pe.wait_ge(S["norm_t_ready"], hat_v.index(NORMS.index(("1", g * HB, HB))) + 1)
                src, w = ((norm_t, wqkv1[:, 2, :]), (ctx_hat_t, wkvc[:, 1, :]))[a]
                if n == 0:
                    pe.wait_ge(S["layer1_in"], 16)
                o = claim(("values", n), "values_rest", n + 1, free())
                for j in range(HB):
                    last = pe.matmul(o[:, j * P:(j + 1) * P], tok(src, g * HB + j), w, start=True, stop=True)
                last.then_inc(S["values_made"], 1)

            def scores_(i, c):
                loop[0] = True
                b = i % NB
                if c == 0:
                    pe.wait_ge(diag_in["k"][i % NR], 16 * HC * (i // NR + 1))
                    if i % HB == 0:
                        n = HEADS.index((("q", "qc")[i // NB], b // HB))
                        pe.wait_ge(S["slots_even"], 2 * n + 2)
                        pe.wait_ge(S["slots_odd"], 2 * n + 2)
                bank = [0, 1, 2][(i * NC + c) % 3]
                o = claim(("scores", i, c), "scores_read", i * NC + c + 1, [bank])
                pe.matmul(o, slots_q[:, b, c, :], diag["k"][:, i % NR, :, c, :],
                          start=True, stop=True).then_inc(S["scores_made"], 1)

            def guard_t_(i):
                pe.wait_ge(S["guard_ready"], i + 1)
                o = claim(("guard_t", i), "guard_t_ready", i + 1, free())
                pe.transpose(o.bitcast(BF16)[:, 0:P], guard_pair[:, i % 2, :], ident_h[:, :])\
                    .then_inc(S["guard_t_made"], 1)

            def probs1_(i, c):
                b = i % NB
                if c == 0:
                    pe.wait_ge(diag_in["q"][i % NR], 16 * HC * (i // NR + 1))
                    pe.wait_ge(S["guard_t_ready"], i + 1)
                    if i == 0:
                        pe.wait_ge(S["head_sel_ready"], 1)
                bank = [3, 4][(i * NC + c) % 2]
                o = claim(("probs1", i, c), "p_high", i * NC + c + 1, [bank])
                pe.matmul(o, slots_k[:, b, c, :], diag["q"][:, i % NR, :, c, :],
                          start=True, stop=False)
                for j in range(HC):
                    last = pe.matmul(o[:, j * P:(j + 1) * P], head_sel[:, c * HC + j, :], guard_t[:, i % 2, :],
                                     start=False, stop=(j == HC - 1))
                last.then_inc(S["scores_t_made"], 1)

            def mix_(i):
                a, b = divmod(i, NB)
                if b % HB == 0:
                    pe.wait_ge(S["values_low"], VALUES.index((a, b // HB)) + 1)
                pe.wait_ge(S["p_high"], NC * (i + 1))
                pe.wait_ge(S["p_low"], NC * (i + 1))
                o = claim(("mix", i), "mix_read", i + 1, [5])
                for h in range(NH):
                    c, j = divmod(h, HC)
                    at = o[:, h * VW:(h + 1) * VW]
                    pe.matmul(at, ph[:, i % 2, c, j * P:(j + 1) * P], vals[:, a, b, h, :], start=True, stop=False)
                    last = pe.matmul(at, pl[:, i % 2, c, j * P:(j + 1) * P], vals[:, a, b, h, :],
                                     start=False, stop=True)
                last.then_inc(S["mix_made"], 1)

            def attn_t_(p):
                a, b0, nb = OUTS[p]
                pe.wait_ge(S["attn_ready"], a * NB + b0 + nb)
                o = claim(("attn_t", p), "attn_t_ready", p + 1, free())
                transposes(o, attn, b0, nb).then_inc(S["attn_t_made"], 1)

            def attn_proj_(p):
                a, b0, nb = OUTS[p]
                pe.wait_ge(S["late_in"], 16)
                pe.wait_ge(S["attn_t_ready"], p + 1)
                o = claim(("attn_proj", p), "y_ready", y_turn["attn_proj", p], free())
                pe.matmul(o[:, 0:nb * P], wproj[a], within(attn_t, b0, nb), start=True, stop=True)\
                    .then_inc(S["attn_proj_made"], 1)

            def attn_y_(p):
                a, b0, nb = OUTS[p]
                pe.wait_ge(S["y_ready"], y_turn["attn_proj", p])
                o = claim(("attn_y", p), "res_ready", res_turn["attn_y", p], free())
                transposes(o, by_batch(y_t), b0 % HB, nb).then_inc(S["attn_y_made"], 1)

            def mlp1_(g, m):
                b0, nb, n = MLPS[g]
                if m == 0:
                    pe.wait_ge(S["norm_t_ready"], hat_v.index(n) + 1)
                k = g * NM + m
                o = claim(("mlp1", k), "mlp1_ready", k + 1, free())
                pe.matmul(o[:, 0:nb * P], wm1[:, m, :], norm_t[:, b0 * P:(b0 + nb) * P], start=True, stop=True)\
                    .then_inc(S["mlp1_made"], 1)

            def mlp2_(g):
                nb = MLPS[g][1]
                o = claim(("mlp2", g), "y_ready", y_turn["mlp2", g], free())
                for m in range(NM):
                    pe.wait_ge(S["mlp1_ready"], g * NM + m + 1)
                    last = pe.matmul(o[:, 0:nb * P], wm2[:, m, :], mlp_h[g][:, m * nb * P:(m + 1) * nb * P],
                                     start=(m == 0), stop=(m == NM - 1))
                last.then_inc(S["mlp2_made"], 1)

            def last_(g):
                nb = MLPS[g][1]
                pe.wait_ge(S["y_ready"], y_turn["mlp2", g])
                o = claim(("last", g), "res_ready", res_turn["last", g], free())
                transposes(o, mlp_y[g].rearrange("p (b n) -> p b n", b=nb), 0, nb).then_inc(S["last_made"], 1)

            mine = {"hat": hat_, "kq_w": kq_w_, "anchor": anchor_, "mod": mod_, "kq": kq_, "v0": v0_, "s0": s0_, "p0_t": p0_t_, "ev": ev_, "gate1": gate1_,
                    "hidden": hidden_, "router": router_, "probs": probs_, "gate2": gate2_, "expert": expert_,
                    "routed_t": routed_t_, "out0": out0_, "delta_t": delta_t_, "proj": proj_, "sel": sel_,
                    "values": values_, "scores": scores_, "guard_t": guard_t_, "probs1": probs1_, "mix": mix_,
                    "attn_t": attn_t_, "attn_proj": attn_proj_, "attn_y": attn_y_, "mlp1": mlp1_, "mlp2": mlp2_,
                    "last": last_}
            for st in steps:
                if st[0] in mine:
                    mine[st[0]](*st[1:])

        @block.vector
        def _(dve):
            chain = [0]

            def link(ins):
                chain[0] += 1
                ins.then_inc(S["vec"], 1)
                dve.wait_ge(S["vec"], chain[0])

            def bank(key):
                return banks[:, bank_of[key], :]

            link(dve.memset(slot_sel[:].rearrange("p a c j s d -> p (a c j s d)").bitcast(F32), 0.0))
            dve.memset(guard_pair[:], 0.0)
            dve.memset(vals[:, :, :, :, 3 * D:VW].rearrange("p a b h o -> p (a b h o)"), 1.0)
            dve.wait_ge(S["ident_made"], 1)
            dve.tensor_copy(ident_h[:], ident[:])
            src = ident[:, :].rearrange("p (c j d) -> p c j d", c=NC, j=HC)
            for a, slots in enumerate(((0, 2), (1, 3), (0, 1), (2, 3))):
                for s in slots:
                    last = dve.tensor_copy(slot_sel[:, a, :, :, s, :], src)
            last.then_inc(S["vec_const"], 1)

            def cols_(_):
                dve.wait_ge(S["first_in"], 16)
                dve.tensor_scalar(gate_b2_half[:], col("gate_b2"), 0.5, None, ALU.mult).then_inc(S["cols_ready"], 1)

            def stats_(n):
                kind, b0, nb = NORMS[n]
                k = norm_turn["stats", n]
                if kind == "x":
                    dve.wait_ge(S[f"x_in{b0 // HB}"], 16)
                elif kind == "c":
                    dve.wait_ge(S["ctx_in"], 16)
                else:
                    before = {4: ("delta_t", 0), 5: ("delta_t", 1), 6: ("attn_y", 0), 7: ("attn_y", 1),
                              8: ("attn_y", 2), 9: ("attn_y", 3), 10: ("attn_y", 4)}[n]
                    dve.wait_ge(S["res_ready"], res_turn[before])
                if k > 1:
                    dve.wait_ge(S["moments_ready"], k - 1)
                t = ctx_tok if kind == "c" else res
                for j in range(nb):
                    last = dve.bn_stats(bn[:, j, :], t[:, b0 + j, :])
                link(last)
                for j in range(nb):
                    last = dve.bn_aggr(moments[:, n, j, :], bn[:, j, :])
                last.then_inc(S["moments_ready"], 1)

            def norm_(n):
                kind, b0, nb = NORMS[n]
                k = norm_turn["stats", n]
                t = ctx_tok if kind == "c" else res
                dve.wait_ge(S["rstd_made"], k)
                if k > 2:
                    dve.wait_ge(S["hat_t_made"], k - 2)
                for j in range(nb):
                    last = dve.tensor_scalar(hat[:, k % 2, j, :], t[:, b0 + j, :], moments[:, n, j, 0:1],
                                             rstd[:, n, j:j + 1], ALU.subtract, ALU.mult)
                last.then_inc(S["hat_ready"], 1)

            def hat_(n):
                kind, b0, nb = NORMS[n]
                if n in hat_v:
                    a = 0 if kind == "1" else 1
                    dve.wait_ge(S["mod_ready"], 1)
                    dve.wait_ge(S["hat_t_made"], norm_turn["stats", n])
                    for j in range(nb):
                        b = b0 + j
                        last = dve.tensor_scalar(tok(norm_t, b), bank(("hat", n))[:, j * P:(j + 1) * P],
                                                 mod1[:, a, b:b + 1], mod[:, 3 * a, b:b + 1], ALU.mult, ALU.add)
                    last.then_inc(S["norm_t_ready"], 1)

            def kq_w_(_):
                dve.wait_ge(S["kq_w_made"], 1)
                dve.tensor_copy(kq_w[:], bank("kq_w")[:, 0:P]).then_inc(S["kq_w_ready"], 1)

            def anchor_(_):
                dve.wait_ge(S["anchor_made"], 1)
                o = bank("anchor")
                a = COL["e_b1"][0]
                dve.tensor_scalar(rbias[:], o[0:E, (MH + 1) * NB:(MH + 2) * NB], col("router_b")[0:E], None, ALU.add)
                dve.tensor_tensor(abias[:], o[:, 0:(MH + 1) * NB].rearrange("p (m b) -> p m b", b=NB),
                                  cols[:, a:a + MH + 1].unsqueeze(2).to_broadcast([P, MH + 1, NB]), ALU.add)\
                    .then_inc(S["abias_ready"], 1)

            def mod_(_):
                dve.wait_ge(S["mod_made"], 1)
                link(dve.tensor_tensor(mod[:], bank("mod")[:, 0:6 * NB].rearrange("p (m b) -> p m b", b=NB),
                                       cols_of("b_mod").unsqueeze(2).to_broadcast([P, 6, NB]), ALU.add))
                dve.tensor_scalar(mod1[:], mod[:, 1:6:3, :], 1.0, None, ALU.add).then_inc(S["mod_ready"], 1)

            def kq_(g):
                dve.wait_ge(S["kq_made"], g + 1)
                dve.tensor_copy(half(kq_t, g), bank(("kq", g))).then_inc(S["kq_ready"], 1)

            def s0_(g):
                dve.wait_ge(S["s0_made"], g + 1)
                if g:
                    dve.wait_ge(S["p0_ready"], g)
                link(dve.tensor_reduce(smallm[:], by_batch(bank(("s0", g))), AX_X, ALU.max, negate=True))
                if g:
                    dve.wait_ge(S["s0_exp"], g)
                dve.tensor_scalar(small[:, 0, :], smallm[:], SCALE0, None, ALU.mult).then_inc(S["s0_max"], 1)

            def p0_(g):
                dve.wait_ge(S["s0_exp"], g + 1)
                link(dve.reciprocal(small[:, 2, :], small[:, 1, :]))
                t = p0[:, g * HB:(g + 1) * HB, :]
                dve.tensor_tensor(t, t, small[:, 2, :].unsqueeze(2).to_broadcast([P, HB, P]), ALU.mult)\
                    .then_inc(S["p0_ready"], 1)

            def ev_(g):
                dve.wait_ge(S["ev_made"], g + 1)
                dve.tensor_copy(half(ev_t, g), bank(("ev", g))).then_inc(S["ev_ready"], 1)

            def router_(g):
                dve.wait_ge(S["router_made"], g + 1)
                if g == 0:
                    dve.wait_ge(S["abias_ready"], 1)
                if g:
                    dve.wait_ge(S["probs_t_made"], g)
                    dve.wait_ge(S["out0_made"], g)
                dve.tensor_tensor(by_batch(logit_t[0:E, :]), by_batch(bank(("router", g))[0:E, :]),
                                  rbias[:, g * HB:(g + 1) * HB].unsqueeze(2).to_broadcast([E, HB, P]), ALU.add)\
                    .then_inc(S["router_ready"], 1)

            def probs_(g):
                dve.wait_ge(S["probs_t_made"], g + 1)
                if g:
                    dve.wait_ge(S["router_p_ready"], g)
                o = bank(("probs", g))[:, 0:HB * E].rearrange("p (b e) -> p b e", e=E)
                link(dve.tensor_reduce(smalls[:, 0, :], o, AX_X, ALU.max))
                dve.tensor_tensor(small3[:, 0], o, smalls[:, 0, :].unsqueeze(2).to_broadcast([P, HB, E]),
                                  ALU.subtract).then_inc(S["probs_centered"], 1)

            def router_p_(g):
                dve.wait_ge(S["probs_exp"], g + 1)
                link(dve.tensor_reduce(smalls[:, 1, :], small3[:, 1], AX_X, ALU.add))
                link(dve.reciprocal(small[:, 3, :], smalls[:, 1, :]))
                dve.tensor_tensor(router_p[:, g], small3[:, 1], small[:, 3, :].unsqueeze(2).to_broadcast([P, HB, E]),
                                  ALU.mult).then_inc(S["router_p_ready"], 1)

            def gate2_(g):
                dve.wait_ge(S["gate_tanh"], g + 1)
                dve.tensor_scalar(gate[g], gate[g], 0.5, 0.5, ALU.mult, ALU.add).then_inc(S["gate_ready"], 1)

            def expert_(b):
                g, j = divmod(b, HB)
                if j == 0:
                    dve.wait_ge(S["router_p_ready"], g + 1)
                if b == 0:
                    dve.wait_ge(S["hat_ready"], max(norm_turn["stats", 2], norm_turn["stats", 3]))
                dve.wait_ge(S["expert_made"], b + 1)
                o = bank(("expert", b))
                link(dve.tensor_scalar(routed[:, b, :], o[:, 0:P], router_p[:, g, j, 0:1], None, ALU.mult))
                for e in range(1, E):
                    ins = dve.scalar_tensor_tensor(out=routed[:, b, :], in0=o[:, e * P:(e + 1) * P],
                                                   scalar=router_p[:, g, j, e:e + 1], in1=routed[:, b, :],
                                                   op0=ALU.mult, op1=ALU.add)
                    if e < E - 1:
                        link(ins)
                ins.then_inc(S["routed_ready"], 1)

            def out0_(g):
                dve.wait_ge(S["out0_made"], g + 1)
                dve.wait_ge(S["gate_ready"], g + 1)
                if g:
                    dve.wait_ge(S["delta_made"], g)
                dve.scalar_tensor_tensor(out=delta_t, in0=bank(("out0", g)), scalar=col("out_b"), in1=gate[g],
                                         op0=ALU.add, op1=ALU.mult).then_inc(S["delta_t_ready"], 1)

            def add_to_res(key, b0, nb):
                t = res[:, b0:b0 + nb, :]
                dve.tensor_tensor(t, t, by_batch(bank(key))[:, 0:nb, :], ALU.add).then_inc(S["res_ready"], 1)

            def delta_t_(g):
                dve.wait_ge(S["delta_made"], g + 1)
                add_to_res(("delta_t", g), g * HB, HB)

            def head_bias(n):
                return {"kc": col("b_kvc"), "k": col("b_qkv", 1), "q": col("b_qkv"), "qc": col("b_qc")}[HEADS[n][0]]

            def proj_(n):
                dve.wait_ge(S["high_ready"], n + 1)
                dve.scalar_tensor_tensor(out=low[:, n % 2, :], in0=bank(("proj", n)), scalar=head_bias(n),
                                         in1=high[:, n % 2, :].bitcast(F32), op0=ALU.add, op1=ALU.subtract)\
                    .then_inc(S["low_ready"], 1)

            def sel_(n, c):
                kind, g = HEADS[n]
                t = slots_k if kind[0] == "k" else slots_q
                if c % 2 == 0:
                    if kind[1:] == "c":
                        dve.wait_ge(S["scores_t_made"], NC * HB * (g + 1))
                    dve.wait_ge(S["sel_made"], n * NC + c + 1)
                    dve.tensor_copy(t[:, g * HB:(g + 1) * HB, c, :], by_batch(bank(("sel", n, c))))\
                        .then_inc(S["slots_even"], 1)

            def values_(n):
                a, g = VALUES[n]
                dve.wait_ge(S["values_made"], n + 1)
                if n:
                    dve.wait_ge(S["values_low"], n)
                o = bank(("values", n)).rearrange("p (x d) -> p x d", d=D)
                v = vals[:, a, g * HB:(g + 1) * HB].rearrange("p b h w -> p (b h) w")
                link(dve.tensor_copy(v[:, :, 0:D], o))
                dve.tensor_tensor(vrest[:, :].rearrange("p (x d) -> p x d", d=D), o, v[:, :, 0:D], ALU.subtract)\
                    .then_inc(S["values_rest"], 1)

            def scores_(i, c):
                n = i * NC + c
                dve.wait_ge(S["scores_made"], n + 1)
                if i >= 2 and c == 0:
                    dve.wait_ge(S["guard_ready"], i - 1)
                dve.tensor_reduce(guard[:, i % 2, c * HC:(c + 1) * HC], by_batch(bank(("scores", i, c))), AX_X,
                                  ALU.max, negate=True).then_inc(S["scores_read"], 1)

            def guard_(i):
                dve.wait_ge(S["scores_read"], NC * (i + 1))
                if i == 0:
                    dve.wait_ge(S["vec_const"], 1)
                if i >= 2:
                    dve.wait_ge(S["guard_t_made"], i - 1)
                link(dve.tensor_copy(guard_pair[:, i % 2, 0:NH], guard[:, i % 2, :]))
                dve.tensor_tensor(guard_pair[:, i % 2, NH:2 * NH], guard[:, i % 2, :], guard_pair[:, i % 2, 0:NH],
                                  ALU.subtract).then_inc(S["guard_ready"], 1)

            def guard_t_(i):
                dve.wait_ge(S["guard_t_made"], i + 1)
                if i >= 2:
                    dve.wait_ge(S["scores_t_made"], NC * (i - 1))
                dve.tensor_copy(guard_t[:, i % 2, :], bank(("guard_t", i)).bitcast(BF16)[:, 0:P])\
                    .then_inc(S["guard_t_ready"], 1)

            def mix_(i):
                dve.wait_ge(S["mix_made"], i + 1)
                b = i % NB
                if i >= NB and i % HB == 0:
                    dve.wait_ge(S["attn_t_made"], i // HB - 1)
                if i:
                    dve.wait_ge(S["attn_ready"], i)
                o = bank(("mix", i))[:, 0:NH * VW].rearrange("p (h w) -> p h w", w=VW)
                t = attn[:, b, :].rearrange("p (h d) -> p h d", d=D)
                link(dve.tensor_reduce(t, o[:, :, 0:3 * D].rearrange("p h (s d) -> p h d s", s=3), AX_X, ALU.add))
                ins = dve.reciprocal(rden[:], o[:, :, 3 * D])
                ins.then_inc(S["mix_read"], 1)
                dve.wait_ge(S["mix_read"], i + 1)
                dve.tensor_tensor(t, t, rden[:, :].unsqueeze(2).to_broadcast([P, NH, D]), ALU.mult)\
                    .then_inc(S["attn_ready"], 1)

            def gated(out, o, bias, which, b0, nb):
                return dve.scalar_tensor_tensor(out=out.rearrange("p (b n) -> p b n", b=nb),
                                                in0=o.rearrange("p (b n) -> p b n", b=nb), scalar=bias,
                                                in1=mod[:, which, b0:b0 + nb].unsqueeze(2).to_broadcast([P, nb, P]),
                                                op0=ALU.add, op1=ALU.mult)

            def attn_proj_(p):
                a, b0, nb = OUTS[p]
                dve.wait_ge(S["attn_proj_made"], p + 1)
                if p:
                    dve.wait_ge(S["attn_y_made"], p)
                o = bank(("attn_proj", p))[:, 0:nb * P]
                y = within(y_t, b0, nb)
                if a == 0:
                    last = gated(y, o, col("b_proj"), 2, b0, nb)
                else:
                    last = dve.tensor_scalar(y, o, col("b_cproj"), None, ALU.add)
                last.then_inc(S["y_ready"], 1)

            def attn_y_(p):
                dve.wait_ge(S["attn_y_made"], p + 1)
                add_to_res(("attn_y", p), *OUTS[p][1:])

            def mlp2_(g):
                b0, nb, _ = MLPS[g]
                dve.wait_ge(S["mlp2_made"], g + 1)
                gated(mlp_y[g], bank(("mlp2", g))[:, 0:nb * P], col("b_mlp2"), 5, b0, nb).then_inc(S["y_ready"], 1)

            def last_(g):
                dve.wait_ge(S["last_made"], g + 1)
                add_to_res(("last", g), *MLPS[g][0:2])

            mine = {"cols": cols_, "stats": stats_, "norm": norm_, "hat": hat_, "kq_w": kq_w_,
                    "anchor": anchor_, "mod": mod_, "kq": kq_, "s0": s0_, "p0": p0_, "router_p": router_p_, "ev": ev_, "router": router_, "probs": probs_,
                    "gate2": gate2_, "expert": expert_, "out0": out0_, "delta_t": delta_t_, "proj": proj_,
                    "sel": sel_, "values": values_, "scores": scores_, "guard": guard_, "guard_t": guard_t_, "mix": mix_,
                    "attn_proj": attn_proj_, "attn_y": attn_y_, "mlp2": mlp2_, "last": last_}
            for st in steps:
                if st[0] in mine:
                    mine[st[0]](*st[1:])

        @block.scalar
        def _(act):
            def bank(key):
                return banks[:, bank_of[key], :]

            act.wait_ge(S["first_in"], 16)
            act.activation(silu_c[:], cols_of("cond"), ACT.Silu).then_inc(S["silu_c_ready"], 1)
            act.wait_ge(S["pair_sel_made"], 1)
            act.copy(head_sel[:], pair_sel[:, :].unsqueeze(2).to_broadcast([P, NH, P])).then_inc(S["head_sel_ready"], 1)

            def hat_(n):
                kind, b0, nb = NORMS[n]
                if n in hat_v:
                    return
                act.wait_ge(S["hat_t_made"], norm_turn["stats", n])
                g = b0 // HB
                if kind == "x":
                    ins = act.activation(half(x_hat_t, g), bank(("hat", n)), ACT.Identity, scale=col("gamma"),
                                         bias=col("beta"))
                else:
                    ins = act.copy(half(ctx_hat_t if kind == "c" else norm_t, g), bank(("hat", n)))
                ins.then_inc(S["hat_t_ready"], 1)

            def v0_(g):
                act.wait_ge(S["v0_made"], g + 1)
                act.copy(v0[:, g * HB:(g + 1) * HB, :], by_batch(bank(("v0", g)))).then_inc(S["v0_ready"], 1)

            def s0_(g):
                act.wait_ge(S["s0_max"], g + 1)
                if g:
                    act.wait_ge(S["p0_ready"], g)
                for j in range(HB):
                    last = act.activation(p0[:, g * HB + j, :], bank(("s0", g))[:, j * P:(j + 1) * P], ACT.Exp,
                                          scale=SCALE0, bias=small[:, 0, j:j + 1], accum_out=small[:, 1, j:j + 1])
                last.then_inc(S["s0_exp"], 1)

            def p0_t_(g):
                act.wait_ge(S["p0_t_made"], g + 1)
                act.copy(p0_t[:, g * HB:(g + 1) * HB, :], by_batch(bank(("p0_t", g)))).then_inc(S["p0_t_ready"], 1)

            def silu_by_batch(out, o, m, g):
                for j in range(HB):
                    last = act.activation(out[:, j * P:(j + 1) * P], o[:, j * P:(j + 1) * P], ACT.Silu,
                                          bias=abias[:, m, g * HB + j:g * HB + j + 1])
                return last

            def gate1_(g):
                act.wait_ge(S["abias_ready"], 1)
                act.wait_ge(S["gate1_made"], g + 1)
                silu_by_batch(gate[g], bank(("gate1", g)), MH, g).then_inc(S["gate_h_ready"], 1)

            def hidden_(g, m):
                n = g * MH + m
                if n == 0:
                    act.wait_ge(S["abias_ready"], 1)
                act.wait_ge(S["hidden_made"], n + 1)
                if g and m == 0:
                    act.wait_ge(S["expert_made"], HB * g)
                silu_by_batch(hidden[:, m, :], bank(("hidden", n)), m, g).then_inc(S["hidden_ready"], 1)

            def probs_(g):
                act.wait_ge(S["probs_centered"], g + 1)
                if g:
                    act.wait_ge(S["router_p_ready"], g)
                act.activation(small3[:, 1], small3[:, 0], ACT.Exp).then_inc(S["probs_exp"], 1)

            def gate2_(g):
                if g == 0:
                    act.wait_ge(S["cols_ready"], 1)
                act.wait_ge(S["gate2_made"], g + 1)
                act.activation(gate[g], bank(("gate2", g)), ACT.Tanh, scale=0.5, bias=gate_b2_half[:, 0:1])\
                    .then_inc(S["gate_tanh"], 1)

            def routed_t_(g):
                act.wait_ge(S["routed_t_made"], g + 1)
                if g:
                    act.wait_ge(S["out0_made"], g)
                act.copy(routed_t, bank(("routed_t", g))).then_inc(S["routed_t_ready"], 1)

            def head_bias(n):
                return {"kc": col("b_kvc"), "k": col("b_qkv", 1), "q": col("b_qkv"), "qc": col("b_qc")}[HEADS[n][0]]

            def proj_(n):
                act.wait_ge(S["proj_made"], n + 1)
                if n >= 2:
                    act.wait_ge(S["sel_made"], NC * (n - 1))
                act.activation(high[:, n % 2, :], bank(("proj", n)), ACT.Identity, bias=head_bias(n))\
                    .then_inc(S["high_ready"], 1)

            def sel_(n, c):
                kind, g = HEADS[n]
                t = slots_k if kind[0] == "k" else slots_q
                if c % 2:
                    if kind[1:] == "c":
                        act.wait_ge(S["scores_t_made"], NC * HB * (g + 1))
                    act.wait_ge(S["sel_made"], n * NC + c + 1)
                    act.copy(t[:, g * HB:(g + 1) * HB, c, :], by_batch(bank(("sel", n, c))))\
                        .then_inc(S["slots_odd"], 1)

            def probs1_(i, c):
                n = i * NC + c
                if n == 0:
                    act.wait_ge(S["ev_made"], NHALF)
                act.wait_ge(S["scores_t_made"], n + 1)
                if n >= PR:
                    act.wait_ge(S["p_low"], n - PR + 1)
                act.activation(pf[:, n % PR, :], bank(("probs1", i, c)), ACT.Exp, scale=SCALE1)\
                    .then_inc(S["p_full"], 1)
                if i >= 2 and c == 0:
                    act.wait_ge(S["mix_made"], i - 1)
                act.activation(ph[:, i % 2, c, :], bank(("probs1", i, c)), ACT.Exp, scale=SCALE1)\
                    .then_inc(S["p_high"], 1)

            def attn_t_(p):
                act.wait_ge(S["attn_t_made"], p + 1)
                if p:
                    act.wait_ge(S["attn_proj_made"], p)
                a, b0, nb = OUTS[p]
                act.activation(within(attn_t, b0, nb), bank(("attn_t", p))[:, 0:nb * P], ACT.Identity,
                               bias=col("b_kvc", 1) if a else col("b_qkv", 2)).then_inc(S["attn_t_ready"], 1)

            def mlp1_(g, m):
                k = g * NM + m
                n = MLPS[g][1] * P
                act.wait_ge(S["mlp1_made"], k + 1)
                act.activation(mlp_h[g][:, m * n:(m + 1) * n], bank(("mlp1", k))[:, 0:n], ACT.Gelu_apprx_tanh,
                               bias=col("b_mlp1", m))\
                    .then_inc(S["mlp1_ready"], 1)

            mine = {"hat": hat_, "v0": v0_, "s0": s0_, "p0_t": p0_t_, "gate1": gate1_,
                    "hidden": hidden_, "probs": probs_, "gate2": gate2_, "routed_t": routed_t_, "proj": proj_,
                    "sel": sel_, "probs1": probs1_, "attn_t": attn_t_, "mlp1": mlp1_}
            for st in steps:
                if st[0] in mine:
                    mine[st[0]](*st[1:])

        @block.gpsimd
        def _(pool):
            chain = [0]

            def link(ins):
                chain[0] += 1
                ins.then_inc(S["pool"], 1)
                pool.wait_ge(S["pool"], chain[0])

            link(pool.memset(ident[:], 0.0))
            pool.affine_select(out=ident[:, :], in_=ident[:, :], compare_op=ALU.not_equal, fill=1.0, base=0,
                               pattern=[[-1, P]], channel_multiplier=1).then_inc(S["ident_made"], 1)
            pool.wait_ge(S["ident_made"], 1)
            pool.tensor_tensor(pair_sel[:], ident[:, 0:NH], ident[:, NH:2 * NH], ALU.add)\
                .then_inc(S["pair_sel_made"], 1)
            link(pool.memset(power[:], -0.5))

            def stats_(n):
                k = norm_turn["stats", n]
                pool.wait_ge(S["moments_ready"], k)
                if k > 1:
                    pool.wait_ge(S["rstd_made"], k - 1)
                kind, _, nb = NORMS[n]
                link(pool.tensor_scalar(var_eps[:, 0:nb], moments[:, n, 0:nb, 1], EPS0 if kind == "x" else EPS1, None,
                                        ALU.add))
                pool.tensor_tensor(rstd[:, n, 0:nb], var_eps[:, 0:nb], power[:, 0:nb], ALU.pow).then_inc(S["rstd_made"], 1)

            def anchor_(_):
                pool.memset(diag["k"][:].rearrange("p r j c n -> p (r j c n)").bitcast(F32), 0.0)
                pool.memset(diag["q"][:].rearrange("p r j c n -> p (r j c n)").bitcast(F32), 0.0)\
                    .then_inc(S["diag_zero"], 1)

            def split_(_):
                pool.wait_ge(S["eb2_in"], 16)
                link(pool.tensor_copy(eb2_parts[:], eb2[:]))
                link(pool.tensor_tensor(eb2[:], eb2[:], eb2_parts[:], ALU.subtract))
                link(pool.tensor_copy(eb2_parts[32:64, :], eb2[32:64, :]))
                link(pool.tensor_copy(eb2_parts[64:P, :], eb2[64:P, :]))
                link(pool.tensor_tensor(eb2[64:P, :], eb2[64:P, :], eb2_parts[64:P, :], ALU.subtract))
                link(pool.tensor_copy(eb2_parts[64:P, :], eb2[64:P, :]))
                link(pool.memset(eb2_parts[96:P, :], 0.0))
                pool.memset(share[:], 1.0 / 32).then_inc(S["eb2_split"], 1)

            def values_(n):
                a, g = VALUES[n]
                v = vals[:, a, g * HB:(g + 1) * HB].rearrange("p b h w -> p (b h) w")
                r = vrest[:, :].rearrange("p (x d) -> p x d", d=D)
                pool.wait_ge(S["values_rest"], n + 1)
                link(pool.tensor_copy(v[:, :, D:2 * D], r))
                pool.tensor_tensor(v[:, :, 2 * D:3 * D], r, v[:, :, D:2 * D], ALU.subtract)\
                    .then_inc(S["values_low"], 1)

            def probs1_(i, c):
                n = i * NC + c
                pool.wait_ge(S["p_high"], n + 1)
                pool.tensor_tensor(pl[:, i % 2, c, :], pf[:, n % PR, :], ph[:, i % 2, c, :], ALU.subtract)\
                    .then_inc(S["p_low"], 1)

            mine = {"stats": stats_, "anchor": anchor_, "split": split_, "values": values_, "probs1": probs1_}
            for st in steps:
                if st[0] in mine:
                    mine[st[0]](*st[1:])

        @block.sync
        def _(sp):
            for tile, src, name in (
                    (res[:, 0:HB, :], x[0], "x_in0"), (first_sb[:], first, "first_in"),
                    (ctx_t, ctx_turned, "ctx_turned_in"), (res[:, HB:NB, :], x[1], "x_in1"),
                    (hidden_sb[:], hidden_w, "hidden_w_in"), (ctx_tok[:], ctx, "ctx_in"),
                    (layer1_sb[:], layer1, "layer1_in"), (second_sb[:], second, "second_in"),
                    (eb2[:], e_b2.partition_broadcast(P), "eb2_in"),
                    (late_sb[:], late, "late_in")):
                sp.dma_start(tile, src).then_inc(S[name], 16)

            sp.wait_ge(S["diag_zero"], 1)
            for i in range(NI):
                a, b = divmod(i, NB)
                for k, kind, dense, used in (("k", ("k", "kc")[a], slots_k, "scores_made"),
                                             ("q", ("q", "qc")[a], slots_q, "scores_t_made")):
                    n = HEADS.index((kind, b // HB))
                    sp.wait_ge(S["slots_even"], 2 * n + 2)
                    sp.wait_ge(S["slots_odd"], 2 * n + 2)
                    if i >= NR:
                        sp.wait_ge(S[used], NC * (i - NR + 1))
                    for j in range(HC):
                        at = slice(j * 4 * D, (j + 1) * 4 * D)
                        sp.dma_start(diag[k][at, i % NR, j].bitcast(F32), dense[at, b].bitcast(F32))\
                            .then_inc(diag_in[k][i % NR], 16)

            for g, (b0, nb, _) in enumerate(MLPS):
                sp.wait_ge(S["res_ready"], res_turn["last", g])
                sp.dma_start(within(out[b0 // HB], b0, nb), res[:, b0:b0 + nb, :]).then_inc(S["out_done"], 16)
            sp.wait_ge(S["out_done"], 16 * len(MLPS))


def laid_out(inputs):
    import numpy as np

    z = {n.replace("L0_xcond_", "").replace("L1_xcond_", ""): np.asarray(a) for n, a in inputs.items()}

    def by_row_blocks(w):
        return w.reshape(-1, P, w.shape[-1]).transpose(1, 0, 2).reshape(P, -1)

    def tokens(a):
        return a.reshape(NHALF, HB, P, P).transpose(0, 2, 1, 3).reshape(NHALF, P, HN)

    z["router_b"] = np.concatenate([z["router_b"], np.zeros(P - E, z["router_b"].dtype)])
    z["gamma"], z["beta"], z["cond"] = z["ln_gamma"], z["ln_beta"], z["cond_1024"]
    parts = {
        "cols": np.concatenate([z[n].reshape(-1, P) for n in COL]).T,
        "WqT": z["Wq"].T, "WkT": z["Wk"].T, "Wv": z["Wv"],
        "e_w1": np.concatenate([by_row_blocks(w) for w in z["e_w1"]], axis=1),
        "e_w2": np.concatenate([by_row_blocks(w) for w in z["e_w2"]], axis=1),
        **{n: by_row_blocks(z[n]) for n in ("gate_w1", "router_W", "W_mlp2")},
        **{n: z[n] for n in ("gate_w2", "out_w", "W_mod", "W_qkv", "W_kvc", "W_qc", "W_proj", "W_cproj", "W_mlp1")},
    }
    pack = lambda names: np.concatenate([parts[n] for n, _ in names], axis=1)
    ctx = z["ctx_1024"]
    return {"x": tokens(z["x"]), "ctx": ctx.transpose(1, 0, 2).reshape(P, NB * P),
            "ctx_turned": ctx.transpose(2, 0, 1).reshape(P, NB * P), "first": pack(FIRST), "hidden_w": pack(HIDDEN),
            "second": pack(SECOND), "layer1": pack(LAYER1), "late": pack(LATE), "e_b2": z["e_b2"].reshape(-1)}


def kernel(**inputs):
    import numpy as _np
    import concourse.bacc as _bacc
    from concourse import mybir as _mybir
    from concourse.bass_utils import run_bass_kernel_spmd as _run

    nc = _bacc.Bacc("TRN2", target_bir_lowering=False, num_devices=1)
    arrays, args = {}, []
    for name, a in laid_out(inputs).items():
        a = _np.ascontiguousarray(a)
        arrays[f"in_{name}_dram"] = a
        args.append(nc.dram_tensor(f"in_{name}_dram", a.shape, _mybir.dt.from_np(a.dtype), kind="ExternalInput").ap())
    out = nc.dram_tensor("out_dram", (NHALF, P, HN), _mybir.dt.float32, kind="ExternalOutput").ap()
    pixart_block(nc, *args, out)
    got = _run(nc, [arrays], core_ids=[0]).results[0]["out_dram"]
    return _np.ascontiguousarray(got.reshape(NHALF, P, HB, P).transpose(0, 2, 1, 3).reshape(NB, P, P))
```

```python
from contextlib import ExitStack

import concourse.bass as bass
from concourse import mybir

ALU = mybir.AluOpType
ACT = mybir.ActivationFunctionType
AX_X = mybir.AxisListType.X
F32 = mybir.dt.float32
F32R = mybir.dt.float32r
BF16 = mybir.dt.bfloat16
F16 = mybir.dt.float16

P = 128
NB = 8
HB = 4
NHALF = NB // HB
HN = HB * P
E = 3
MH = 6
NH = 16
D = P // NH
NC = 4
HC = NH // NC
NM = 4
VW = 3 * D + 1
NI = 2 * NB
NR = 2
PR = 3
EPS0 = 1e-5
EPS1 = 1e-6
SCALE0 = float(P) ** -0.5
SCALE1 = float(D) ** -0.5

COL = {}
for _name, _n in (("gamma", 1), ("beta", 1), ("e_b1", MH), ("gate_b1", 1), ("gate_b2", 1), ("out_b", 1), ("b_mod", 6),
                  ("b_qkv", 3), ("b_proj", 1), ("b_qc", 1), ("b_kvc", 2), ("b_mlp1", NM),
                  ("b_mlp2", 1), ("cond", NB), ("router_b", 1)):
    COL[_name] = sum(n for _, n in COL.values()), _n
COLS = sum(n for _, n in COL.values())

NORMS = [("x", 0, HB), ("x", HB, HB), ("c", 0, HB), ("c", HB, HB), ("1", 0, HB), ("1", HB, HB), ("2", 0, HB),
         ("2", HB, HB), ("3", 0, HB), ("3", HB, 2), ("3", HB + 2, 2)]
HEADS = [("k", 0), ("q", 0), ("k", 1), ("q", 1), ("kc", 0), ("qc", 0), ("kc", 1), ("qc", 1)]
VALUES = [(1, 0), (1, 1), (0, 0), (0, 1)]
OUTS = [(0, 0, HB), (0, HB, HB), (1, 0, HB), (1, HB, 2), (1, HB + 2, 2)]
MLPS = [(0, HB, 8), (HB, 2, 9), (HB + 2, 2, 10)]


START = [
    ("kq_w",), ("kq_w_out",), ("kq", 0), ("kq", 1), ("stats", 0), ("stats", 1), ("norm", 0), ("kq_out", 0),
    ("hat", 0), ("hat", 1), ("hat_out", 0), ("hat_out", 1), ("cols",), ("begin", 0, 0), ("s0", 0), ("begin", 0, 1),
    ("begin", 0, 2), ("begin", 0, 3), ("norm", 1), ("s0_out", 0), ("s0", 1), ("anchor",), ("p0_t", 0), ("kq_out", 1),
    ("v0", 0), ("v0", 1), ("p0", 0), ("s0_out", 1), ("anchor_out",), ("ev", 0), ("p0_t", 1), ("p0_t_out", 0),
    ("router", 0), ("p0", 1), ("ev_out", 0), ("ev", 1), ("v0_out", 0), ("hidden", 0, 0), ("v0_out", 1),
    ("p0_t_out", 1), ("stats", 2), ("stats", 3), ("router_out", 0), ("ev_out", 1), ("norm", 2), ("norm", 3),
    ("gate1", 0), ("mod",), ("hidden_out", 0, 0), ("hat", 2), ("mod_out",), ("hidden", 0, 1), ("hidden", 0, 2),
    ("gate1_out", 0), ("split",), ("hat_out", 2), ("hat", 3), ("hidden", 0, 3), ("hidden", 0, 4), ("hidden", 0, 5),
    ("hidden_out", 0, 1), ("values", 0), ("gate2", 0), ("hat_out", 3), ("probs", 0), ("expert", 0), ("expert", 1),
    ("expert", 2), ("hidden_out", 0, 2), ("hidden_out", 0, 3), ("values_out", 0), ("hidden_out", 0, 4),
    ("hidden_out", 0, 5), ("expert", 3), ("probs_out", 0), ("router_p", 0), ("expert_out", 0), ("gate2_out", 0),
    ("values", 1), ("expert_out", 1), ("routed_t", 0), ("expert_out", 2), ("out0", 0), ("hidden", 1, 0),
    ("routed_t_out", 0), ("expert_out", 3), ("values_out", 1), ("delta_t", 0), ("hidden", 1, 1),
    ("hidden_out", 1, 0), ("hidden", 1, 2), ("out0_out", 0), ("gate1", 1), ("hat", 4), ("hidden", 1, 3), ("proj", 0),
    ("hidden_out", 1, 1), ("hidden_out", 1, 2), ("hat_out", 4), ("delta_t_out", 0), ("proj", 1), ("hidden", 1, 4),
    ("sel", 0, 0), ("gate1_out", 1), ("stats", 4), ("sel", 0, 1), ("sel", 0, 2), ("sel", 0, 3), ("router", 1),
    ("norm", 4), ("sel", 1, 0), ("sel", 1, 1), ("proj_out", 0), ("sel", 1, 2), ("sel_out", 0, 0), ("sel", 1, 3),
    ("gate2", 1), ("hidden", 1, 5), ("proj_out", 1), ("hidden_out", 1, 3), ("hidden_out", 1, 4), ("scores", 0, 0),
    ("sel_out", 0, 1), ("sel_out", 0, 2), ("sel_out", 0, 3), ("sel_out", 1, 0), ("router_out", 1),
    ("scores_out", 0, 0), ("sel_out", 1, 1), ("sel_out", 1, 2), ("scores", 0, 1), ("scores_out", 0, 1),
    ("sel_out", 1, 3), ("scores", 0, 2), ("scores_out", 0, 2), ("scores", 0, 3), ("scores_out", 0, 3), ("probs", 1),
    ("values", 2), ("guard", 0), ("guard_t", 0), ("gate2_out", 1), ("guard_t_out", 0)]
ITEM = [
    ("scores", 1, 0), ("scores_out", 1, 0), ("scores", 1, 1), ("scores_out", 1, 1), ("probs1", 0, 0),
    ("probs1_out", 0, 0), ("scores", 1, 2), ("scores_out", 1, 2), ("probs1", 0, 1), ("probs1_out", 0, 1),
    ("scores", 1, 3), ("scores_out", 1, 3), ("probs1", 0, 2), ("probs1_out", 0, 2), ("guard", 1), ("mix", -1),
    ("mix_out", -1), ("probs1", 0, 3), ("probs1_out", 0, 3), ("guard_t", 1), ("guard_t_out", 1)]

SIDE_WORK = {
    (0, 1): [("hidden_out", 1, 5), ("probs_out", 1)], (0, 2): [("values_out", 2)], (0, 11): [("router_p", 1)],
    (0, 12): [("expert", 4), ("expert", 5), ("expert", 6), ("expert", 7), ("expert_out", 4)],
    (0, 15): [("expert_out", 5)], (0, 18): [("expert_out", 6)], (0, 20): [("expert_out", 7)],
    (1, 6): [("routed_t", 1)], (1, 13): [("routed_t_out", 1)], (1, 21): [("out0", 1), ("out0_out", 1)],
    (2, 2): [("delta_t", 1), ("delta_t_out", 1), ("stats", 5)], (2, 7): [("norm", 5)], (2, 13): [("hat", 5)],
    (2, 14): [("hat_out", 5)], (2, 18): [("proj", 2), ("proj", 3), ("sel", 2, 0), ("sel", 2, 1)],
    (2, 19): [("sel", 2, 2), ("proj_out", 2), ("sel", 2, 3), ("sel", 3, 0), ("sel", 3, 1), ("proj_out", 3),
        ("sel_out", 2, 0), ("sel_out", 2, 1), ("sel", 3, 2), ("values", 3), ("sel_out", 2, 2), ("sel", 3, 3),
        ("sel_out", 2, 3), ("sel_out", 3, 0), ("values_out", 3)],
    (2, 20): [("sel_out", 3, 1), ("sel_out", 3, 2), ("sel_out", 3, 3)], (5, 1): [("attn_t", 0)],
    (5, 2): [("attn_t_out", 0)], (5, 8): [("attn_proj", 0)], (5, 11): [("attn_proj_out", 0)],
    (5, 12): [("attn_y", 0), ("proj", 4), ("attn_y_out", 0), ("stats", 6)], (5, 13): [("proj_out", 4)],
    (5, 21): [("sel", 4, 0), ("sel", 4, 1), ("sel_out", 4, 0), ("sel_out", 4, 1), ("norm", 6), ("sel", 4, 2),
        ("sel", 4, 3), ("hat", 6), ("sel_out", 4, 2)],
    (6, 3): [("sel_out", 4, 3), ("hat_out", 6)], (6, 5): [("proj", 5)], (6, 7): [("proj_out", 5)],
    (6, 15): [("sel", 5, 0), ("sel_out", 5, 0), ("sel", 5, 1)], (6, 16): [("sel", 5, 2)],
    (6, 17): [("sel_out", 5, 1), ("sel_out", 5, 2), ("sel", 5, 3), ("sel_out", 5, 3)], (8, 20): [("proj", 6)],
    (8, 21): [("attn_t", 1)], (9, 4): [("attn_t_out", 1)], (9, 5): [("proj_out", 6)], (9, 6): [("attn_proj", 1)],
    (9, 7): [("attn_proj_out", 1)], (9, 11): [("attn_y", 1)], (9, 13): [("attn_y_out", 1), ("stats", 7)],
    (9, 16): [("sel", 6, 0), ("sel", 6, 1), ("sel_out", 6, 0)],
    (9, 18): [("sel", 6, 2), ("sel_out", 6, 1), ("norm", 7), ("sel", 6, 3)],
    (9, 20): [("sel_out", 6, 2), ("sel_out", 6, 3)], (10, 4): [("hat", 7)], (10, 5): [("hat_out", 7)],
    (10, 8): [("proj", 7), ("proj_out", 7)],
    (10, 14): [("sel", 7, 0), ("sel", 7, 1), ("sel_out", 7, 0), ("sel_out", 7, 1)],
    (10, 16): [("sel", 7, 2), ("sel", 7, 3)], (10, 18): [("sel_out", 7, 2), ("sel_out", 7, 3)],
    (13, 3): [("attn_t", 2)], (13, 4): [("attn_t_out", 2)], (13, 12): [("attn_proj", 2)],
    (13, 14): [("attn_proj_out", 2)], (13, 21): [("stats", 8)], (14, 20): [("attn_t", 3)],
    (14, 21): [("attn_t_out", 3)], (15, 9): [("attn_proj", 3), ("hat", 8)], (15, 10): [("norm", 8)],
    (15, 13): [("hat_out", 8)],
    (15, 19): [("mlp1", 0, 0), ("mlp1", 0, 1), ("mlp1", 0, 2), ("attn_proj_out", 3), ("stats", 9)]}
END = [
    ("norm", 9), ("mlp1", 0, 3), ("attn_t", 4), ("mlp2", 0, 0), ("attn_proj", 4), ("mlp1_out", 0, 0),
    ("mlp1_out", 0, 1), ("hat", 9), ("mlp2", 0, 1), ("attn_proj_out", 4), ("mlp2", 0, 2), ("stats", 10),
    ("mlp2", 0, 3), ("norm", 10), ("mlp1", 1, 0), ("hat", 10), ("mlp1", 1, 1), ("mlp1", 1, 2), ("mlp1", 1, 3),
    ("mlp2_out", 0), ("mlp1", 2, 0), ("attn_t_out", 4), ("mlp1", 2, 1), ("mlp2", 1, 0), ("mlp2", 1, 1),
    ("mlp1_out", 0, 2), ("last", 0), ("mlp2", 1, 2), ("mlp2", 1, 3), ("mlp1", 2, 2), ("mlp1_out", 0, 3),
    ("hat_out", 9), ("hat_out", 10), ("mlp1_out", 1, 0), ("last_out", 0), ("mlp2_out", 1), ("mlp1_out", 1, 1),
    ("mlp2", 2, 0), ("mlp1", 2, 3), ("mlp2", 2, 1), ("mlp2", 2, 2), ("mlp2", 2, 3), ("mlp2_out", 2),
    ("mlp1_out", 1, 2), ("mlp1_out", 1, 3), ("last", 1), ("last", 2), ("mlp1_out", 2, 0), ("last_out", 1),
    ("mlp1_out", 2, 1), ("mlp1_out", 2, 2), ("last_out", 2), ("mlp1_out", 2, 3)]


def schedule():
    o = list(START)
    for i in range(NI):
        o += SIDE_WORK.get((i, 0), [])
        for k, (kind, ahead, *c) in enumerate(ITEM):
            if 0 <= i + ahead < NI:
                o.append((kind, i + ahead, *c))
            o += SIDE_WORK.get((i, k + 1), [])
    o += [("mix", NI - 1), ("mix_out", NI - 1)] + END
    return [st if len(st) > 1 else st + (0,) for st in o]


FIRST = [("cols", COLS), ("WqT", P), ("WkT", P), ("Wv", P)]
HIDDEN = [("gate_w1", 3 * P), ("router_W", 3 * E), ("e_w1", E * 3 * 2 * P)]
SECOND = [("gate_w2", P), ("out_w", P), ("e_w2", E * 2 * P)]
LAYER1 = [("W_mod", 6 * P), ("W_qkv", 3 * P), ("W_kvc", 2 * P), ("W_qc", P)]
LATE = [("W_proj", P), ("W_cproj", P), ("W_mlp1", NM * P), ("W_mlp2", NM * P)]


def width(parts):
    return sum(n for _, n in parts)


def pixart_block(nc, x, ctx, ctx_turned, first, hidden_w, second, layer1, late, bias_rows, out):
    steps = schedule()

    with ExitStack() as stack:
        def sb(name, shape, dt=F32):
            return stack.enter_context(nc.sbuf_tensor(name, shape, dt))

        def sem(name):
            return stack.enter_context(nc.semaphore(name))

        res = sb("res", [P, NB, P])
        ctx_tok = sb("ctx_tok", [P, NB, P])
        first_sb = sb("first_sb", [P, width(FIRST)])
        hidden_sb = sb("hidden_sb", [P, width(HIDDEN)])
        second_sb = sb("second_sb", [P, width(SECOND)])
        layer1_sb = sb("layer1_sb", [P, width(LAYER1)])
        late_sb = sb("late_sb", [P, width(LATE)])
        rows = sb("rows", [P, (E + 1) * P])

        def cut(tile, parts, name):
            names = [n for n, _ in parts]
            at = width(parts[:names.index(name)])
            return tile[:, at:at + parts[names.index(name)][1]]

        cols = cut(first_sb, FIRST, "cols")
        wq_t = cut(first_sb, FIRST, "WqT")
        wk_t = cut(first_sb, FIRST, "WkT")
        wv = cut(first_sb, FIRST, "Wv")
        gw1 = cut(hidden_sb, HIDDEN, "gate_w1").rearrange("p (k h) -> p k h", k=3)
        rw = cut(hidden_sb, HIDDEN, "router_W").rearrange("p (k e) -> p k e", k=3)
        ew1 = cut(hidden_sb, HIDDEN, "e_w1").rearrange("p (e k r) -> p e k r", e=E, k=3)
        gw2 = cut(second_sb, SECOND, "gate_w2")
        ow = cut(second_sb, SECOND, "out_w")
        ew2 = cut(second_sb, SECOND, "e_w2").rearrange("p (e r h) -> p e r h", e=E, r=2)
        wmod = cut(layer1_sb, LAYER1, "W_mod").rearrange("p (m n) -> p m n", m=6)
        wqkv1 = cut(layer1_sb, LAYER1, "W_qkv").rearrange("p (m n) -> p m n", m=3)
        wkvc = cut(layer1_sb, LAYER1, "W_kvc").rearrange("p (m n) -> p m n", m=2)
        wqc = cut(layer1_sb, LAYER1, "W_qc")
        wproj = [cut(late_sb, LATE, "W_proj"), cut(late_sb, LATE, "W_cproj")]
        wm1 = cut(late_sb, LATE, "W_mlp1").rearrange("p (m n) -> p m n", m=NM)
        wm2 = cut(late_sb, LATE, "W_mlp2").rearrange("p (m n) -> p m n", m=NM)

        ident = sb("ident", [P, P])
        ident_h = sb("ident_h", [P, P], BF16)
        slot_sel = sb("slot_sel", [P, 4, NC, HC, 4, D], F32R)
        pair_sel = sb("pair_sel", [P, NH])
        head_sel = sb("head_sel", [P, NH, P], BF16)
        power = sb("power", [P, HB])
        share = sb("share", [P, P], BF16)
        row_parts = sb("row_parts", [P, (E + 1) * P], BF16)

        gate_b2_half = sb("gate_b2_half", [P, 1])
        silu_c = sb("silu_c", [P, NB])
        kq_w = sb("kq_w", [P, P])
        abias = sb("abias", [P, MH + 1, NB])
        rbias = sb("rbias", [E, NB])
        mod = sb("mod", [P, 6, NB])
        mod1 = sb("mod1", [P, 2, NB])
        bn = sb("bn", [P, HB, 6])
        moments = sb("moments", [P, len(NORMS), HB, 2])
        rstd = sb("rstd", [P, len(NORMS), HB])
        var_eps = sb("var_eps", [P, HB])
        small = sb("small", [P, 4, HB])
        small3 = sb("small3", [P, 4, HB, E])
        smallm = sb("smallm", [P, HB])
        smalls = sb("smalls", [P, 2, HB])
        router_p = sb("router_p", [P, NHALF, HB, E])
        guard = sb("guard", [P, 2, NH])
        guard_pair = sb("guard_pair", [P, 2, P], BF16)
        guard_t = sb("guard_t", [P, 2, P], BF16)
        rden = sb("rden", [P, NH])

        ctx_hat_t = sb("ctx_hat_t", [P, NB * P])
        norm_t = sb("norm_t", [P, NB * P])
        hat = sb("hat", [P, 2, HB, P])
        high = sb("high", [P, 2, HN], F32R)
        low = sb("low", [P, 2, HN], F32R)
        diag = sb("diag", [P, NR, 2, HC, NC, P], F32R)
        vals = sb("vals", [P, 2, NB, NH, VW], BF16)
        vrest = sb("vrest", [P, HN])
        slots = sb("slots", [P, NB, 2, NC, P], F32R)
        slots_k, slots_q = slots[:, :, 0], slots[:, :, 1]

        arena0 = sb("arena0", [P, 6144])
        ev_t = arena0[:, 0:1024]
        hidden = arena0[:, 1024:4096].rearrange("p (m n) -> p m n", m=MH)
        gate = [arena0[:, 4096:4608], arena0[:, 4608:5120]]
        logit_t = arena0[:, 5120:5632]
        routed_t = arena0[:, 5120:5632]
        delta_t = arena0[:, 5632:6144]
        mlp_h = [arena0[:, 1024:3072], arena0[:, 3072:4096], arena0[:, 4096:5120]]
        mlp_y = [arena0[:, 5120:5632], arena0[:, 5632:5888], arena0[:, 5888:6144]]
        routed = ctx_tok
        x_hat_t = norm_t

        arena1 = sb("arena1", [P, 7680])

        def part(at, n):
            return arena1[:, at:at + n]

        ctx_t, kq_t = part(0, 1024), part(1024, 1024)
        v0 = part(2048, 1024).rearrange("p (b n) -> p b n", b=NB)
        p0 = part(3072, 1024).rearrange("p (b n) -> p b n", b=NB)
        p0_t = part(4096, 1024).rearrange("p (b n) -> p b n", b=NB)

        pf = part(0, PR * HN).rearrange("p (r n) -> p r n", r=PR)
        ph = part(1536, 2048).bitcast(F16).rearrange("p (r c n) -> p r c n", r=2, c=NC)
        pl = part(3584, 2048).bitcast(F16).rearrange("p (r c n) -> p r c n", r=2, c=NC)
        attn = part(5632, 1024).rearrange("p (b n) -> p b n", b=NB)
        attn_t = part(6656, 512)
        y_t = part(7168, 512)

        banks = stack.enter_context(nc.psum_tensor("banks", [P, 8, HN], F32))

        S = {n: sem(n) for n in (
            "x_in0", "x_in1", "ctx_in", "ctx_turned_in", "first_in", "hidden_w_in", "second_in", "layer1_in",
            "late_in", "rows_in", "out_done",
            "pool", "ident_made", "pair_sel_made", "diag_zero", "rstd_made", "rows_split", "values_low", "p_low",
            "hat_t_made", "kq_w_made", "anchor_made", "mod_made", "kq_made",
            "v0_made", "s0_made", "p0_t_made", "ev_made", "gate1_made", "hidden_made", "router_made", "probs_t_made",
            "gate2_made", "expert_made", "routed_t_made", "out0_made", "delta_made", "proj_made", "sel_made",
            "values_made", "guard_t_made", "scores_made", "scores_t_made", "mix_made", "attn_t_made",
            "attn_proj_made", "attn_y_made", "mlp1_made", "mlp2_made", "last_made",
            "vec", "vec_const", "cols_ready", "kq_w_ready", "abias_ready", "mod_ready", "moments_ready", "hat_ready",
            "kq_ready", "s0_max", "p0_ready", "ev_ready", "router_ready",
            "probs_centered", "router_p_ready", "gate_ready", "routed_ready", "delta_t_ready", "res_ready",
            "low_ready", "slots_first", "values_rest", "guard_ready", "guard_t_ready", "scores_read", "mix_read",
            "attn_ready", "y_ready",
            "head_sel_ready", "silu_c_ready", "hat_t_ready", "v0_ready", "s0_exp", "p0_t_ready", "gate_h_ready",
            "hidden_ready", "probs_exp", "gate_tanh", "routed_t_ready", "high_ready", "slots_rest",
            "p_high", "attn_t_ready", "mlp1_ready")}
        diag_in = [sem(f"diag_in{r}") for r in range(NR)]
        diag_k_in = sem("diag_k_in")

        def col(name, j=0):
            a = COL[name][0] + j
            return cols[:, a:a + 1]

        def cols_of(name):
            a, n = COL[name]
            return cols[:, a:a + n]

        def half(t, g):
            return t[:, g * HN:(g + 1) * HN]

        def tok(t, b):
            return t[:, b * P:(b + 1) * P]

        def within(t, b0, nb):
            return t[:, (b0 % HB) * P:(b0 % HB + nb) * P]

        def by_batch(ap):
            return ap.rearrange("p (b n) -> p b n", b=HB)

        def turns(*kinds):
            chosen = [st for st in steps if st[0] in kinds]
            return {st: k + 1 for k, st in enumerate(chosen)}

        norm_turn = turns("stats")
        gated_out = [st for st in steps if st[0] == "mlp2_out" or st[0] == "attn_proj_out" and OUTS[st[1]][0] == 0]
        added = [st for st in steps if st[0] in ("delta_t_out", "attn_y_out", "attn_proj_out", "last_out")
                 and st not in gated_out]
        y_turn = {st: k + 1 for k, st in enumerate(gated_out)}
        res_turn = {st: k + 1 for k, st in enumerate(added)}
        bank_of = {}
        block = stack.enter_context(nc.Block())

        @block.tensor
        def _(pe):
            released = {}
            turn = [0]
            held = set()

            def claim(key, reader, count, among):
                bank = among[turn[0] % len(among)]
                turn[0] += 1
                while bank in held:
                    bank = among[turn[0] % len(among)]
                    turn[0] += 1
                bank_of[key] = bank
                if bank in released:
                    pe.wait_ge(S[released[bank][0]], released[bank][1])
                released[bank] = (reader, count)
                return banks[:, bank, :]

            ALL = list(range(8))
            side = []

            def free():
                return side or ALL

            def transposes(o, src, b0, nb=HB):
                for j in range(nb):
                    last = pe.transpose(o[:, j * P:(j + 1) * P], src[:, b0 + j, :], ident[:, :])
                return last

            def hat_(n):
                k = norm_turn["stats", n]
                pe.wait_ge(S["hat_ready"], k)
                o = claim(("hat", n), "hat_t_ready", k, free())
                transposes(o, hat[:, k % 2], 0, NORMS[n][2]).then_inc(S["hat_t_made"], 1)

            def kq_w_(_):
                pe.wait_ge(S["first_in"], 16)
                o = claim("kq_w", "kq_w_ready", 1, ALL)
                pe.matmul(o[:, 0:P], wk_t, wq_t, start=True, stop=True).then_inc(S["kq_w_made"], 1)

            def anchor_(_):
                pe.wait_ge(S["hidden_w_in"], 16)
                o = claim("anchor", "abias_ready", 1, ALL)
                c = cols_of("cond")
                for m in range(MH):
                    pe.matmul(o[:, m * NB:(m + 1) * NB], ew1[:, m // 2, 2, (m % 2) * P:(m % 2 + 1) * P], c,
                              start=True, stop=True)
                pe.matmul(o[:, MH * NB:(MH + 1) * NB], gw1[:, 2, :], c, start=True, stop=True)
                pe.matmul(o[0:E, (MH + 1) * NB:(MH + 2) * NB], rw[:, 2, :], c, start=True, stop=True)\
                    .then_inc(S["anchor_made"], 1)

            def mod_(_):
                pe.wait_ge(S["silu_c_ready"], 1)
                pe.wait_ge(S["layer1_in"], 16)
                o = claim("mod", "mod_ready", 1, ALL)
                for j in range(6):
                    last = pe.matmul(o[:, j * NB:(j + 1) * NB], wmod[:, j, :], silu_c[:, :], start=True, stop=True)
                last.then_inc(S["mod_made"], 1)

            def kq_(g):
                if g == 0:
                    pe.wait_ge(S["kq_w_ready"], 1)
                    pe.wait_ge(S["ctx_turned_in"], 16)
                o = claim(("kq", g), "kq_ready", g + 1, ALL)
                pe.matmul(o, kq_w[:, :], half(ctx_t, g), start=True, stop=True).then_inc(S["kq_made"], 1)

            def v0_(g):
                if g == 0:
                    pe.wait_ge(S["first_in"], 16)
                    pe.wait_ge(S["ctx_turned_in"], 16)
                o = claim(("v0", g), "v0_ready", g + 1, ALL)
                for j in range(HB):
                    last = pe.matmul(o[:, j * P:(j + 1) * P], tok(ctx_t, g * HB + j), wv,
                                     start=True, stop=True)
                last.then_inc(S["v0_made"], 1)

            def s0_(g):
                pe.wait_ge(S["kq_ready"], g + 1)
                pe.wait_ge(S["hat_t_ready"], norm_turn["stats", g])
                o = claim(("s0", g), "s0_exp", g + 1, ALL)
                for j in range(HB):
                    b = g * HB + j
                    last = pe.matmul(o[:, j * P:(j + 1) * P], tok(x_hat_t, b), tok(kq_t, b), start=True, stop=True)
                last.then_inc(S["s0_made"], 1)

            def p0_t_(g):
                pe.wait_ge(S["p0_ready"], g + 1)
                o = claim(("p0_t", g), "p0_t_ready", g + 1, ALL)
                transposes(o, p0, g * HB).then_inc(S["p0_t_made"], 1)

            def ev_(g):
                pe.wait_ge(S["v0_ready"], g + 1)
                pe.wait_ge(S["p0_t_ready"], g + 1)
                o = claim(("ev", g), "ev_ready", g + 1, ALL)
                for j in range(HB):
                    b = g * HB + j
                    last = pe.matmul(o[:, j * P:(j + 1) * P], v0[:, b, :], p0_t[:, b, :], start=True, stop=True)
                last.then_inc(S["ev_made"], 1)

            def pair(o, lhs, g):
                pe.matmul(o, lhs(0), half(x_hat_t, g), start=True, stop=False)
                return pe.matmul(o, lhs(1), half(ev_t, g), start=False, stop=True)

            def combined_ready(g):
                pe.wait_ge(S["ev_ready"], g + 1)
                if g == 0:
                    pe.wait_ge(S["hidden_w_in"], 16)

            def gate1_(g):
                combined_ready(g)
                o = claim(("gate1", g), "gate_h_ready", g + 1, ALL)
                pair(o, lambda k: gw1[:, k, :], g).then_inc(S["gate1_made"], 1)

            def begin_(g, m):
                n = g * MH + m
                pe.wait_ge(S["hat_t_ready"], norm_turn["stats", g])
                pe.wait_ge(S["hidden_w_in"], 16)
                o = claim(("hidden", n), "hidden_ready", n + 1, ALL)
                held.add(bank_of["hidden", n])
                pe.matmul(o, ew1[:, m // 2, 0, (m % 2) * P:(m % 2 + 1) * P], half(x_hat_t, g), start=True, stop=False)

            def hidden_(g, m):
                n = g * MH + m
                if m == 0:
                    combined_ready(g)
                w = lambda k: ew1[:, m // 2, k, (m % 2) * P:(m % 2 + 1) * P]
                if ("hidden", n) in bank_of:
                    o = banks[:, bank_of["hidden", n], :]
                    held.remove(bank_of["hidden", n])
                    last = pe.matmul(o, w(1), half(ev_t, g), start=False, stop=True)
                else:
                    o = claim(("hidden", n), "hidden_ready", n + 1, ALL)
                    last = pair(o, w, g)
                last.then_inc(S["hidden_made"], 1)

            def router_(g):
                combined_ready(g)
                o = claim(("router", g), "router_ready", g + 1, ALL)
                pair(o[0:E, :], lambda k: rw[:, k, :], g).then_inc(S["router_made"], 1)

            def probs_(g):
                pe.wait_ge(S["router_ready"], g + 1)
                o = claim(("probs", g), "probs_centered", g + 1, ALL)
                for j in range(HB):
                    last = pe.transpose(o[:, j * E:(j + 1) * E], logit_t[0:E, j * P:(j + 1) * P], ident[0:E, 0:E])
                last.then_inc(S["probs_t_made"], 1)

            def gate2_(g):
                pe.wait_ge(S["gate_h_ready"], g + 1)
                pe.wait_ge(S["second_in"], 16)
                o = claim(("gate2", g), "gate_tanh", g + 1, ALL)
                pe.matmul(o, gw2, gate[g], start=True, stop=True).then_inc(S["gate2_made"], 1)

            def expert_(b):
                if b % HB == 0:
                    pe.wait_ge(S["hidden_ready"], MH * (b // HB + 1))
                    pe.wait_ge(S["second_in"], 16)
                if b == 0:
                    pe.wait_ge(S["rows_split"], 1)
                o = claim(("expert", b), "routed_ready", b + 1, ALL)
                pe.matmul(o[:, 0:E * P], share[:, :], row_parts[:, 0:E * P], start=True, stop=False)
                for e in range(E):
                    for r in range(2):
                        last = pe.matmul(o[:, e * P:(e + 1) * P], tok(hidden[:, 2 * e + r, :], b % HB),
                                         ew2[:, e, r, :], start=False, stop=(e == E - 1 and r == 1))
                last.then_inc(S["expert_made"], 1)

            def routed_t_(g):
                pe.wait_ge(S["routed_ready"], HB * (g + 1))
                o = claim(("routed_t", g), "routed_t_ready", g + 1, ALL)
                transposes(o, routed, g * HB).then_inc(S["routed_t_made"], 1)

            def out0_(g):
                pe.wait_ge(S["routed_t_ready"], g + 1)
                o = claim(("out0", g), "delta_t_ready", g + 1, ALL)
                pe.matmul(o, ow, routed_t, start=True, stop=True).then_inc(S["out0_made"], 1)

            def delta_t_(g):
                pe.wait_ge(S["delta_t_ready"], g + 1)
                o = claim(("delta_t", g), "res_ready", res_turn["delta_t_out", g], ALL)
                transposes(o, by_batch(delta_t), 0).then_inc(S["delta_made"], 1)

            def normed(kind, g):
                pe.wait_ge(S["hat_t_ready"], norm_turn["stats", NORMS.index((kind, g * HB, HB))])

            def proj_(n):
                kind, g = HEADS[n]
                if n == 0:
                    pe.wait_ge(S["layer1_in"], 16)
                src, w = {"kc": (ctx_hat_t, wkvc[:, 0, :]), "k": (norm_t, wqkv1[:, 1, :]),
                          "q": (norm_t, wqkv1[:, 0, :]), "qc": (norm_t, wqc)}[kind]
                if kind == "kc":
                    normed("c", g)
                elif kind == "qc":
                    normed("2", g)
                else:
                    normed("1", g)
                o = claim(("proj", n), "low_ready", n + 1, free())
                pe.matmul(o, w, half(src, g), start=True, stop=True).then_inc(S["proj_made"], 1)

            def sel_(n, c):
                k = 2 if HEADS[n][0][0] == "k" else 0
                pe.wait_ge(S["vec_const"], 1)
                pe.wait_ge(S["low_ready"], n + 1)
                reader = ("slots_rest", 3 * n + c) if c else ("slots_first", n + 1)
                o = claim(("sel", n, c), *reader, free())
                pe.matmul(o, slot_sel[:, k, c].rearrange("p j s d -> p (j s d)"), high[:, n % 2, :],
                          start=True, stop=False)
                pe.matmul(o, slot_sel[:, k + 1, c].rearrange("p j s d -> p (j s d)"), low[:, n % 2, :],
                          start=False, stop=True).then_inc(S["sel_made"], 1)

            def values_(n):
                a, g = VALUES[n]
                if a:
                    normed("c", g)
                else:
                    normed("1", g)
                src, w = ((norm_t, wqkv1[:, 2, :]), (ctx_hat_t, wkvc[:, 1, :]))[a]
                if n == 0:
                    pe.wait_ge(S["layer1_in"], 16)
                o = claim(("values", n), "values_rest", n + 1, free())
                for j in range(HB):
                    last = pe.matmul(o[:, j * P:(j + 1) * P], tok(src, g * HB + j), w, start=True, stop=True)
                last.then_inc(S["values_made"], 1)

            def scores_(i, c):
                if (i, c) == (0, 0):
                    side.extend([6, 7])
                b = i % NB
                if c == 0:
                    if i % HB == 0:
                        pe.wait_ge(diag_k_in, 16 * HC * (i // HB + 1))
                    else:
                        pe.wait_ge(diag_in[(i - 1) % NR], 16 * HC * ((i - 1) // NR + 1))
                    if i % HB == 0:
                        n = HEADS.index((("q", "qc")[i // NB], b // HB))
                        pe.wait_ge(S["slots_first"], n + 1)
                        pe.wait_ge(S["slots_rest"], 3 * n + 3)
                bank = [0, 1, 2][(i * NC + c) % 3]
                o = claim(("scores", i, c), "scores_read", i * NC + c + 1, [bank])
                pe.matmul(o, slots_q[:, b, c, :], diag[:, (i - 1) % NR, 1, :, c, :],
                          start=True, stop=True).then_inc(S["scores_made"], 1)
                if (i, c) == (NI - 1, NC - 1):
                    side.extend([0, 1, 2])

            def guard_t_(i):
                pe.wait_ge(S["guard_ready"], i + 1)
                o = claim(("guard_t", i), "guard_t_ready", i + 1, free())
                pe.transpose(o.bitcast(BF16)[:, 0:P], guard_pair[:, i % 2, :], ident_h[:, :])\
                    .then_inc(S["guard_t_made"], 1)

            def probs1_(i, c):
                b = i % NB
                if c == 0:
                    pe.wait_ge(diag_in[i % NR], 16 * HC * (i // NR + 1))
                    pe.wait_ge(S["guard_t_ready"], i + 1)
                    if i == 0:
                        pe.wait_ge(S["head_sel_ready"], 1)
                bank = [3, 4][(i * NC + c) % 2]
                o = claim(("probs1", i, c), "p_high", i * NC + c + 1, [bank])
                pe.matmul(o, slots_k[:, b, c, :], diag[:, i % NR, 0, :, c, :],
                          start=True, stop=False)
                for j in range(HC):
                    last = pe.matmul(o[:, j * P:(j + 1) * P], head_sel[:, c * HC + j, :], guard_t[:, i % 2, :],
                                     start=False, stop=(j == HC - 1))
                last.then_inc(S["scores_t_made"], 1)
                if (i, c) == (NI - 1, NC - 1):
                    side.extend([3, 4])

            def mix_(i):
                a, b = divmod(i, NB)
                if b % HB == 0:
                    pe.wait_ge(S["values_low"], VALUES.index((a, b // HB)) + 1)
                pe.wait_ge(S["p_high"], NC * (i + 1))
                pe.wait_ge(S["p_low"], NC * (i + 1))
                o = claim(("mix", i), "mix_read", i + 1, [5])
                for h in range(NH):
                    c, j = divmod(h, HC)
                    at = o[:, h * VW:(h + 1) * VW]
                    pe.matmul(at, ph[:, i % 2, c, j * P:(j + 1) * P], vals[:, a, b, h, :], start=True, stop=False)
                    last = pe.matmul(at, pl[:, i % 2, c, j * P:(j + 1) * P], vals[:, a, b, h, :],
                                     start=False, stop=True)
                last.then_inc(S["mix_made"], 1)
                if i == NI - 1:
                    side.append(5)

            def attn_t_(p):
                a, b0, nb = OUTS[p]
                pe.wait_ge(S["attn_ready"], a * NB + b0 + nb)
                o = claim(("attn_t", p), "attn_t_ready", p + 1, free())
                transposes(o, attn, b0, nb).then_inc(S["attn_t_made"], 1)

            def attn_proj_(p):
                a, b0, nb = OUTS[p]
                pe.wait_ge(S["late_in"], 16)
                pe.wait_ge(S["attn_t_ready"], p + 1)
                if a == 0:
                    o = claim(("attn_proj", p), "y_ready", y_turn["attn_proj_out", p], free())
                    pe.matmul(o[:, 0:nb * P], wproj[a], within(attn_t, b0, nb), start=True, stop=True)\
                        .then_inc(S["attn_proj_made"], 1)
                    return
                o = claim(("attn_proj", p), "res_ready", res_turn["attn_proj_out", p], free())
                pe.matmul(by_batch(o)[:, 0:nb, :], share[:, :],
                          row_parts[:, E * P:].unsqueeze(1).to_broadcast([P, nb, P]), start=True, stop=False)
                for j in range(nb):
                    last = pe.matmul(tok(o, j), tok(attn_t, b0 % HB + j), wproj[a], start=False, stop=(j == nb - 1))
                last.then_inc(S["attn_proj_made"], 1)

            def attn_y_(p):
                a, b0, nb = OUTS[p]
                pe.wait_ge(S["y_ready"], y_turn["attn_proj_out", p])
                o = claim(("attn_y", p), "res_ready", res_turn["attn_y_out", p], free())
                transposes(o, by_batch(y_t), b0 % HB, nb).then_inc(S["attn_y_made"], 1)

            def mlp1_(g, m):
                b0, nb, n = MLPS[g]
                if m == 0:
                    pe.wait_ge(S["hat_t_ready"], norm_turn["stats", n])
                k = g * NM + m
                o = claim(("mlp1", k), "mlp1_ready", k + 1, free())
                pe.matmul(o[:, 0:nb * P], wm1[:, m, :], norm_t[:, b0 * P:(b0 + nb) * P], start=True, stop=True)\
                    .then_inc(S["mlp1_made"], 1)

            def mlp2_(g, m):
                nb = MLPS[g][1]
                if m == 0:
                    claim(("mlp2", g), "y_ready", y_turn["mlp2_out", g], free())
                    held.add(bank_of["mlp2", g])
                pe.wait_ge(S["mlp1_ready"], g * NM + m + 1)
                last = pe.matmul(banks[:, bank_of["mlp2", g], 0:nb * P], wm2[:, m, :],
                                 mlp_h[g][:, m * nb * P:(m + 1) * nb * P], start=(m == 0), stop=(m == NM - 1))
                if m == NM - 1:
                    last.then_inc(S["mlp2_made"], 1)
                    held.remove(bank_of["mlp2", g])

            def last_(g):
                nb = MLPS[g][1]
                pe.wait_ge(S["y_ready"], y_turn["mlp2_out", g])
                o = claim(("last", g), "res_ready", res_turn["last_out", g], free())
                transposes(o, mlp_y[g].rearrange("p (b n) -> p b n", b=nb), 0, nb).then_inc(S["last_made"], 1)

            mine = {"hat": hat_, "kq_w": kq_w_, "anchor": anchor_, "mod": mod_, "kq": kq_, "v0": v0_, "s0": s0_,
                    "p0_t": p0_t_, "ev": ev_, "gate1": gate1_, "begin": begin_,
                    "hidden": hidden_, "router": router_, "probs": probs_, "gate2": gate2_, "expert": expert_,
                    "routed_t": routed_t_, "out0": out0_, "delta_t": delta_t_, "proj": proj_, "sel": sel_,
                    "values": values_, "scores": scores_, "guard_t": guard_t_, "probs1": probs1_, "mix": mix_,
                    "attn_t": attn_t_, "attn_proj": attn_proj_, "attn_y": attn_y_, "mlp1": mlp1_, "mlp2": mlp2_,
                    "last": last_}
            for st in steps:
                if st[0] in mine:
                    mine[st[0]](*st[1:])

        @block.vector
        def _(dve):
            chain = [0]

            def link(ins):
                chain[0] += 1
                ins.then_inc(S["vec"], 1)
                dve.wait_ge(S["vec"], chain[0])

            def bank(key):
                return banks[:, bank_of[key], :]

            link(dve.memset(slot_sel[:].rearrange("p a c j s d -> p (a c j s d)").bitcast(F32), 0.0))
            dve.memset(guard_pair[:], 0.0)
            dve.memset(vals[:, :, :, :, 3 * D:VW].rearrange("p a b h o -> p (a b h o)"), 1.0)
            dve.wait_ge(S["ident_made"], 1)
            dve.tensor_copy(ident_h[:], ident[:])
            src = ident[:, :].rearrange("p (c j d) -> p c j d", c=NC, j=HC)
            for a, slots in enumerate(((0, 2), (1, 3), (0, 1), (2, 3))):
                for s in slots:
                    last = dve.tensor_copy(slot_sel[:, a, :, :, s, :], src)
            last.then_inc(S["vec_const"], 1)

            def cols_(_):
                dve.wait_ge(S["first_in"], 16)
                dve.tensor_scalar(gate_b2_half[:], col("gate_b2"), 0.5, None, ALU.mult).then_inc(S["cols_ready"], 1)

            def stats_(n):
                kind, b0, nb = NORMS[n]
                k = norm_turn["stats", n]
                if kind == "x":
                    dve.wait_ge(S[f"x_in{b0 // HB}"], 16)
                elif kind == "c":
                    dve.wait_ge(S["ctx_in"], 16)
                else:
                    before = {4: ("delta_t_out", 0), 5: ("delta_t_out", 1), 6: ("attn_y_out", 0), 7: ("attn_y_out", 1),
                              8: ("attn_proj_out", 2), 9: ("attn_proj_out", 3), 10: ("attn_proj_out", 4)}[n]
                    dve.wait_ge(S["res_ready"], res_turn[before])
                if k > 1:
                    dve.wait_ge(S["moments_ready"], k - 1)
                t = ctx_tok if kind == "c" else res
                for j in range(nb):
                    last = dve.bn_stats(bn[:, j, :], t[:, b0 + j, :])
                link(last)
                for j in range(nb):
                    last = dve.bn_aggr(moments[:, n, j, :], bn[:, j, :])
                last.then_inc(S["moments_ready"], 1)

            def norm_(n):
                kind, b0, nb = NORMS[n]
                k = norm_turn["stats", n]
                t = ctx_tok if kind == "c" else res
                dve.wait_ge(S["rstd_made"], k)
                if k > 2:
                    dve.wait_ge(S["hat_t_made"], k - 2)
                for j in range(nb):
                    last = dve.tensor_scalar(hat[:, k % 2, j, :], t[:, b0 + j, :], moments[:, n, j, 0:1],
                                             rstd[:, n, j:j + 1], ALU.subtract, ALU.mult)
                last.then_inc(S["hat_ready"], 1)

            def kq_w_(_):
                dve.wait_ge(S["kq_w_made"], 1)
                dve.tensor_copy(kq_w[:], bank("kq_w")[:, 0:P]).then_inc(S["kq_w_ready"], 1)

            def anchor_(_):
                dve.wait_ge(S["anchor_made"], 1)
                o = bank("anchor")
                a = COL["e_b1"][0]
                dve.tensor_scalar(rbias[:], o[0:E, (MH + 1) * NB:(MH + 2) * NB], col("router_b")[0:E], None, ALU.add)
                dve.tensor_tensor(abias[:], o[:, 0:(MH + 1) * NB].rearrange("p (m b) -> p m b", b=NB),
                                  cols[:, a:a + MH + 1].unsqueeze(2).to_broadcast([P, MH + 1, NB]), ALU.add)\
                    .then_inc(S["abias_ready"], 1)

            def mod_(_):
                dve.wait_ge(S["mod_made"], 1)
                link(dve.tensor_tensor(mod[:], bank("mod")[:, 0:6 * NB].rearrange("p (m b) -> p m b", b=NB),
                                       cols_of("b_mod").unsqueeze(2).to_broadcast([P, 6, NB]), ALU.add))
                dve.tensor_scalar(mod1[:], mod[:, 1:6:3, :], 1.0, None, ALU.add).then_inc(S["mod_ready"], 1)

            def kq_(g):
                dve.wait_ge(S["kq_made"], g + 1)
                dve.tensor_copy(half(kq_t, g), bank(("kq", g))).then_inc(S["kq_ready"], 1)

            def s0_(g):
                dve.wait_ge(S["s0_made"], g + 1)
                if g:
                    dve.wait_ge(S["p0_ready"], g)
                link(dve.tensor_reduce(smallm[:], by_batch(bank(("s0", g))), AX_X, ALU.max, negate=True))
                if g:
                    dve.wait_ge(S["s0_exp"], g)
                dve.tensor_scalar(small[:, 0, :], smallm[:], SCALE0, None, ALU.mult).then_inc(S["s0_max"], 1)

            def p0_(g):
                dve.wait_ge(S["s0_exp"], g + 1)
                link(dve.reciprocal(small[:, 2, :], small[:, 1, :]))
                t = p0[:, g * HB:(g + 1) * HB, :]
                dve.tensor_tensor(t, t, small[:, 2, :].unsqueeze(2).to_broadcast([P, HB, P]), ALU.mult)\
                    .then_inc(S["p0_ready"], 1)

            def ev_(g):
                dve.wait_ge(S["ev_made"], g + 1)
                dve.tensor_copy(half(ev_t, g), bank(("ev", g))).then_inc(S["ev_ready"], 1)

            def router_(g):
                dve.wait_ge(S["router_made"], g + 1)
                if g == 0:
                    dve.wait_ge(S["abias_ready"], 1)
                if g:
                    dve.wait_ge(S["probs_t_made"], g)
                    dve.wait_ge(S["out0_made"], g)
                dve.tensor_tensor(by_batch(logit_t[0:E, :]), by_batch(bank(("router", g))[0:E, :]),
                                  rbias[:, g * HB:(g + 1) * HB].unsqueeze(2).to_broadcast([E, HB, P]), ALU.add)\
                    .then_inc(S["router_ready"], 1)

            def probs_(g):
                dve.wait_ge(S["probs_t_made"], g + 1)
                if g:
                    dve.wait_ge(S["router_p_ready"], g)
                o = bank(("probs", g))[:, 0:HB * E].rearrange("p (b e) -> p b e", e=E)
                link(dve.tensor_reduce(smalls[:, 0, :], o, AX_X, ALU.max))
                dve.tensor_tensor(small3[:, 0], o, smalls[:, 0, :].unsqueeze(2).to_broadcast([P, HB, E]),
                                  ALU.subtract).then_inc(S["probs_centered"], 1)

            def router_p_(g):
                dve.wait_ge(S["probs_exp"], g + 1)
                link(dve.tensor_reduce(smalls[:, 1, :], small3[:, 1], AX_X, ALU.add))
                link(dve.reciprocal(small[:, 3, :], smalls[:, 1, :]))
                dve.tensor_tensor(router_p[:, g], small3[:, 1], small[:, 3, :].unsqueeze(2).to_broadcast([P, HB, E]),
                                  ALU.mult).then_inc(S["router_p_ready"], 1)

            def gate2_(g):
                dve.wait_ge(S["gate_tanh"], g + 1)
                dve.tensor_scalar(gate[g], gate[g], 0.5, 0.5, ALU.mult, ALU.add).then_inc(S["gate_ready"], 1)

            def expert_(b):
                g, j = divmod(b, HB)
                if j == 0:
                    dve.wait_ge(S["router_p_ready"], g + 1)
                if b == 0:
                    dve.wait_ge(S["hat_ready"], max(norm_turn["stats", 2], norm_turn["stats", 3]))
                dve.wait_ge(S["expert_made"], b + 1)
                o = bank(("expert", b))
                link(dve.tensor_scalar(routed[:, b, :], o[:, 0:P], router_p[:, g, j, 0:1], None, ALU.mult))
                for e in range(1, E):
                    ins = dve.scalar_tensor_tensor(out=routed[:, b, :], in0=o[:, e * P:(e + 1) * P],
                                                   scalar=router_p[:, g, j, e:e + 1], in1=routed[:, b, :],
                                                   op0=ALU.mult, op1=ALU.add)
                    if e < E - 1:
                        link(ins)
                ins.then_inc(S["routed_ready"], 1)

            def out0_(g):
                dve.wait_ge(S["out0_made"], g + 1)
                dve.wait_ge(S["gate_ready"], g + 1)
                if g:
                    dve.wait_ge(S["delta_made"], g)
                dve.scalar_tensor_tensor(out=delta_t, in0=bank(("out0", g)), scalar=col("out_b"), in1=gate[g],
                                         op0=ALU.add, op1=ALU.mult).then_inc(S["delta_t_ready"], 1)

            def add_to_res(key, b0, nb):
                t = res[:, b0:b0 + nb, :]
                dve.tensor_tensor(t, t, by_batch(bank(key))[:, 0:nb, :], ALU.add).then_inc(S["res_ready"], 1)

            def delta_t_(g):
                dve.wait_ge(S["delta_made"], g + 1)
                add_to_res(("delta_t", g), g * HB, HB)

            def head_bias(n):
                return {"kc": col("b_kvc"), "k": col("b_qkv", 1), "q": col("b_qkv"), "qc": col("b_qc")}[HEADS[n][0]]

            def proj_(n):
                dve.wait_ge(S["high_ready"], n + 1)
                dve.scalar_tensor_tensor(out=low[:, n % 2, :], in0=bank(("proj", n)), scalar=head_bias(n),
                                         in1=high[:, n % 2, :].bitcast(F32), op0=ALU.add, op1=ALU.subtract)\
                    .then_inc(S["low_ready"], 1)

            def sel_(n, c):
                kind, g = HEADS[n]
                t = slots_k if kind[0] == "k" else slots_q
                if c == 0:
                    if kind[1:] == "c":
                        dve.wait_ge(S["scores_t_made"], NC * HB * (g + 1))
                    dve.wait_ge(S["sel_made"], n * NC + c + 1)
                    dve.tensor_copy(t[:, g * HB:(g + 1) * HB, c, :], by_batch(bank(("sel", n, c))))\
                        .then_inc(S["slots_first"], 1)

            def values_(n):
                a, g = VALUES[n]
                dve.wait_ge(S["values_made"], n + 1)
                if n:
                    dve.wait_ge(S["values_low"], n)
                o = bank(("values", n)).rearrange("p (x d) -> p x d", d=D)
                v = vals[:, a, g * HB:(g + 1) * HB].rearrange("p b h w -> p (b h) w")
                link(dve.tensor_copy(v[:, :, 0:D], o))
                dve.tensor_tensor(vrest[:, :].rearrange("p (x d) -> p x d", d=D), o, v[:, :, 0:D], ALU.subtract)\
                    .then_inc(S["values_rest"], 1)

            def scores_(i, c):
                n = i * NC + c
                dve.wait_ge(S["scores_made"], n + 1)
                if i >= 2 and c == 0:
                    dve.wait_ge(S["guard_ready"], i - 1)
                dve.tensor_reduce(guard[:, i % 2, c * HC:(c + 1) * HC], by_batch(bank(("scores", i, c))), AX_X,
                                  ALU.max, negate=True).then_inc(S["scores_read"], 1)

            def guard_(i):
                dve.wait_ge(S["scores_read"], NC * (i + 1))
                if i == 0:
                    dve.wait_ge(S["vec_const"], 1)
                if i >= 2:
                    dve.wait_ge(S["guard_t_made"], i - 1)
                link(dve.tensor_copy(guard_pair[:, i % 2, 0:NH], guard[:, i % 2, :]))
                dve.tensor_tensor(guard_pair[:, i % 2, NH:2 * NH], guard[:, i % 2, :], guard_pair[:, i % 2, 0:NH],
                                  ALU.subtract).then_inc(S["guard_ready"], 1)

            def guard_t_(i):
                dve.wait_ge(S["guard_t_made"], i + 1)
                if i >= 2:
                    dve.wait_ge(S["scores_t_made"], NC * (i - 1))
                dve.tensor_copy(guard_t[:, i % 2, :], bank(("guard_t", i)).bitcast(BF16)[:, 0:P])\
                    .then_inc(S["guard_t_ready"], 1)

            def mix_(i):
                dve.wait_ge(S["mix_made"], i + 1)
                b = i % NB
                if i >= NB and i % HB == 0:
                    dve.wait_ge(S["attn_t_made"], i // HB - 1)
                if i:
                    dve.wait_ge(S["attn_ready"], i)
                o = bank(("mix", i))[:, 0:NH * VW].rearrange("p (h w) -> p h w", w=VW)
                t = attn[:, b, :].rearrange("p (h d) -> p h d", d=D)
                dve.reciprocal(rden[:], o[:, :, 3 * D])
                dve.tensor_reduce(t, o[:, :, 0:3 * D].rearrange("p h (s d) -> p h d s", s=3), AX_X, ALU.add)\
                    .then_inc(S["mix_read"], 1)
                dve.wait_ge(S["mix_read"], i + 1)
                dve.tensor_tensor(t, t, rden[:, :].unsqueeze(2).to_broadcast([P, NH, D]), ALU.mult)\
                    .then_inc(S["attn_ready"], 1)

            def gated(out, o, bias, which, b0, nb):
                return dve.scalar_tensor_tensor(out=out.rearrange("p (b n) -> p b n", b=nb),
                                                in0=o.rearrange("p (b n) -> p b n", b=nb), scalar=bias,
                                                in1=mod[:, which, b0:b0 + nb].unsqueeze(2).to_broadcast([P, nb, P]),
                                                op0=ALU.add, op1=ALU.mult)

            def attn_proj_(p):
                a, b0, nb = OUTS[p]
                dve.wait_ge(S["attn_proj_made"], p + 1)
                if a:
                    add_to_res(("attn_proj", p), b0, nb)
                    return
                if p:
                    dve.wait_ge(S["attn_y_made"], p)
                gated(within(y_t, b0, nb), bank(("attn_proj", p))[:, 0:nb * P], col("b_proj"), 2, b0, nb)\
                    .then_inc(S["y_ready"], 1)

            def attn_y_(p):
                dve.wait_ge(S["attn_y_made"], p + 1)
                add_to_res(("attn_y", p), *OUTS[p][1:])

            def mlp2_(g):
                b0, nb, _ = MLPS[g]
                dve.wait_ge(S["mlp2_made"], g + 1)
                gated(mlp_y[g], bank(("mlp2", g))[:, 0:nb * P], col("b_mlp2"), 5, b0, nb).then_inc(S["y_ready"], 1)

            def last_(g):
                dve.wait_ge(S["last_made"], g + 1)
                add_to_res(("last", g), *MLPS[g][0:2])

            mine = {"cols": cols_, "stats": stats_, "norm": norm_, "kq_w_out": kq_w_,
                    "anchor_out": anchor_, "mod_out": mod_, "kq_out": kq_, "s0_out": s0_, "p0": p0_,
                    "router_p": router_p_, "ev_out": ev_, "router_out": router_, "probs_out": probs_,
                    "gate2_out": gate2_, "expert_out": expert_, "out0_out": out0_, "delta_t_out": delta_t_,
                    "proj_out": proj_,
                    "sel_out": sel_, "values_out": values_, "scores_out": scores_, "guard": guard_,
                    "guard_t_out": guard_t_, "mix_out": mix_,
                    "attn_proj_out": attn_proj_, "attn_y_out": attn_y_, "mlp2_out": mlp2_, "last_out": last_}
            for st in steps:
                if st[0] in mine:
                    mine[st[0]](*st[1:])

        @block.scalar
        def _(act):
            def bank(key):
                return banks[:, bank_of[key], :]

            act.wait_ge(S["first_in"], 16)
            act.activation(silu_c[:], cols_of("cond"), ACT.Silu).then_inc(S["silu_c_ready"], 1)
            act.wait_ge(S["pair_sel_made"], 1)
            act.copy(head_sel[:], pair_sel[:, :].unsqueeze(2).to_broadcast([P, NH, P])).then_inc(S["head_sel_ready"], 1)

            def hat_(n):
                kind, b0, nb = NORMS[n]
                act.wait_ge(S["hat_t_made"], norm_turn["stats", n])
                o = bank(("hat", n))[:, 0:nb * P]
                if kind == "x":
                    last = act.activation(x_hat_t[:, b0 * P:(b0 + nb) * P], o, ACT.Identity, scale=col("gamma"),
                                          bias=col("beta"))
                elif kind in "c2":
                    last = act.copy((ctx_hat_t if kind == "c" else norm_t)[:, b0 * P:(b0 + nb) * P], o)
                else:
                    act.wait_ge(S["mod_ready"], 1)
                    a = 0 if kind == "1" else 1
                    for j in range(nb):
                        b = b0 + j
                        last = act.activation(tok(norm_t, b), tok(o, j), ACT.Identity, scale=mod1[:, a, b:b + 1],
                                              bias=mod[:, 3 * a, b:b + 1])
                last.then_inc(S["hat_t_ready"], 1)

            def v0_(g):
                act.wait_ge(S["v0_made"], g + 1)
                act.copy(v0[:, g * HB:(g + 1) * HB, :], by_batch(bank(("v0", g)))).then_inc(S["v0_ready"], 1)

            def s0_(g):
                act.wait_ge(S["s0_max"], g + 1)
                if g:
                    act.wait_ge(S["p0_ready"], g)
                for j in range(HB):
                    last = act.activation(p0[:, g * HB + j, :], bank(("s0", g))[:, j * P:(j + 1) * P], ACT.Exp,
                                          scale=SCALE0, bias=small[:, 0, j:j + 1], accum_out=small[:, 1, j:j + 1])
                last.then_inc(S["s0_exp"], 1)

            def p0_t_(g):
                act.wait_ge(S["p0_t_made"], g + 1)
                act.copy(p0_t[:, g * HB:(g + 1) * HB, :], by_batch(bank(("p0_t", g)))).then_inc(S["p0_t_ready"], 1)

            def silu_by_batch(out, o, m, g):
                for j in range(HB):
                    last = act.activation(out[:, j * P:(j + 1) * P], o[:, j * P:(j + 1) * P], ACT.Silu,
                                          bias=abias[:, m, g * HB + j:g * HB + j + 1])
                return last

            def gate1_(g):
                act.wait_ge(S["abias_ready"], 1)
                act.wait_ge(S["gate1_made"], g + 1)
                silu_by_batch(gate[g], bank(("gate1", g)), MH, g).then_inc(S["gate_h_ready"], 1)

            def hidden_(g, m):
                n = g * MH + m
                if n == 0:
                    act.wait_ge(S["abias_ready"], 1)
                act.wait_ge(S["hidden_made"], n + 1)
                if g and m == 0:
                    act.wait_ge(S["expert_made"], HB * g)
                silu_by_batch(hidden[:, m, :], bank(("hidden", n)), m, g).then_inc(S["hidden_ready"], 1)

            def probs_(g):
                act.wait_ge(S["probs_centered"], g + 1)
                if g:
                    act.wait_ge(S["router_p_ready"], g)
                act.activation(small3[:, 1], small3[:, 0], ACT.Exp).then_inc(S["probs_exp"], 1)

            def gate2_(g):
                if g == 0:
                    act.wait_ge(S["cols_ready"], 1)
                act.wait_ge(S["gate2_made"], g + 1)
                act.activation(gate[g], bank(("gate2", g)), ACT.Tanh, scale=0.5, bias=gate_b2_half[:, 0:1])\
                    .then_inc(S["gate_tanh"], 1)

            def routed_t_(g):
                act.wait_ge(S["routed_t_made"], g + 1)
                if g:
                    act.wait_ge(S["out0_made"], g)
                act.copy(routed_t, bank(("routed_t", g))).then_inc(S["routed_t_ready"], 1)

            def head_bias(n):
                return {"kc": col("b_kvc"), "k": col("b_qkv", 1), "q": col("b_qkv"), "qc": col("b_qc")}[HEADS[n][0]]

            def proj_(n):
                act.wait_ge(S["proj_made"], n + 1)
                if n >= 2:
                    act.wait_ge(S["sel_made"], NC * (n - 1))
                act.activation(high[:, n % 2, :], bank(("proj", n)), ACT.Identity, bias=head_bias(n))\
                    .then_inc(S["high_ready"], 1)

            def sel_(n, c):
                kind, g = HEADS[n]
                t = slots_k if kind[0] == "k" else slots_q
                if c:
                    if kind[1:] == "c":
                        act.wait_ge(S["scores_t_made"], NC * HB * (g + 1))
                    act.wait_ge(S["sel_made"], n * NC + c + 1)
                    act.copy(t[:, g * HB:(g + 1) * HB, c, :], by_batch(bank(("sel", n, c))))\
                        .then_inc(S["slots_rest"], 1)

            def probs1_(i, c):
                n = i * NC + c
                if n == 0:
                    act.wait_ge(S["ev_made"], NHALF)
                act.wait_ge(S["scores_t_made"], n + 1)
                if n >= PR:
                    act.wait_ge(S["p_low"], n - PR + 1)
                act.activation(pf[:, n % PR, :], bank(("probs1", i, c)), ACT.Exp, scale=SCALE1)
                if i >= 2 and c == 0:
                    act.wait_ge(S["mix_made"], i - 1)
                act.activation(ph[:, i % 2, c, :], bank(("probs1", i, c)), ACT.Exp, scale=SCALE1)\
                    .then_inc(S["p_high"], 1)

            def attn_t_(p):
                act.wait_ge(S["attn_t_made"], p + 1)
                if p:
                    act.wait_ge(S["attn_proj_made"], p)
                a, b0, nb = OUTS[p]
                act.activation(within(attn_t, b0, nb), bank(("attn_t", p))[:, 0:nb * P], ACT.Identity,
                               bias=col("b_kvc", 1) if a else col("b_qkv", 2)).then_inc(S["attn_t_ready"], 1)

            def mlp1_(g, m):
                k = g * NM + m
                n = MLPS[g][1] * P
                act.wait_ge(S["mlp1_made"], k + 1)
                act.activation(mlp_h[g][:, m * n:(m + 1) * n], bank(("mlp1", k))[:, 0:n], ACT.Gelu_apprx_tanh,
                               bias=col("b_mlp1", m))\
                    .then_inc(S["mlp1_ready"], 1)

            mine = {"hat_out": hat_, "v0_out": v0_, "s0_out": s0_, "p0_t_out": p0_t_, "gate1_out": gate1_,
                    "hidden_out": hidden_, "probs_out": probs_, "gate2_out": gate2_, "routed_t_out": routed_t_,
                    "proj_out": proj_,
                    "sel_out": sel_, "probs1_out": probs1_, "attn_t_out": attn_t_, "mlp1_out": mlp1_}
            for st in steps:
                if st[0] in mine:
                    mine[st[0]](*st[1:])

        @block.gpsimd
        def _(pool):
            chain = [0]

            def link(ins):
                chain[0] += 1
                ins.then_inc(S["pool"], 1)
                pool.wait_ge(S["pool"], chain[0])

            link(pool.memset(ident[:], 0.0))
            pool.affine_select(out=ident[:, :], in_=ident[:, :], compare_op=ALU.not_equal, fill=1.0, base=0,
                               pattern=[[-1, P]], channel_multiplier=1).then_inc(S["ident_made"], 1)
            pool.wait_ge(S["ident_made"], 1)
            pool.tensor_tensor(pair_sel[:], ident[:, 0:NH], ident[:, NH:2 * NH], ALU.add)\
                .then_inc(S["pair_sel_made"], 1)
            link(pool.memset(power[:], -0.5))

            def stats_(n):
                k = norm_turn["stats", n]
                pool.wait_ge(S["moments_ready"], k)
                if k > 1:
                    pool.wait_ge(S["rstd_made"], k - 1)
                kind, _, nb = NORMS[n]
                link(pool.tensor_scalar(var_eps[:, 0:nb], moments[:, n, 0:nb, 1], EPS0 if kind == "x" else EPS1, None,
                                        ALU.add))
                pool.tensor_tensor(rstd[:, n, 0:nb], var_eps[:, 0:nb], power[:, 0:nb], ALU.pow)\
                    .then_inc(S["rstd_made"], 1)

            def anchor_(_):
                pool.memset(diag[:].rearrange("p r s j c n -> p (r s j c n)").bitcast(F32), 0.0)\
                    .then_inc(S["diag_zero"], 1)

            def split_(_):
                pool.wait_ge(S["rows_in"], 16)
                link(pool.tensor_copy(row_parts[:], rows[:]))
                link(pool.tensor_tensor(rows[:], rows[:], row_parts[:], ALU.subtract))
                link(pool.tensor_copy(row_parts[32:64, :], rows[32:64, :]))
                link(pool.tensor_copy(row_parts[64:P, :], rows[64:P, :]))
                link(pool.tensor_tensor(rows[64:P, :], rows[64:P, :], row_parts[64:P, :], ALU.subtract))
                link(pool.tensor_copy(row_parts[64:P, :], rows[64:P, :]))
                link(pool.memset(row_parts[96:P, :], 0.0))
                pool.memset(share[:], 1.0 / 32).then_inc(S["rows_split"], 1)

            def values_(n):
                a, g = VALUES[n]
                v = vals[:, a, g * HB:(g + 1) * HB].rearrange("p b h w -> p (b h) w")
                r = vrest[:, :].rearrange("p (x d) -> p x d", d=D)
                pool.wait_ge(S["values_rest"], n + 1)
                link(pool.tensor_copy(v[:, :, D:2 * D], r))
                pool.tensor_tensor(v[:, :, 2 * D:3 * D], r, v[:, :, D:2 * D], ALU.subtract)\
                    .then_inc(S["values_low"], 1)

            def probs1_(i, c):
                n = i * NC + c
                pool.wait_ge(S["p_high"], n + 1)
                pool.tensor_tensor(pl[:, i % 2, c, :], pf[:, n % PR, :], ph[:, i % 2, c, :], ALU.subtract)\
                    .then_inc(S["p_low"], 1)

            mine = {"stats": stats_, "anchor_out": anchor_, "split": split_, "values_out": values_,
                    "probs1_out": probs1_}
            for st in steps:
                if st[0] in mine:
                    mine[st[0]](*st[1:])

        @block.sync
        def _(sp):
            for tile, src, name in (
                    (res[:, 0:HB, :], x[0], "x_in0"), (first_sb[:], first, "first_in"),
                    (ctx_t, ctx_turned, "ctx_turned_in"), (res[:, HB:NB, :], x[1], "x_in1"),
                    (hidden_sb[:], hidden_w, "hidden_w_in"), (ctx_tok[:], ctx, "ctx_in"),
                    (layer1_sb[:], layer1, "layer1_in"), (second_sb[:], second, "second_in"),
                    (rows[:], bias_rows.partition_broadcast(P), "rows_in"),
                    (late_sb[:], late, "late_in")):
                sp.dma_start(tile, src).then_inc(S[name], 16)

            sp.wait_ge(S["diag_zero"], 1)
            by_slot = slots[:].rearrange("p b s c n -> p (b s) c n")

            def made(kind, i):
                n = HEADS.index((kind if i < NB else kind + "c", i % NB // HB))
                sp.wait_ge(S["slots_first"], n + 1)
                sp.wait_ge(S["slots_rest"], 3 * n + 3)

            for n in range(-1, NI):
                b = n % NB
                alone = (n + 1) % HB == 0
                if n >= 0:
                    made("q", n)
                    if n >= NR:
                        sp.wait_ge(S["scores_t_made"], NC * (n - NR + 1))
                    if not alone:
                        made("k", n + 1)
                        if n >= 1:
                            sp.wait_ge(S["scores_made"], NC * n)
                    for j in range(HC):
                        at = slice(j * 4 * D, (j + 1) * 4 * D)
                        if alone:
                            to, src = diag[at, n % NR, 0, j], by_slot[at, 2 * b + 1]
                        else:
                            to, src = diag[at, n % NR, :, j], by_slot[at, 2 * b + 1:2 * b + 3]
                        sp.dma_start(to.bitcast(F32), src.bitcast(F32)).then_inc(diag_in[n % NR], 16)
                if alone and n + 1 < NI:
                    made("k", n + 1)
                    if n >= 1:
                        sp.wait_ge(S["scores_made"], NC * n)
                    for j in range(HC):
                        at = slice(j * 4 * D, (j + 1) * 4 * D)
                        sp.dma_start(diag[at, n % NR, 1, j].bitcast(F32), slots_k[at, (n + 1) % NB].bitcast(F32))\
                            .then_inc(diag_k_in, 16)

            for g, (b0, nb, _) in enumerate(MLPS):
                sp.wait_ge(S["res_ready"], res_turn["last_out", g])
                sp.dma_start(within(out[b0 // HB], b0, nb), res[:, b0:b0 + nb, :]).then_inc(S["out_done"], 16)
            sp.wait_ge(S["out_done"], 16 * len(MLPS))


def laid_out(inputs):
    import numpy as np

    z = {n.replace("L0_xcond_", "").replace("L1_xcond_", ""): np.asarray(a) for n, a in inputs.items()}

    def by_row_blocks(w):
        return w.reshape(-1, P, w.shape[-1]).transpose(1, 0, 2).reshape(P, -1)

    def tokens(a):
        return a.reshape(NHALF, HB, P, P).transpose(0, 2, 1, 3).reshape(NHALF, P, HN)

    z["router_b"] = np.concatenate([z["router_b"], np.zeros(P - E, z["router_b"].dtype)])
    z["gamma"], z["beta"], z["cond"] = z["ln_gamma"], z["ln_beta"], z["cond_1024"]
    parts = {
        "cols": np.concatenate([z[n].reshape(-1, P) for n in COL]).T,
        "WqT": z["Wq"].T, "WkT": z["Wk"].T, "Wv": z["Wv"],
        "e_w1": np.concatenate([by_row_blocks(w) for w in z["e_w1"]], axis=1),
        "e_w2": np.concatenate([by_row_blocks(w) for w in z["e_w2"]], axis=1),
        **{n: by_row_blocks(z[n]) for n in ("gate_w1", "router_W", "W_mlp2")},
        **{n: z[n] for n in ("gate_w2", "out_w", "W_mod", "W_qkv", "W_kvc", "W_qc", "W_proj", "W_cproj", "W_mlp1")},
    }
    pack = lambda names: np.concatenate([parts[n] for n, _ in names], axis=1)
    ctx = z["ctx_1024"]
    return {"x": tokens(z["x"]), "ctx": ctx.transpose(1, 0, 2).reshape(P, NB * P),
            "ctx_turned": ctx.transpose(2, 0, 1).reshape(P, NB * P), "first": pack(FIRST), "hidden_w": pack(HIDDEN),
            "second": pack(SECOND), "layer1": pack(LAYER1), "late": pack(LATE),
            "bias_rows": np.concatenate([z["e_b2"].reshape(-1), z["b_cproj"]])}


def kernel(**inputs):
    import numpy as _np
    import concourse.bacc as _bacc
    from concourse import mybir as _mybir
    from concourse.bass_utils import run_bass_kernel_spmd as _run

    nc = _bacc.Bacc("TRN2", target_bir_lowering=False, num_devices=1)
    arrays, args = {}, []
    for name, a in laid_out(inputs).items():
        a = _np.ascontiguousarray(a)
        arrays[f"in_{name}_dram"] = a
        args.append(nc.dram_tensor(f"in_{name}_dram", a.shape, _mybir.dt.from_np(a.dtype), kind="ExternalInput").ap())
    out = nc.dram_tensor("out_dram", (NHALF, P, HN), _mybir.dt.float32, kind="ExternalOutput").ap()
    pixart_block(nc, *args, out)
    got = _run(nc, [arrays], core_ids=[0]).results[0]["out_dram"]
    return _np.ascontiguousarray(got.reshape(NHALF, P, HB, P).transpose(0, 2, 1, 3).reshape(NB, P, P))
```
